# Optimizing a Trainium2 kernel written in Bass

```python
import numpy as np
import jax
import jax.numpy as jnp

def _softmax(x, axis=-1):
    return jax.nn.softmax(x, axis=axis)

def _gelu(x):
    return jax.nn.gelu(x, approximate=True)

def _silu(x):
    return jax.nn.silu(x)

def _sigmoid(x):
    return jax.nn.sigmoid(x)

def _layernorm(x, axis=-1, eps=1e-05):
    m = jnp.mean(x, axis=axis, keepdims=True)
    v = jnp.var(x, axis=axis, keepdims=True)
    return (x - m) / jnp.sqrt(v + eps)

def _scatter_add(tgt, idx, src, axis=0):
    return tgt.at[idx].add(src)

def _segment_sum(src, seg, n):
    return jax.ops.segment_sum(src, seg, n)
kernel_name = 'mk_gnn_preln_d4_gnn_r8_254a35'

def setup_inputs(seed: int=0):
    np.random.seed(seed)
    _w = jnp.asarray

    def _rec_inputs():
        import jax
        import jax.numpy as jnp
        _gk = jax.random.key(seed)
        x = -0.0005121 + 1.001 * jax.random.normal(jax.random.fold_in(_gk, 1), (6250, 64), jnp.float32)
        _s = jax.random.randint(jax.random.fold_in(_gk, 2), (100000,), 0, 6250, jnp.int32)
        _d = jax.random.randint(jax.random.fold_in(_gk, 3), (100000,), 0, 6250, jnp.int32)
        _loop = jnp.arange(6250, dtype=jnp.int32)
        src = jnp.concatenate([_s, _d, _loop])
        dst = jnp.concatenate([_d, _s, _loop])
        _o = jnp.argsort(dst, stable=True)
        src = src[_o]
        dst = dst[_o]
        edge_attr_32 = 0.000189758 + 1.00013 * jax.random.normal(jax.random.fold_in(_gk, 12), (206250, 32), jnp.float32)
        return (x, src, dst, edge_attr_32)
    x, src, dst, edge_attr_32 = _rec_inputs()

    def _L0_gnn_setup():
        import jax, jax.numpy as jnp
        import numpy as np
        N_NODES = 6250
        N_EDGES = 100000
        D = 64
        EPS = 1e-12
        key = jax.random.key(seed)
        k1, k2, k3, k4 = jax.random.split(key, 4)
        features = jax.random.normal(k1, (N_NODES, D), dtype=jnp.float32)
        W = jax.random.normal(k2, (D, D), dtype=jnp.float32) * (1.0 / np.sqrt(D))
        beta = jnp.ones((1,), dtype=jnp.float32)
        src = jax.random.randint(k3, (N_EDGES,), 0, N_NODES)
        dst = jax.random.randint(k4, (N_EDGES,), 0, N_NODES)
        return {'features': features, 'W': W, 'beta': beta, 'src': src, 'dst': dst}
    _L0_gnn_all = _L0_gnn_setup()
    _L0_gnn_in = {k: v for k, v in _L0_gnn_all.items() if k in ('W', 'beta')}
    del _L0_gnn_all

    def _L1_gnn_setup():
        import jax, jax.numpy as jnp
        import numpy as np
        N_NODES = 6250
        key = jax.random.key(seed)
        k1, k2 = jax.random.split(key)
        edge_index = jax.random.randint(k1, (2, 100000), 0, N_NODES, dtype=jnp.int64)
        x = jax.random.normal(k2, (N_NODES, 64), dtype=jnp.float32)
        return {'edge_index': edge_index, 'x': x}
    _L1_gnn_all = _L1_gnn_setup()
    _L1_gnn_in = {k: v for k, v in _L1_gnn_all.items() if k in ()}
    del _L1_gnn_all

    def _L2_gnn_setup():
        import jax, jax.numpy as jnp
        import numpy as np
        N, E = (12500, 200000)
        D_NODE, D_HID_M, D_OUT_M = (64, 128, 64)
        D_HID_U, D_OUT_U = (128, 64)

        def _glorot(key, shape):
            fan_in, fan_out = shape
            lim = (6.0 / (fan_in + fan_out)) ** 0.5
            return jax.random.uniform(key, shape, jnp.float32, -lim, lim)

        def _mlp3(x, W1, b1, W2, b2, W3, b3):
            h = jax.nn.relu(x @ W1 + b1)
            h = jax.nn.relu(h @ W2 + b2)
            return h @ W3 + b3
        key = jax.random.key(seed)
        ks = jax.random.split(key, 16)
        node_features = jax.random.normal(ks[0], (N, D_NODE), jnp.float32)
        edge_index = jax.random.randint(ks[1], (2, E), 0, N, jnp.int64)
        d_in_U = D_NODE + D_OUT_M
        return {'node_features': node_features, 'edge_index': edge_index, 'WM1': _glorot(ks[2], (D_NODE, D_HID_M)), 'bM1': jnp.zeros((D_HID_M,), jnp.float32), 'WM2': _glorot(ks[3], (D_HID_M, D_HID_M)), 'bM2': jnp.zeros((D_HID_M,), jnp.float32), 'WM3': _glorot(ks[4], (D_HID_M, D_OUT_M)), 'bM3': jnp.zeros((D_OUT_M,), jnp.float32), 'WU1': _glorot(ks[5], (d_in_U, D_HID_U)), 'bU1': jnp.zeros((D_HID_U,), jnp.float32), 'WU2': _glorot(ks[6], (D_HID_U, D_HID_U)), 'bU2': jnp.zeros((D_HID_U,), jnp.float32), 'WU3': _glorot(ks[7], (D_HID_U, D_OUT_U)), 'bU3': jnp.zeros((D_OUT_U,), jnp.float32)}
    _L2_gnn_all = _L2_gnn_setup()
    _L2_gnn_in = {k: v for k, v in _L2_gnn_all.items() if k in ('WM1', 'bM1', 'WM2', 'bM2', 'WM3', 'bM3', 'WU1', 'bU1', 'WU2', 'bU2', 'WU3', 'bU3')}
    del _L2_gnn_all

    def _L3_gnn_setup():
        import jax, jax.numpy as jnp
        import numpy as np
        V = 12500
        E = 200000
        D = 64
        EF = 32
        EPS = 1e-05
        key = jax.random.key(seed)
        ks = jax.random.split(key, 10)
        h = jax.random.normal(ks[0], (V, D), dtype=jnp.float32)
        edge_index = jax.random.randint(ks[1], (2, E), 0, V, dtype=jnp.int64)
        edge_attr = jax.random.normal(ks[2], (E, EF), dtype=jnp.float32)
        lim1 = 1.0 / np.sqrt(D + EF)
        lim2 = 1.0 / np.sqrt(D)
        W1 = jax.random.uniform(ks[3], (D + EF, D), jnp.float32, -lim1, lim1)
        b1 = jax.random.uniform(ks[4], (D,), jnp.float32, -lim1, lim1)
        W2 = jax.random.uniform(ks[5], (D, D), jnp.float32, -lim2, lim2)
        b2 = jax.random.uniform(ks[6], (D,), jnp.float32, -lim2, lim2)
        gamma = jnp.ones((D,), jnp.float32)
        beta = jnp.zeros((D,), jnp.float32)
        return {'h': h, 'edge_index': edge_index, 'edge_attr': edge_attr, 'W1': W1, 'b1': b1, 'W2': W2, 'b2': b2, 'gamma': gamma, 'beta': beta}
    _L3_gnn_all = _L3_gnn_setup()
    _L3_gnn_in = {k: v for k, v in _L3_gnn_all.items() if k in ('W1', 'b1', 'W2', 'b2', 'gamma', 'beta')}
    del _L3_gnn_all
    return {'x': x, 'src': src, 'dst': dst, 'edge_attr_32': edge_attr_32, 'L0_gnn_W': _L0_gnn_in['W'], 'L0_gnn_beta': _L0_gnn_in['beta'], 'L2_gnn_WM1': _L2_gnn_in['WM1'], 'L2_gnn_bM1': _L2_gnn_in['bM1'], 'L2_gnn_WM2': _L2_gnn_in['WM2'], 'L2_gnn_bM2': _L2_gnn_in['bM2'], 'L2_gnn_WM3': _L2_gnn_in['WM3'], 'L2_gnn_bM3': _L2_gnn_in['bM3'], 'L2_gnn_WU1': _L2_gnn_in['WU1'], 'L2_gnn_bU1': _L2_gnn_in['bU1'], 'L2_gnn_WU2': _L2_gnn_in['WU2'], 'L2_gnn_bU2': _L2_gnn_in['bU2'], 'L2_gnn_WU3': _L2_gnn_in['WU3'], 'L2_gnn_bU3': _L2_gnn_in['bU3'], 'L3_gnn_W1': _L3_gnn_in['W1'], 'L3_gnn_b1': _L3_gnn_in['b1'], 'L3_gnn_W2': _L3_gnn_in['W2'], 'L3_gnn_b2': _L3_gnn_in['b2'], 'L3_gnn_gamma': _L3_gnn_in['gamma'], 'L3_gnn_beta': _L3_gnn_in['beta']}

def reference(x, src, dst, edge_attr_32, L0_gnn_W, L0_gnn_beta, L2_gnn_WM1, L2_gnn_bM1, L2_gnn_WM2, L2_gnn_bM2, L2_gnn_WM3, L2_gnn_bM3, L2_gnn_WU1, L2_gnn_bU1, L2_gnn_WU2, L2_gnn_bU2, L2_gnn_WU3, L2_gnn_bU3, L3_gnn_W1, L3_gnn_b1, L3_gnn_W2, L3_gnn_b2, L3_gnn_gamma, L3_gnn_beta):
    import jax
    import jax.numpy as jnp

    def _L0_gnn_ref(features, W, beta, src, dst):
        import jax, jax.numpy as jnp
        import numpy as np
        N_NODES = 6250
        N_EDGES = 100000
        D = 64
        EPS = 1e-12
        norm = jnp.maximum(jnp.linalg.norm(features, axis=-1, keepdims=True), EPS)
        nh = features / norm
        cos = jnp.sum(nh[src] * nh[dst], axis=-1)
        e = beta[0] * cos
        emax = jax.ops.segment_max(e, dst, num_segments=N_NODES)
        p = jnp.exp(e - emax[dst])
        psum = jax.ops.segment_sum(p, dst, num_segments=N_NODES)
        p = p / psum[dst]
        msgs = features[src] * p[:, None]
        h = jax.ops.segment_sum(msgs, dst, num_segments=N_NODES)
        h = h @ W.T
        return h

    def _L1_gnn_ref(edge_index, x):
        import jax, jax.numpy as jnp
        import numpy as np
        N_NODES = 6250
        msgs = x[edge_index[1]]
        out = jax.ops.segment_sum(msgs, edge_index[0], num_segments=x.shape[0])
        return out

    def _L2_gnn_ref(node_features, edge_index, WM1, bM1, WM2, bM2, WM3, bM3, WU1, bU1, WU2, bU2, WU3, bU3):
        import jax, jax.numpy as jnp
        import numpy as np
        N, E = (12500, 200000)
        D_NODE, D_HID_M, D_OUT_M = (64, 128, 64)
        D_HID_U, D_OUT_U = (128, 64)

        def _glorot(key, shape):
            fan_in, fan_out = shape
            lim = (6.0 / (fan_in + fan_out)) ** 0.5
            return jax.random.uniform(key, shape, jnp.float32, -lim, lim)

        def _mlp3(x, W1, b1, W2, b2, W3, b3):
            h = jax.nn.relu(x @ W1 + b1)
            h = jax.nn.relu(h @ W2 + b2)
            return h @ W3 + b3
        source, destination = (edge_index[0], edge_index[1])
        message = node_features[source]
        y = _mlp3(message, WM1, bM1, WM2, bM2, WM3, bM3)
        z = jax.ops.segment_sum(y, destination, num_segments=node_features.shape[0])
        return _mlp3(jnp.concatenate([node_features, z], axis=-1), WU1, bU1, WU2, bU2, WU3, bU3)

    def _L3_gnn_ref(h, edge_index, edge_attr, W1, b1, W2, b2, gamma, beta):
        import jax, jax.numpy as jnp
        import numpy as np
        V = 12500
        E = 200000
        D = 64
        EF = 32
        EPS = 1e-05
        src, dst = (edge_index[0], edge_index[1])
        x = jnp.concatenate([h[src], edge_attr], axis=-1)
        msg = jnp.maximum(x @ W1 + b1, 0.0) @ W2 + b2
        n_nodes = h.shape[0]
        agg = jax.ops.segment_sum(msg, dst, num_segments=n_nodes)
        cnt = jax.ops.segment_sum(jnp.ones((dst.shape[0],), h.dtype), dst, num_segments=n_nodes)
        agg = agg / jnp.maximum(cnt, 1.0)[:, None]
        y = h + agg
        mu = jnp.mean(y, axis=-1, keepdims=True)
        var = jnp.mean(jnp.square(y - mu), axis=-1, keepdims=True)
        return (y - mu) * jax.lax.rsqrt(var + EPS) * gamma + beta
    edge_index = jnp.stack([src, dst])
    h = jnp.maximum(_layernorm(x, axis=-1), 0.0)
    x = x + _L0_gnn_ref(h, L0_gnn_W, L0_gnn_beta, src, dst)
    h = jnp.maximum(_layernorm(x, axis=-1), 0.0)
    x = x + _L1_gnn_ref(edge_index, h)
    h = jnp.maximum(_layernorm(x, axis=-1), 0.0)
    x = x + _L2_gnn_ref(h, edge_index, L2_gnn_WM1, L2_gnn_bM1, L2_gnn_WM2, L2_gnn_bM2, L2_gnn_WM3, L2_gnn_bM3, L2_gnn_WU1, L2_gnn_bU1, L2_gnn_WU2, L2_gnn_bU2, L2_gnn_WU3, L2_gnn_bU3)
    h = jnp.maximum(_layernorm(x, axis=-1), 0.0)
    x = x + _L3_gnn_ref(h, edge_index, edge_attr_32, L3_gnn_W1, L3_gnn_b1, L3_gnn_W2, L3_gnn_b2, L3_gnn_gamma, L3_gnn_beta)
    return x

_drawn_inputs = setup_inputs


def setup_inputs(seed=0):
    import zlib

    import numpy as np

    out = dict(_drawn_inputs(seed))
    spreads = {'L2_gnn_bM1': (0.0, 0.1),
     'L2_gnn_bM2': (0.0, 0.1),
     'L2_gnn_bM3': (0.0, 0.1),
     'L2_gnn_bU1': (0.0, 0.8),
     'L2_gnn_bU2': (0.0, 0.8),
     'L2_gnn_bU3': (0.0, 0.8),
     'L3_gnn_gamma': (1.0, 0.6),
     'L3_gnn_beta': (0.0, 0.8)}
    factors = {'edge_attr_32': 8.0,
     'L3_gnn_W1': 5.644,
     'L3_gnn_b1': 8.0,
     'L3_gnn_W2': 3.591,
     'L3_gnn_b2': 7.097}
    for name, (base, spread) in spreads.items():
        noise = np.random.default_rng([zlib.crc32(name.encode()), seed]).standard_normal(out[name].shape)
        drawn = base * np.exp(spread * noise) if base else spread * noise
        out[name] = jnp.asarray(drawn.astype(out[name].dtype))
    for name, factor in factors.items():
        out[name] = (out[name] * factor).astype(out[name].dtype)
    return out
```

```python
from contextlib import ExitStack

import concourse.bass as bass
from concourse import mybir

P = 128
D = 64
EF = 32
H = 128
N = 6250
E = 206250
NT = -(-N // P)
NP = NT * P
HB = 4
NG = 4
AHEAD = 2
BT = NG * HB
ZERO = 1 + (NG - 2) * HB
NB = -(-E // (P * BT))
T = NB * BT
EP = T * P
TB = T // P
TR = T - TB * P
TBS = TB + 1
TW = D + 2
ACC = NP + P
PAD_DST = 16384
LN_EPS = 1e-5
NORM_EPS = 1e-12
FAR = -1.0e38

ALU = mybir.AluOpType
ACT = mybir.ActivationFunctionType
F32 = mybir.dt.float32
I32 = mybir.dt.int32
U32 = mybir.dt.uint32
AX_X = mybir.AxisListType.X
PE_ENGINE = [mybir.EngineType.PE]
DVE_ENGINE = [mybir.EngineType.DVE]
ROWS = ["bM3", "bU3", "b1", "gamma", "beta3"]
assert BT * P * T // BT == EP and EP % P == 0


def gnn_kernel(nc, x, src, dst, edge_t, beta, rows, cols, w0t, wm1, wm2, wm3, wu1, wu2, wu3, w1, w2, b2, out):
    ctx = ExitStack()
    with ctx:
        def sb(name, shape, dt=F32):
            return ctx.enter_context(nc.sbuf_tensor(name, shape, dt))

        table = nc.dram_tensor("node_table", [NP, TW], F32, kind="Internal").ap()
        kept_rows = nc.dram_tensor("kept_rows", [NB, NG, P, HB * TW], F32, kind="Internal").ap()
        edge_line = nc.dram_tensor("edge_line", [EP], F32, kind="Internal").ap()
        weight_line = nc.dram_tensor("weight_line", [EP], F32, kind="Internal").ap()

        ident = sb("ident", [P, P])
        iota = sb("iota", [P, P])
        beta_sb = sb("beta_sb", [P, 1])
        rows_sb = sb("rows_sb", [P, len(ROWS), D])
        cols_sb = sb("cols_sb", [P, 4])
        w0_sb = sb("w0_sb", [D + 1, D + 1])
        wm1_sb = sb("wm1_sb", [D, H])
        wm2_sb = sb("wm2_sb", [H, H])
        wm3_sb = sb("wm3_sb", [H, D])
        wu1_sb = sb("wu1_sb", [D, 2, H])
        wu2_sb = sb("wu2_sb", [H, H])
        wu3_sb = sb("wu3_sb", [H, D])
        w1a_sb = sb("w1a_sb", [D, D])
        w1b_sb = sb("w1b_sb", [EF, D])
        w2_sb = sb("w2_sb", [D + 1, D])
        src_cols = sb("src_cols", [P, T + AHEAD * HB], I32)
        dloc = sb("dloc", [P, T])
        score = sb("score", [P, T])
        base_row = sb("base_row", [1, HB + T], I32)
        x_sb = sb("x_sb", [P, NT, D])
        h_sb = sb("h_sb", [P, NT, TW])
        tmp = sb("tmp", [P, NT, D])
        stat = sb("stat", [P, 4, NT])
        count = sb("count", [P, NT])
        acc = sb("acc", [D + 1, ACC])
        hT = sb("hT", [D, ACC])
        stage = sb("stage", [P, NG, HB], I32)
        got = sb("got", [P, NG, HB, TW])
        onehot = sb("onehot", [P, NG, HB, P])
        gotT = sb("gotT", [D, NG, HB, P])
        msg = sb("msg", [P, NG, HB, D])
        dots = sb("dots", [P, NG, HB])
        edge_sb = sb("edge_sb", [EF, NG, HB * P])
        hid = sb("hid", [P, 2, 2, 512])
        ps = ctx.enter_context(nc.psum_tensor("ps", [P, 8, 512], F32))

        stages = [0]

        class Stage:

            def __init__(self):
                stages[0] += 1
                self.tag = f"s{stages[0]}_"
                self.ctx = ExitStack()
                self.sems = []

            def __enter__(self):
                return self

            def sem(self, name):
                self.sems.append(nc.alloc_semaphore(name=self.tag + name))
                return self.sems[-1]

            def start(self):
                return self.ctx.enter_context(nc.Block())

            def __exit__(self, *what):
                self.ctx.__exit__(*what)
                if what[0] is None:
                    nc.clear_and_free_semaphores(self.sems)
                    nc.all_engine_barrier()

        def linker(eng, sem):
            done = [0]

            def link(ins, n=1):
                done[0] += n
                ins.then_inc(sem, n)
                eng.wait_ge(sem, done[0])
            return link

        def load_indices():
            with ExitStack() as tmp_ctx, Stage() as s:
                src_raw = tmp_ctx.enter_context(nc.sbuf_tensor("src_raw", [P, TBS, P], I32))
                dst_raw = tmp_ctx.enter_context(nc.sbuf_tensor("dst_raw", [P, TBS, P], I32))
                src_f = tmp_ctx.enter_context(nc.sbuf_tensor("src_f", [P, TBS, P], F32))
                dst_f = tmp_ctx.enter_context(nc.sbuf_tensor("dst_f", [P, TBS, P], F32))
                base_f = tmp_ctx.enter_context(nc.sbuf_tensor("base_f", [P, T], F32))
                weights_in, edges_in, consts, ident_zero = s.sem("weights_in"), s.sem("edges_in"), s.sem("consts"), s.sem("ident_zero")
                floats, turned, copied, based, spread, dve_link = (
                    s.sem("floats"), s.sem("turned"), s.sem("copied"), s.sem("based"), s.sem("spread"), s.sem("dve_link"))
                loads = [(x_sb[:], x.rearrange("(k p) d -> p k d", p=P)), (beta_sb[:], beta), (rows_sb[:], rows), (cols_sb[:], cols),
                         (w0_sb[0:D, 0:D], w0t), (wm1_sb[:], wm1), (wm2_sb[:], wm2), (wm3_sb[:], wm3),
                         (wu1_sb[:], wu1.rearrange("(c k) h -> k c h", c=2)), (wu2_sb[:], wu2), (wu3_sb[:], wu3),
                         (w1a_sb[:], w1[0:D, :]), (w1b_sb[:], w1[D:D + EF, :]), (w2_sb[0:D, :], w2), (w2_sb[D:D + 1, :], b2)]
                block = s.start()

                @block.sync
                def _(sp):
                    whole = TB * P * P
                    for raw, line in ((src_raw, src), (dst_raw, dst)):
                        sp.dma_start(raw[:, 0:TB, :], line[0:whole].rearrange("(k p e) -> p k e", p=P, e=P)).then_inc(edges_in, 16)
                        sp.dma_start(raw[0:TR, TB, :], line[whole:EP].rearrange("(p e) -> p e", e=P)).then_inc(edges_in, 16)
                    for to, what in loads:
                        sp.dma_start(to, what).then_inc(weights_in, 16)
                    sp.wait_ge(weights_in, 16 * len(loads))

                @block.gpsimd
                def _(pool):
                    nc.gpsimd.memset(ident[:], 0.0).then_inc(ident_zero, 1)
                    nc.gpsimd.iota(iota[:], pattern=[[1, P]], base=0, channel_multiplier=0,
                                   allow_small_or_imprecise_dtypes=True)
                    pool.wait_ge(ident_zero, 1)
                    nc.gpsimd.affine_select(out=ident[:], in_=ident[:], compare_op=ALU.not_equal, fill=1.0,
                                            base=0, pattern=[[-1, P]], channel_multiplier=1).then_inc(consts, 1)
                    pool.wait_ge(based, 1)
                    nc.gpsimd.partition_broadcast(base_f[:], base_f[0:1, :], P).then_inc(spread, 1)

                @block.tensor
                def _(pe):
                    pe.wait_ge(consts, 1)
                    pe.wait_ge(floats, 2)
                    n = 0
                    for raw in (src_f, dst_f):
                        for k in range(TBS):
                            rows_in = P if k < TB else TR
                            if n >= 8:
                                pe.wait_ge(copied, n - 7)
                            nc.tensor.transpose(ps[:, n % 8, 0:rows_in], raw[0:rows_in, k, :], ident[0:rows_in, 0:rows_in]).then_inc(turned, 1)
                            n += 1

                @block.vector
                def _(dve):
                    nc.vector.memset(w0_sb[:, D:D + 1], 0.0).then_inc(dve_link, 1)
                    nc.vector.memset(w0_sb[D:D + 1, 0:D], 0.0)
                    nc.vector.memset(base_row[:], 0)
                    nc.vector.memset(score[:], 0.0)
                    nc.vector.memset(src_cols[:, T:], 0)
                    nc.vector.memset(hT[:], 0.0)
                    dve.wait_ge(dve_link, 1)
                    nc.vector.memset(w0_sb[D:D + 1, D:D + 1], 1.0)
                    dve.wait_ge(edges_in, 64)
                    for f, raw in ((src_f, src_raw), (dst_f, dst_raw)):
                        nc.vector.tensor_copy(f[:, 0:TB, :], raw[:, 0:TB, :])
                        nc.vector.tensor_copy(f[0:TR, TB, :], raw[0:TR, TB, :]).then_inc(floats, 1)
                    n = 0
                    for to in (src_cols, dloc):
                        for k in range(TBS):
                            cols_in = P if k < TB else TR
                            dve.wait_ge(turned, n + 1)
                            nc.vector.tensor_copy(to[:, k * P:k * P + cols_in], ps[:, n % 8, 0:cols_in]).then_inc(copied, 1)
                            n += 1
                    dve.wait_ge(copied, n)
                    nc.vector.tensor_scalar(base_f[0:1, :], dloc[0:1, :], float(NP - 1), None, ALU.min).then_inc(based, 1)
                    dve.wait_ge(spread, 1)
                    nc.vector.tensor_copy(base_row[:, HB:HB + T], base_f[0:1, :])
                    nc.vector.tensor_tensor(dloc[:], dloc[:], base_f[:], ALU.subtract)

        def norm_relu(dve, link, act_in, act_out, at):
            v = lambda i: stat[:, i, :]
            wide = lambda i: stat[:, i, :].unsqueeze(2).to_broadcast([P, NT, D])
            link(nc.vector.tensor_reduce(v(0), x_sb[:], AX_X, ALU.add))
            link(nc.vector.tensor_scalar(v(0), v(0), 1.0 / D, None, ALU.mult))
            link(nc.vector.tensor_tensor(tmp[:], x_sb[:], wide(0), ALU.subtract))
            link(nc.vector.tensor_tensor(h_sb[:, :, 0:D], tmp[:], tmp[:], ALU.mult))
            link(nc.vector.tensor_reduce(v(1), h_sb[:, :, 0:D], AX_X, ALU.add))
            nc.vector.tensor_scalar(v(1), v(1), 1.0 / D, LN_EPS, ALU.mult, ALU.add).then_inc(act_in, 1)
            dve.wait_ge(act_out, at)
            link(nc.vector.reciprocal(v(2), v(1)))
            link(nc.vector.tensor_tensor(tmp[:], tmp[:], wide(2), ALU.mult))
            link(nc.vector.tensor_scalar(h_sb[:, :, 0:D], tmp[:], 0.0, None, ALU.max))

        def turn_nodes(pe, source, ready, turned, freed):
            for k in range(NT):
                if k % 4 == 0 and k >= 32:
                    pe.wait_ge(freed, k // 4 - 7)
                last = nc.tensor.transpose(ps[0:D, (k // 4) % 8, (k % 4) * P:(k % 4 + 1) * P], source[:, k, 0:D], ident[:])
                if k % 4 == 3 or k == NT - 1:
                    last.then_inc(turned, 1)

        def save_turned(act, turned, freed):
            for q in range(-(-NT // 4)):
                act.wait_ge(turned, q + 1)
                wide = min(512, NP - q * 512)
                nc.scalar.copy(hT[:, q * 512:q * 512 + wide], ps[0:D, q % 8, 0:wide]).then_inc(freed, 1)

        def attention_nodes():
            with Stage() as s:
                dve_link, var_ready, root, norm_ready, norm_root, unit, turned, freed, stored, table_ready = (
                    s.sem(n) for n in ("dve_link", "var_ready", "root", "norm_ready", "norm_root", "unit", "turned", "freed", "stored", "table_ready"))
                block = s.start()

                @block.vector
                def _(dve):
                    link = linker(dve, dve_link)
                    norm_relu(dve, link, var_ready, root, 1)
                    nc.vector.memset(h_sb[:, :, D:D + 1], 1.0)
                    link(nc.vector.tensor_tensor(tmp[:], h_sb[:, :, 0:D], h_sb[:, :, 0:D], ALU.mult))
                    nc.vector.tensor_reduce(stat[:, 0, :], tmp[:], AX_X, ALU.add).then_inc(norm_ready, 1)
                    dve.wait_ge(norm_root, 1)
                    link(nc.vector.tensor_scalar(stat[:, 1, :], stat[:, 0, :], NORM_EPS, None, ALU.max))
                    link(nc.vector.reciprocal(stat[:, 2, :], stat[:, 1, :]))
                    nc.vector.tensor_copy(h_sb[:, :, D + 1], stat[:, 2, :]).then_inc(table_ready, 1)
                    nc.vector.tensor_tensor(tmp[:], h_sb[:, :, 0:D], stat[:, 2, :].unsqueeze(2).to_broadcast([P, NT, D]), ALU.mult).then_inc(unit, 1)

                @block.scalar
                def _(act):
                    act.wait_ge(var_ready, 1)
                    nc.scalar.activation(stat[:, 1, :], stat[:, 1, :], ACT.Sqrt).then_inc(root, 1)
                    act.wait_ge(norm_ready, 1)
                    nc.scalar.activation(stat[:, 0, :], stat[:, 0, :], ACT.Sqrt).then_inc(norm_root, 1)
                    save_turned(act, turned, freed)

                @block.tensor
                def _(pe):
                    pe.wait_ge(unit, 1)
                    turn_nodes(pe, tmp, unit, turned, freed)

                @block.sync
                def _(sp):
                    sp.wait_ge(table_ready, 1)
                    sp.dma_start(table.rearrange("(k p) d -> p k d", p=P), h_sb[:]).then_inc(stored, 16)
                    sp.wait_ge(stored, 16)

        def tile_bases(engines, at):
            _, values = nc.values_load_multi_w_load_instructions(
                base_row[0:1, bass.ds(at, HB)], engines=engines, min_val=0, max_val=NP - 1,
                skip_runtime_bounds_check_because="the setup clamps every start to the last node")
            return values

        def one_hot(h, i):
            return nc.vector.tensor_tensor(
                onehot[:, h, :, :], iota[:].unsqueeze(1).to_broadcast([P, HB, P]),
                dloc[:, bass.ds(i * BT + h * HB, HB)].unsqueeze(2).to_broadcast([P, HB, P]), ALU.is_equal)

        def gather(pool, i, h, staged, gathered, batches):
            pool.wait_ge(staged[h], i + 1)
            pool.sem_inc(batches, 1)
            for g in range(HB):
                pool.indirect_dma_start(out=got[:, h, g, :], out_offset=None, in_=table,
                                        in_offset=bass.IndirectOffsetOnAxis(ap=stage[:, h, g:g + 1].bitcast(U32), axis=0)
                                        ).then_inc(gathered[h], 16)

        def later(i, h):
            return (i, h + AHEAD) if h + AHEAD < NG else (i + 1, h + AHEAD - NG)

        def stage_indices(i, h, rows_free, staged):
            rows_free(i, h)
            nc.scalar.copy(stage[:, h, :], src_cols[:, i * BT + h * HB:i * BT + (h + 1) * HB] if isinstance(i, int)
                           else src_cols[:, bass.ds(i * BT + h * HB, HB)]).then_inc(staged[h], 1)

        def attention_scores():
            with Stage() as s:
                per_group = lambda n: [s.sem(f"{n}_{h}") for h in range(NG)]
                staged, gathered, turned, saved, dotted, used, kept, stored = (
                    per_group(n) for n in ("staged", "gathered", "turned", "saved", "dotted", "used", "kept", "stored"))
                batches, begun, picked, summed, hot = s.sem("batches"), s.sem("begun"), s.sem("picked"), s.sem("summed"), s.sem("hot")
                block = s.start()

                @block.gpsimd
                def _(pool):
                    with pool.Fori(0, NB) as i:
                        for h in range(NG):
                            gather(pool, i, h, staged, gathered, batches)

                @block.sync
                def _(sp):
                    for h in range(NG):
                        sp.sem_inc(kept[h], 1)
                    with sp.Fori(0, NB) as i:
                        for h in range(NG):
                            sp.wait_ge(gathered[h], i * (16 * HB) + 16 * HB)
                            sp.dma_start(kept_rows[bass.ds(i, 1), h, :, :].rearrange("a p f -> p (a f)"),
                                         got[:, h, :, :].rearrange("p g f -> p (g f)")).then_inc(stored[h], 16)
                            sp.wait_ge(stored[h], i * 16 + 16)
                            sp.sem_inc(kept[h], 1)

                @block.scalar
                def _(act):
                    def rows_free(i, h):
                        act.wait_ge(used[h], i + 1)
                        act.wait_ge(kept[h], i + 1)

                    def save(i, h):
                        act.wait_ge(turned[h], i + 1)
                        nc.scalar.copy(gotT[:, h, :, :], ps[0:D, h, :].rearrange("p (g e) -> p g e", e=P)).then_inc(saved[h], 1)

                    for h in range(AHEAD):
                        stage_indices(0, h, rows_free, staged)
                    with act.Fori(0, NB) as i:
                        for h in range(NG):
                            save(i, h)
                            stage_indices(*later(i, h), rows_free, staged)

                @block.tensor
                def _(pe):
                    for h in range(NG):
                        pe.sem_inc(dotted[h], 1)
                    with pe.Fori(0, NB) as i:
                        for h in range(NG):
                            bases = tile_bases(PE_ENGINE, i * BT + h * HB + HB)
                            pe.wait_ge(gathered[h], i * (16 * HB) + 16 * HB)
                            pe.sem_inc(begun, 1)
                            for g in range(HB):
                                last = nc.tensor.transpose(ps[0:D, h, g * P:(g + 1) * P], got[:, h, g, 0:D], ident[:])
                            last.then_inc(turned[h], 1)
                            pe.wait_ge(saved[h], i + 1)
                            pe.wait_ge(used[h], i + 1)
                            for g in range(HB):
                                last = nc.tensor.matmul(ps[:, NG + h, g * P:(g + 1) * P], gotT[:, h, g, :],
                                                        hT[:, bass.ds(bases[g], P)], start=True, stop=True)
                            last.then_inc(dotted[h], 1)

                @block.vector
                def _(dve):
                    for h in range(NG):
                        dve.sem_inc(used[h], 1)
                    with dve.Fori(0, NB) as i:
                        for h in range(NG):
                            one_hot(h, i).then_inc(hot, 1)
                            dve.wait_ge(hot, i * NG + h + 1)
                            dve.wait_ge(dotted[h], i + 2)
                            nc.vector.tensor_tensor(onehot[:, h, :, :], onehot[:, h, :, :],
                                                    ps[:, NG + h, :].rearrange("p (g e) -> p g e", e=P), ALU.mult).then_inc(picked, 1)
                            dve.wait_ge(picked, i * NG + h + 1)
                            nc.vector.tensor_reduce(dots[:, h, :], onehot[:, h, :, :], AX_X, ALU.add).then_inc(summed, 1)
                            dve.wait_ge(summed, i * NG + h + 1)
                            nc.vector.tensor_tensor(score[:, bass.ds(i * BT + h * HB, HB)], dots[:, h, :], got[:, h, :, D + 1], ALU.mult).then_inc(used[h], 1)

        def attention_weights():
            with ExitStack() as tmp_ctx, Stage() as s:
                def tb(name, shape, dt=F32):
                    return tmp_ctx.enter_context(nc.sbuf_tensor(name, shape, dt))
                lines = onehot[:].rearrange("p a g e -> p (a g) e")[:, 0:TBS, :]
                value = hid[:].rearrange("p a b e -> p (a b e)")[:, 0:T]
                dst_i = tb("dst_i", [P, T], I32)
                dst_l = tb("dst_l", [P, T])
                cut = tb("cut", [P, T + 1])
                run = tb("run", [P, T])
                best = tmp[:].rearrange("p k d -> p (k d)")[:, 0:T]
                ends = tb("ends", [P, 4])
                line = tb("line", [4, P])
                flat = tb("flat", [1, 12, P + 2])
                carry = tb("carry", [P, 2])
                dst_in, turned, copied, sent, back, dve_link, pe_go, pe_done, shifted, wexp, out_sent, back2, turned2 = (
                    s.sem(n) for n in ("dst_in", "turned", "copied", "sent", "back", "dve_link", "pe_go", "pe_done", "shifted",
                                       "wexp", "out_sent", "back2", "turned2"))
                row_moved = s.sem("row_moved")
                scaled = s.sem("scaled")
                whole = TB * P * P
                block = s.start()

                @block.tensor
                def _(pe):
                    pe.wait_ge(scaled, 1)
                    for k in range(TBS):
                        n_in = P if k < TB else TR
                        if k >= 8:
                            pe.wait_ge(copied, k - 7)
                        nc.tensor.transpose(ps[0:n_in, k % 8, 0:P], score[:, k * P:k * P + n_in], ident[:]).then_inc(turned, 1)
                    pe.wait_ge(pe_go, 1)
                    nc.tensor.transpose(ps[0:4, 0, 0:P], ends[:], ident[:]).then_inc(pe_done, 1)
                    pe.wait_ge(pe_go, 2)
                    for n in range(2):
                        last = nc.tensor.matmul(ps[:, 1, n:n + 1], flat[0:1, 10 + n, 0:P], ident[0:1, 0:1], start=True, stop=True)
                    last.then_inc(pe_done, 1)
                    pe.wait_ge(back2, 32)
                    pe.wait_ge(copied, TBS + 2)
                    for k in range(TBS):
                        n_in = P if k < TB else TR
                        if k >= 8:
                            pe.wait_ge(copied, TBS + 2 + k - 7)
                        nc.tensor.transpose(ps[:, k % 8, 0:n_in], lines[0:n_in, k, :], ident[0:n_in, 0:n_in]).then_inc(turned2, 1)

                @block.sync
                def _(sp):
                    sp.dma_start(dst_i[:], dst.rearrange("(p j) -> p j", p=P)).then_inc(dst_in, 16)
                    sp.wait_ge(copied, TBS)
                    sp.dma_start(edge_line[0:whole].rearrange("(k p e) -> p k e", p=P, e=P), lines[:, 0:TB, :]).then_inc(sent, 16)
                    sp.dma_start(edge_line[whole:EP].rearrange("(p e) -> p e", e=P), lines[0:TR, TB, :]).then_inc(sent, 16)
                    sp.wait_ge(sent, 32)
                    sp.dma_start(value, edge_line.rearrange("(p j) -> p j", p=P)).then_inc(back, 16)
                    sp.wait_ge(copied, TBS + 1)
                    for n in range(4):
                        sp.dma_start(flat[0:1, n, 1:P + 1], line[n:n + 1, :]).then_inc(row_moved, 16)
                    sp.wait_ge(wexp, 1)
                    sp.dma_start(weight_line.rearrange("(p j) -> p j", p=P), run[:]).then_inc(out_sent, 16)
                    sp.wait_ge(out_sent, 16)
                    sp.dma_start(lines[:, 0:TB, :], weight_line[0:whole].rearrange("(k p e) -> p k e", p=P, e=P)).then_inc(back2, 16)
                    sp.dma_start(lines[0:TR, TB, :], weight_line[whole:EP].rearrange("(p e) -> p e", e=P)).then_inc(back2, 16)
                    sp.wait_ge(back2, 32)

                @block.scalar
                def _(act):
                    act.wait_ge(shifted, 1)
                    nc.scalar.activation(run[:], run[:], ACT.Exp).then_inc(wexp, 1)

                @block.vector
                def _(dve):
                    link = linker(dve, dve_link)
                    nc.vector.tensor_scalar(score[:], score[:], beta_sb[:, 0:1], None, ALU.mult).then_inc(scaled, 1)
                    for k in range(TBS):
                        n_in = P if k < TB else TR
                        dve.wait_ge(turned, k + 1)
                        nc.vector.tensor_copy(lines[0:n_in, k, :], ps[0:n_in, k % 8, 0:P]).then_inc(copied, 1)
                    dve.wait_ge(dst_in, 16)
                    link(nc.vector.tensor_copy(dst_l[:], dst_i[:]))
                    nc.vector.memset(cut[:, 0:1], FAR)
                    nc.vector.memset(cut[:, T:T + 1], FAR)
                    link(nc.vector.tensor_tensor(cut[:, 1:T], dst_l[:, 1:T], dst_l[:, 0:T - 1], ALU.not_equal))
                    link(nc.vector.tensor_scalar(cut[:, 1:T], cut[:, 1:T], FAR, None, ALU.mult))
                    dve.wait_ge(back, 16)
                    link(nc.vector.tensor_tensor_scan(run[:], cut[:, 0:T], value, FAR, ALU.add, ALU.max))
                    link(nc.vector.tensor_tensor_scan(best[:, ::-1], cut[:, 1:T + 1][:, ::-1], value[:, ::-1], FAR, ALU.add, ALU.max))
                    nc.vector.tensor_copy(ends[:, 0:1], dst_l[:, 0:1])
                    nc.vector.tensor_copy(ends[:, 1:2], dst_l[:, T - 1:T])
                    nc.vector.tensor_copy(ends[:, 2:3], run[:, T - 1:T])
                    nc.vector.tensor_copy(ends[:, 3:4], best[:, 0:1]).then_inc(pe_go, 1)
                    dve.wait_ge(pe_done, 1)
                    link(nc.vector.memset(flat[:], -1.0))
                    nc.vector.tensor_copy(line[:], ps[0:4, 0, 0:P]).then_inc(copied, 1)
                    dve.wait_ge(row_moved, 64)
                    row = lambda n, a, b: flat[0:1, n, a:b]
                    link(nc.vector.tensor_tensor(row(4, 1, P + 2), row(0, 1, P + 2), row(1, 0, P + 1), ALU.not_equal))
                    link(nc.vector.tensor_scalar(row(4, 1, P + 2), row(4, 1, P + 2), FAR, None, ALU.mult))
                    link(nc.vector.tensor_tensor(row(5, 1, P + 1), row(0, 1, P + 1), row(1, 1, P + 1), ALU.not_equal))
                    link(nc.vector.tensor_scalar(row(5, 1, P + 1), row(5, 1, P + 1), FAR, None, ALU.mult))
                    link(nc.vector.tensor_tensor(row(6, 1, P + 1), row(4, 1, P + 1), row(5, 1, P + 1), ALU.min))
                    link(nc.vector.tensor_tensor(row(7, 1, P + 1), row(4, 2, P + 2), row(5, 1, P + 1), ALU.min))
                    link(nc.vector.memset(row(8, 0, P + 2), FAR))
                    link(nc.vector.memset(row(9, 0, P + 2), FAR))
                    link(nc.vector.tensor_tensor_scan(row(8, 1, P + 1), row(6, 1, P + 1), row(2, 1, P + 1), FAR, ALU.add, ALU.max))
                    link(nc.vector.tensor_tensor_scan(row(9, 1, P + 1)[:, ::-1], row(7, 1, P + 1)[:, ::-1], row(3, 1, P + 1)[:, ::-1], FAR, ALU.add, ALU.max))
                    link(nc.vector.tensor_tensor(row(10, 0, P), row(8, 0, P), row(4, 1, P + 1), ALU.add))
                    link(nc.vector.tensor_tensor(row(11, 0, P), row(9, 2, P + 2), row(4, 2, P + 2), ALU.add))
                    nc.vector.tensor_scalar(flat[0:1, 10:12, 0:P], flat[0:1, 10:12, 0:P], FAR, None, ALU.max).then_inc(pe_go, 1)
                    dve.wait_ge(pe_done, 2)
                    nc.vector.tensor_copy(carry[:], ps[:, 1, 0:2]).then_inc(copied, 1)
                    dve.wait_ge(copied, TBS + 2)
                    nc.vector.memset(cut[:, 0:1], 0.0)
                    link(nc.vector.memset(cut[:, T:T + 1], 0.0))
                    link(nc.vector.tensor_tensor_scan(run[:], cut[:, 0:T], value, carry[:, 0:1], ALU.add, ALU.max))
                    link(nc.vector.tensor_tensor_scan(best[:, ::-1], cut[:, 1:T + 1][:, ::-1], value[:, ::-1], carry[:, 1:2], ALU.add, ALU.max))
                    link(nc.vector.tensor_tensor(best, best, run[:], ALU.max))
                    nc.vector.tensor_tensor(run[:], value, best, ALU.subtract).then_inc(shifted, 1)
                    for k in range(TBS):
                        n_in = P if k < TB else TR
                        dve.wait_ge(turned2, k + 1)
                        nc.vector.tensor_copy(score[:, k * P:k * P + n_in], ps[:, k % 8, 0:n_in]).then_inc(copied, 1)

        def aggregate(kind, width):
            with Stage() as s:
                per_group = lambda n: [s.sem(f"{n}_{h}") for h in range(NG)]
                rows_in, ready, summed = (per_group(n) for n in ("rows_in", "ready", "summed"))
                if kind != "kept":
                    staged, batches = per_group("staged"), s.sem("batches")
                if kind == "edge":
                    joined, relued, edges_in, mapped = (per_group(n) for n in ("joined", "relued", "edges_in", "mapped"))
                added = s.sem("added")
                per_half = 16 if kind == "kept" else 16 * HB
                rows_used = joined if kind == "edge" else summed
                block = s.start()

                if kind != "kept":
                    @block.gpsimd
                    def _(pool):
                        with pool.Fori(0, NB) as i:
                            for h in range(NG):
                                gather(pool, i, h, staged, rows_in, batches)

                    @block.scalar
                    def _(act):
                        def rows_free(i, h):
                            act.wait_ge(rows_used[h], i + 1)

                        for h in range(AHEAD):
                            stage_indices(0, h, rows_free, staged)
                        with act.Fori(0, NB) as i:
                            for h in range(NG):
                                if kind == "edge":
                                    act.wait_ge(joined[h], i + 2)
                                    nc.scalar.activation(msg[:, h, :, :], msg[:, h, :, :], ACT.Relu).then_inc(relued[h], 1)
                                stage_indices(*later(i, h), rows_free, staged)

                @block.sync
                def _(sp):
                    if kind == "kept":
                        with sp.Fori(0, NB) as i:
                            for h in range(NG):
                                sp.wait_ge(summed[h], i + 1)
                                sp.dma_start(got[:, h, :, :].rearrange("p g f -> p (g f)"),
                                             kept_rows[bass.ds(i, 1), h, :, :].rearrange("a p f -> p (a f)")).then_inc(rows_in[h], 16)
                    if kind == "edge":
                        with sp.Fori(0, NB) as i:
                            for h in range(NG):
                                sp.wait_ge(mapped[h], i + 1)
                                sp.dma_start(edge_sb[:, h, :], edge_t[:, bass.ds(i * (BT * P) + h * (HB * P), HB * P)]).then_inc(edges_in[h], 16)

                @block.tensor
                def _(pe):
                    if kind == "edge":
                        for h in range(NG):
                            pe.sem_inc(mapped[h], 1)
                    with pe.Fori(0, NB) as i:
                        for h in range(NG):
                            if kind == "edge":
                                pe.wait_ge(edges_in[h], i * 16 + 16)
                                pe.wait_ge(joined[h], i + 1)
                                for g in range(HB):
                                    last = nc.tensor.matmul(ps[:, h // 2, (h % 2 * HB + g) * D:(h % 2 * HB + g + 1) * D], edge_sb[:, h, g * P:(g + 1) * P], w1b_sb[:], start=True, stop=True)
                                last.then_inc(mapped[h], 1)
                            pe.wait_ge(rows_in[h], i * per_half + per_half)
                            pe.wait_ge(ready[h], i + 1)
                            pe.wait_ge(added, i * BT + ZERO + (h - 2) * HB)
                            if kind == "edge":
                                pe.wait_ge(relued[h], i + 1)
                            for g in range(HB):
                                rows_g = msg[:, h, g, 0:width] if kind == "edge" else got[:, h, g, 0:width]
                                last = nc.tensor.matmul(ps[0:width, NG + h, g * P:(g + 1) * P], rows_g,
                                                        onehot[:, h, g, :], start=True, stop=True)
                            last.then_inc(summed[h], 1)

                @block.vector
                def _(dve):
                    nc.vector.memset(ps[0:width, 2 * NG - 1, :], 0.0).then_inc(summed[NG - 1], 1)
                    for h in range(NG - 1):
                        dve.sem_inc(summed[h], 1)
                    if kind == "edge":
                        for h in range(NG):
                            dve.sem_inc(joined[h], 1)
                    nc.vector.memset(acc[0:width, :], 0.0).then_inc(added, ZERO)

                    def add_sums(bases, count, h):
                        for g in range(HB):
                            window = acc[0:width, bass.ds(bases[g], P)]
                            dve.wait_ge(added, count + g + ZERO)
                            nc.vector.tensor_tensor(window, window, ps[0:width, NG + h, g * P:(g + 1) * P],
                                                    ALU.add).then_inc(added, 1)

                    with dve.Fori(0, NB) as i:
                        for h in range(NG):
                            dve.wait_ge(summed[h], i + 1)
                            if kind == "kept":
                                for g in range(HB):
                                    at = i * BT + h * HB + g
                                    last = nc.vector.tensor_scalar(onehot[:, h, g, :], iota[:], dloc[:, bass.ds(at, 1)], score[:, bass.ds(at, 1)],
                                                                   ALU.is_equal, ALU.mult)
                                last.then_inc(ready[h], 1)
                            else:
                                one_hot(h, i).then_inc(ready[h], 1)
                            bases = tile_bases(DVE_ENGINE, i * BT + h * HB)
                            if kind == "edge":
                                dve.wait_ge(mapped[h], i + 2)
                                dve.wait_ge(rows_in[h], i * per_half + per_half)
                                nc.vector.tensor_tensor(msg[:, h, :, :], got[:, h, :, 0:D], ps[:, h // 2, h % 2 * HB * D:(h % 2 + 1) * HB * D].rearrange("p (g d) -> p g d", d=D),
                                                        ALU.add).then_inc(joined[h], 1)
                            dve.wait_ge(summed[h - 1], i + 1 + (h > 0))
                            add_sums(bases, i * BT + h * HB, (h - 1) % NG)
                    dve.wait_ge(summed[NG - 1], NB + 1)
                    add_sums(tile_bases(DVE_ENGINE, T), T, NG - 1)

        def add_attention():
            with Stage() as s:
                dve_link, var_ready, root, out_ready, taken, stored = (
                    s.sem(n) for n in ("dve_link", "var_ready", "root", "out_ready", "taken", "stored"))
                table_ready = s.sem("table_ready")
                block = s.start()

                @block.tensor
                def _(pe):
                    for k in range(NT):
                        if k >= 8:
                            pe.wait_ge(taken, k - 7)
                        nc.tensor.matmul(ps[:, k % 8, 0:D + 1], acc[:, k * P:(k + 1) * P], w0_sb[:], start=True, stop=True).then_inc(out_ready, 1)

                @block.vector
                def _(dve):
                    link = linker(dve, dve_link)
                    for k in range(NT):
                        dve.wait_ge(out_ready, k + 1)
                        link(nc.vector.tensor_scalar(stat[:, 0, k:k + 1], ps[:, k % 8, D:D + 1], 1e-30, None, ALU.max))
                        link(nc.vector.reciprocal(stat[:, 1, k:k + 1], stat[:, 0, k:k + 1]))
                        nc.vector.scalar_tensor_tensor(x_sb[:, k, :], ps[:, k % 8, 0:D], stat[:, 1, k:k + 1], x_sb[:, k, :],
                                                       ALU.mult, ALU.add).then_inc(taken, 1)
                    dve.wait_ge(taken, NT)
                    norm_relu(dve, link, var_ready, root, 1)
                    dve.sem_inc(table_ready, 1)

                @block.scalar
                def _(act):
                    act.wait_ge(var_ready, 1)
                    nc.scalar.activation(stat[:, 1, :], stat[:, 1, :], ACT.Sqrt).then_inc(root, 1)

                @block.sync
                def _(sp):
                    sp.wait_ge(table_ready, 1)
                    sp.dma_start(table.rearrange("(k p) d -> p k d", p=P), h_sb[:]).then_inc(stored, 16)
                    sp.wait_ge(stored, 16)

        CH = [(c, min(512, NP - c)) for c in range(0, NP, 512)]

        def mlp(s, first, last_w, last_rows, take, bias, sems, second):
            m1, a1, m2, a2, m3, t3 = sems

            def tensor(pe, start_waits):
                start_waits(pe)
                for n, (c, wide) in enumerate(CH):
                    if n >= 2:
                        pe.wait_ge(a1, n - 1)
                    for j, (w, rows_of) in enumerate(first):
                        last = nc.tensor.matmul(ps[:, n % 2, 0:wide], w, rows_of[0:D, c:c + wide], start=(j == 0), stop=(j == len(first) - 1))
                    last.then_inc(m1, 1)
                    pe.wait_ge(a1, n + 1)
                    nc.tensor.matmul(ps[:, 2 + n % 2, 0:wide], second, hid[:, 0, n % 2, 0:wide], start=True, stop=True).then_inc(m2, 1)
                    pe.wait_ge(a2, n + 1)
                    if n >= 2:
                        pe.wait_ge(t3, n - 1)
                    for q in range(wide // P):
                        last = nc.tensor.matmul(ps[:, 4 + n % 2, q * D:(q + 1) * D], hid[:, 1, n % 2, q * P:(q + 1) * P], last_w, start=True, stop=True)
                    last.then_inc(m3, 1)

            def scalar(act):
                for n, (c, wide) in enumerate(CH):
                    act.wait_ge(m1, n + 1)
                    if n >= 2:
                        act.wait_ge(m2, n - 1)
                    nc.scalar.activation(hid[:, 0, n % 2, 0:wide], ps[:, n % 2, 0:wide], ACT.Relu, bias=cols_sb[:, bias:bias + 1]).then_inc(a1, 1)
                    act.wait_ge(m2, n + 1)
                    if n >= 2:
                        act.wait_ge(m3, n - 1)
                    nc.scalar.activation(hid[:, 1, n % 2, 0:wide], ps[:, 2 + n % 2, 0:wide], ACT.Relu, bias=cols_sb[:, bias + 1:bias + 2]).then_inc(a2, 1)

            def vector(dve):
                for n, (c, wide) in enumerate(CH):
                    dve.wait_ge(m3, n + 1)
                    q = wide // P
                    take(c // P, q, ps[:, 4 + n % 2, 0:q * D].rearrange("p (k d) -> p k d", d=D)).then_inc(t3, 1)

            return tensor, scalar, vector

        def row_of(name, q):
            return rows_sb[:, ROWS.index(name), :].unsqueeze(1).to_broadcast([P, q, D])

        def message_nodes():
            with Stage() as s:
                dve_link, var_ready, root, out_ready, taken, stored, h_ready, turned, freed, table_ready = (
                    s.sem(n) for n in ("dve_link", "var_ready", "root", "out_ready", "taken", "stored", "h_ready", "turned", "freed", "table_ready"))
                sems = [s.sem(n) for n in ("m1", "a1", "m2", "a2", "m3", "t3")]
                take = lambda k, q, got_ps: nc.vector.tensor_tensor(tmp[:, k:k + q, :], got_ps, row_of("bM3", q), ALU.add)
                tensor, scalar, vector = mlp(s, [(wm1_sb[:], hT)], wm3_sb[:], None, take, 0, sems, wm2_sb[:])
                block = s.start()

                @block.tensor
                def _(pe):
                    for k in range(NT):
                        if k >= 8:
                            pe.wait_ge(taken, k - 7)
                        nc.tensor.matmul(ps[:, k % 8, 0:D + 1], acc[:, k * P:(k + 1) * P], ident[0:D + 1, 0:D + 1], start=True, stop=True).then_inc(out_ready, 1)
                    pe.wait_ge(h_ready, 1)
                    turn_nodes(pe, h_sb, h_ready, turned, freed)
                    tensor(pe, lambda pe: pe.wait_ge(freed, -(-NT // 4)))

                @block.vector
                def _(dve):
                    link = linker(dve, dve_link)
                    for k in range(NT):
                        dve.wait_ge(out_ready, k + 1)
                        nc.vector.tensor_copy(count[:, k:k + 1], ps[:, k % 8, D:D + 1])
                        nc.vector.tensor_tensor(x_sb[:, k, :], ps[:, k % 8, 0:D], x_sb[:, k, :], ALU.add).then_inc(taken, 1)
                    dve.wait_ge(taken, NT)
                    norm_relu(dve, link, var_ready, root, 1)
                    dve.sem_inc(h_ready, 1)
                    vector(dve)
                    dve.wait_ge(sems[5], len(CH))
                    dve.sem_inc(table_ready, 1)

                @block.scalar
                def _(act):
                    act.wait_ge(var_ready, 1)
                    nc.scalar.activation(stat[:, 1, :], stat[:, 1, :], ACT.Sqrt).then_inc(root, 1)
                    save_turned(act, turned, freed)
                    scalar(act)

                @block.sync
                def _(sp):
                    sp.wait_ge(table_ready, 1)
                    sp.dma_start(table.rearrange("(k p) d -> p k d", p=P)[:, :, 0:D], tmp[:]).then_inc(stored, 16)
                    sp.wait_ge(stored, 16)

        def update_nodes():
            with Stage() as s:
                dve_link, var_ready, root, stored, h_ready, turned, freed, table_ready = (
                    s.sem(n) for n in ("dve_link", "var_ready", "root", "stored", "h_ready", "turned", "freed", "table_ready"))
                mapped, taken = s.sem("mapped"), s.sem("taken")
                biased = s.sem("biased")
                sems = [s.sem(n) for n in ("m1", "a1", "m2", "a2", "m3", "t3")]
                take = lambda k, q, got_ps: nc.vector.tensor_tensor(x_sb[:, k:k + q, :], got_ps, x_sb[:, k:k + q, :], ALU.add)
                tensor, scalar, vector = mlp(s, [(wu1_sb[:, 0, :], hT), (wu1_sb[:, 1, :], acc)], wu3_sb[:], None, take, 2, sems, wu2_sb[:])
                block = s.start()

                @block.tensor
                def _(pe):
                    pe.wait_ge(biased, 1)
                    tensor(pe, lambda pe: None)
                    pe.wait_ge(h_ready, 1)
                    turn_nodes(pe, h_sb, h_ready, turned, freed)
                    pe.wait_ge(freed, -(-NT // 4))
                    for k in range(NT):
                        if k % 8 == 0 and k >= 64:
                            pe.wait_ge(taken, k // 8 - 7)
                        last = nc.tensor.matmul(ps[:, (k // 8) % 8, (k % 8) * D:(k % 8 + 1) * D], hT[:, k * P:(k + 1) * P], w1a_sb[:], start=True, stop=True)
                        if k % 8 == 7 or k == NT - 1:
                            last.then_inc(mapped, 1)

                @block.vector
                def _(dve):
                    link = linker(dve, dve_link)
                    nc.vector.tensor_tensor(x_sb[:], x_sb[:], row_of("bU3", NT), ALU.add).then_inc(biased, 1)
                    vector(dve)
                    dve.wait_ge(sems[5], len(CH))
                    norm_relu(dve, link, var_ready, root, 1)
                    dve.sem_inc(h_ready, 1)
                    for b in range(-(-NT // 8)):
                        q = min(8, NT - 8 * b)
                        dve.wait_ge(mapped, b + 1)
                        last = nc.vector.tensor_tensor(tmp[:, 8 * b:8 * b + q, :], ps[:, b % 8, 0:q * D].rearrange("p (k d) -> p k d", d=D),
                                                       row_of("b1", q), ALU.add)
                        last.then_inc(taken, 1)
                    dve.wait_ge(taken, -(-NT // 8))
                    dve.sem_inc(table_ready, 1)

                @block.scalar
                def _(act):
                    scalar(act)
                    act.wait_ge(var_ready, 1)
                    nc.scalar.activation(stat[:, 1, :], stat[:, 1, :], ACT.Sqrt).then_inc(root, 1)
                    save_turned(act, turned, freed)

                @block.sync
                def _(sp):
                    sp.wait_ge(table_ready, 1)
                    sp.dma_start(table.rearrange("(k p) d -> p k d", p=P)[:, :, 0:D], tmp[:]).then_inc(stored, 16)
                    sp.wait_ge(stored, 16)

        def finish_nodes():
            with Stage() as s:
                dve_link, out_ready, taken, var_ready, root, stored, done, count_turned, count_row = (
                    s.sem(n) for n in ("dve_link", "out_ready", "taken", "var_ready", "root", "stored", "done", "count_turned", "count_row"))
                block = s.start()

                @block.tensor
                def _(pe):
                    for k in range(NT):
                        if k >= 8:
                            pe.wait_ge(taken, k - 7)
                        nc.tensor.matmul(ps[:, k % 8, 0:D], acc[0:D, k * P:(k + 1) * P], w2_sb[0:D, :], start=True, stop=False)
                        nc.tensor.matmul(ps[:, k % 8, 0:D], acc[D:D + 1, k * P:(k + 1) * P], w2_sb[D:D + 1, :], start=False, stop=True).then_inc(out_ready, 1)

                @block.vector
                def _(dve):
                    link = linker(dve, dve_link)
                    link(nc.vector.tensor_scalar(stat[:, 0, :], count[:], 1.0, None, ALU.max))
                    link(nc.vector.reciprocal(stat[:, 1, :], stat[:, 0, :]))
                    for k in range(NT):
                        dve.wait_ge(out_ready, k + 1)
                        nc.vector.scalar_tensor_tensor(tmp[:, k, :], ps[:, k % 8, 0:D], stat[:, 1, k:k + 1], h_sb[:, k, 0:D],
                                                       ALU.mult, ALU.add).then_inc(taken, 1)
                    dve.wait_ge(taken, NT)
                    v = lambda i: stat[:, i, :]
                    wide = lambda i: stat[:, i, :].unsqueeze(2).to_broadcast([P, NT, D])
                    link(nc.vector.tensor_reduce(v(0), tmp[:], AX_X, ALU.add))
                    link(nc.vector.tensor_scalar(v(0), v(0), 1.0 / D, None, ALU.mult))
                    link(nc.vector.tensor_tensor(tmp[:], tmp[:], wide(0), ALU.subtract))
                    link(nc.vector.tensor_tensor(h_sb[:, :, 0:D], tmp[:], tmp[:], ALU.mult))
                    link(nc.vector.tensor_reduce(v(1), h_sb[:, :, 0:D], AX_X, ALU.add))
                    nc.vector.tensor_scalar(v(1), v(1), 1.0 / D, LN_EPS, ALU.mult, ALU.add).then_inc(var_ready, 1)
                    dve.wait_ge(root, 1)
                    link(nc.vector.reciprocal(v(2), v(1)))
                    link(nc.vector.tensor_tensor(tmp[:], tmp[:], wide(2), ALU.mult))
                    link(nc.vector.tensor_tensor(tmp[:], tmp[:], row_of("gamma", NT), ALU.mult))
                    link(nc.vector.tensor_tensor(tmp[:], tmp[:], row_of("beta3", NT), ALU.add))
                    nc.vector.tensor_tensor(x_sb[:], x_sb[:], tmp[:], ALU.add).then_inc(done, 1)

                @block.scalar
                def _(act):
                    act.wait_ge(var_ready, 1)
                    nc.scalar.activation(stat[:, 1, :], stat[:, 1, :], ACT.Sqrt).then_inc(root, 1)

                @block.sync
                def _(sp):
                    sp.wait_ge(done, 1)
                    sp.dma_start(out.rearrange("(k p) d -> p k d", p=P), x_sb[:]).then_inc(stored, 16)
                    sp.wait_ge(stored, 16)

        load_indices()
        attention_nodes()
        attention_scores()
        attention_weights()
        aggregate("kept", D + 1)
        add_attention()
        aggregate("table", D + 1)
        message_nodes()
        aggregate("table", D)
        update_nodes()
        aggregate("edge", D)
        finish_nodes()


def kernel(x, src, dst, edge_attr_32, L0_gnn_W, L0_gnn_beta, L2_gnn_WM1, L2_gnn_bM1, L2_gnn_WM2, L2_gnn_bM2, L2_gnn_WM3, L2_gnn_bM3,
           L2_gnn_WU1, L2_gnn_bU1, L2_gnn_WU2, L2_gnn_bU2, L2_gnn_WU3, L2_gnn_bU3, L3_gnn_W1, L3_gnn_b1, L3_gnn_W2, L3_gnn_b2,
           L3_gnn_gamma, L3_gnn_beta):
    import numpy as np
    import concourse.bacc as bacc
    from concourse.bass_utils import run_bass_kernel_spmd

    f = np.float32
    x_pad = np.zeros((NP, D), f)
    x_pad[:N] = x
    src_pad = np.zeros(EP, np.int32)
    src_pad[:E] = src
    dst_pad = np.full(EP, PAD_DST, np.int32)
    dst_pad[:E] = dst
    edge_t = np.zeros((EF, EP), f)
    edge_t[:, :E] = np.asarray(edge_attr_32).T
    row_vectors = [L2_gnn_bM3, L2_gnn_bU3, L3_gnn_b1, L3_gnn_gamma, L3_gnn_beta]
    rows = np.ascontiguousarray(np.broadcast_to(np.stack([np.asarray(v) for v in row_vectors])[None], (P, len(row_vectors), D)))
    cols = np.ascontiguousarray(np.stack([np.asarray(v) for v in (L2_gnn_bM1, L2_gnn_bM2, L2_gnn_bU1, L2_gnn_bU2)], axis=1))
    arrays = {
        "x": x_pad, "src": src_pad, "dst": dst_pad, "edge_t": edge_t,
        "beta": np.ascontiguousarray(np.broadcast_to(np.asarray(L0_gnn_beta)[None], (P, 1))), "rows": rows, "cols": cols,
        "w0t": np.ascontiguousarray(np.asarray(L0_gnn_W).T),
        "wm1": np.asarray(L2_gnn_WM1), "wm2": np.asarray(L2_gnn_WM2), "wm3": np.asarray(L2_gnn_WM3),
        "wu1": np.asarray(L2_gnn_WU1), "wu2": np.asarray(L2_gnn_WU2), "wu3": np.asarray(L2_gnn_WU3),
        "w1": np.asarray(L3_gnn_W1), "w2": np.asarray(L3_gnn_W2), "b2": np.asarray(L3_gnn_b2).reshape(1, D),
    }
    nc = bacc.Bacc("TRN2", target_bir_lowering=False, num_devices=1)
    args = [nc.dram_tensor("in_" + n, a.shape, mybir.dt.from_np(a.dtype), kind="ExternalInput").ap() for n, a in arrays.items()]
    result = nc.dram_tensor("out_x", (NP, D), F32, kind="ExternalOutput").ap()
    gnn_kernel(nc, *args, result)
    r = run_bass_kernel_spmd(nc, [{"in_" + n: a for n, a in arrays.items()}], core_ids=[0])
    return r.results[0]["out_x"][:N]
```

```python
from contextlib import ExitStack

import concourse.bass as bass
from concourse import mybir

P = 128
D = 64
EF = 32
H = 128
N = 6250
E = 206250
NT = -(-N // P)
NP = NT * P
HB = 4
NG = 4
AHEAD = 2
BT = NG * HB
ZERO = 1 + (NG - 2) * HB
NB = -(-E // (P * BT))
T = NB * BT
EP = T * P
TB = T // P
TR = T - TB * P
TBS = TB + 1
TW = D + 2
ACC = NP + P
PAD_DST = 16384
SPAN = 32
CD = 9
CW = P // CD
WD = CW * CD
NW = -(-N // WD)
NC = NW * CW
CT = 4
KEYS = NT * CD
WT = 36
CP = NC // 7
GROUP_CHUNKS = [2, 2, 2, 1] * 2
SPLIT = 3
LN_EPS = 1e-5
NORM_EPS = 1e-12
FAR = -1.0e38

ALU = mybir.AluOpType
ACT = mybir.ActivationFunctionType
F32 = mybir.dt.float32
I32 = mybir.dt.int32
U32 = mybir.dt.uint32
BF16 = mybir.dt.bfloat16
F16 = mybir.dt.float16
AX_X = mybir.AxisListType.X
PE_ENGINE = [mybir.EngineType.PE]
DVE_ENGINE = [mybir.EngineType.DVE]
ROWS = ["bM3", "bU3", "b1", "gamma", "beta3"]
assert EP == T * P and NC == 7 * CP and sum(GROUP_CHUNKS) == CW and 2 * NW + 1 == NB and NW % 2 == 0 and NW * WD <= ACC and NT % 2


def gnn_kernel(nc, x, src, dst, edge_t, beta, rows, cols, w0t, wm1, wm2, wm3, wu1, wu2, wu3, w1, w2, b2, out):
    ctx = ExitStack()
    with ctx:
        def sb(name, shape, dt=F32):
            return ctx.enter_context(nc.sbuf_tensor(name, shape, dt))

        table = nc.dram_tensor("node_table", [NP, TW], F32, kind="Internal").ap()
        kept_rows = nc.dram_tensor("kept_rows", [P, T * TW], F32, kind="Internal").ap()
        counts = nc.dram_tensor("counts", [NW, 2, P, WD * NT // 2], F16, kind="Internal").ap()
        tiles_before = nc.dram_tensor("tiles_before", [8 * CP], F32, kind="Internal").ap()
        edge_line = nc.dram_tensor("edge_line", [EP], F32, kind="Internal").ap()
        weight_line = nc.dram_tensor("weight_line", [EP], F32, kind="Internal").ap()

        ident = sb("ident", [P, P])
        iota = sb("iota", [P, P])
        iota_lo = sb("iota_lo", [P, P], F16)
        iota_key = sb("iota_key", [P, KEYS], F16)
        beta_sb = sb("beta_sb", [P, 1])
        rows_sb = sb("rows_sb", [P, len(ROWS), D])
        cols_sb = sb("cols_sb", [P, 4])
        w0_sb = sb("w0_sb", [D + 1, D + 1])
        wm1_sb = sb("wm1_sb", [D, H])
        wm2_sb = sb("wm2_sb", [H, H])
        wm3_sb = sb("wm3_sb", [H, D])
        wu1_sb = sb("wu1_sb", [D, 2, H])
        wu2_sb = sb("wu2_sb", [H, H])
        wu3_sb = sb("wu3_sb", [H, D])
        w1a_sb = sb("w1a_sb", [D, D])
        w1b_sb = sb("w1b_sb", [EF, D])
        w2_sb = sb("w2_sb", [D + 1, D])
        src_cols = sb("src_cols", [P, T + AHEAD * HB], I32)
        dst_cols = sb("dst_cols", [P, T])
        dloc = sb("dloc", [P, T])
        key_lo = sb("key_lo", [P, T, 2])
        key_start = sb("key_start", [P, NC + 2, 2])
        window_start = sb("window_start", [P, NW])
        chunk_tile = sb("chunk_tile", [1, NC + 2], I32)
        window_tile = sb("window_tile", [1, NW], I32)
        regular = sb("regular", [1, 1], I32)
        score = sb("score", [P, T])
        base_row = sb("base_row", [1, HB + T], I32)
        x_sb = sb("x_sb", [P, NT, D])
        h_sb = sb("h_sb", [P, NT, TW])
        tmp = sb("tmp", [P, NT, D])
        stat = sb("stat", [P, 4, NT])
        count = sb("count", [P, NT])
        acc = sb("acc", [D + 1, ACC])
        hT = sb("hT", [D, ACC])
        ps = ctx.enter_context(nc.psum_tensor("ps", [P, 8, 512], F32))

        stages = [0]

        class Stage:

            def __init__(self):
                stages[0] += 1
                self.tag = f"s{stages[0]}_"
                self.ctx = ExitStack()
                self.sems = []

            def __enter__(self):
                return self

            def sem(self, name):
                self.sems.append(nc.alloc_semaphore(name=self.tag + name))
                return self.sems[-1]

            def sb(self, name, shape, dt=F32):
                return self.ctx.enter_context(nc.sbuf_tensor(self.tag + name, shape, dt))

            def start(self):
                self.idle = self.sem("idle")
                return self.ctx.enter_context(nc.Block())

            def __exit__(self, *what):
                self.ctx.__exit__(*what)
                if what[0] is None:
                    nc.clear_and_free_semaphores(self.sems)
                    nc.all_engine_barrier()

        def linker(eng, sem):
            done = [0]

            def link(ins, n=1):
                done[0] += n
                ins.then_inc(sem, n)
                eng.wait_ge(sem, done[0])
            return link

        def load_indices():
            with Stage() as s:
                src_raw, dst_raw = s.sb("src_raw", [P, TBS, P], I32), s.sb("dst_raw", [P, TBS, P], I32)
                src_f, dst_f = s.sb("src_f", [P, TBS, P]), s.sb("dst_f", [P, TBS, P])
                first = s.sb("first", [P, T])
                below = s.sb("below", [P, T])
                threshold = s.sb("threshold", [P, 8])
                before = s.sb("before", [P, 8])
                row = s.sb("row", [1, 4, 8 * CP])
                ints = h_sb[:].rearrange("p k d -> p (k d)")[:, 0:2 * T].bitcast(I32).rearrange("p (a t) -> p a t", a=2)
                verdict = s.sb("verdict", [1, 8])
                names = ("weights_in", "edges_in", "consts", "zeroed", "floats", "turned", "copied", "first_row", "spread",
                         "dve_link", "counted", "row_out", "row_back", "numbered")
                (weights_in, edges_in, consts, zeroed, floats, turned, copied, first_row, spread,
                 dve_link, counted, row_out, row_back, numbered) = (s.sem(n) for n in names)
                loads = [(x_sb[:], x.rearrange("(k p) d -> p k d", p=P)), (beta_sb[:], beta), (rows_sb[:], rows), (cols_sb[:], cols),
                         (w0_sb[0:D, 0:D], w0t), (wm1_sb[:], wm1), (wm2_sb[:], wm2), (wm3_sb[:], wm3),
                         (wu1_sb[:], wu1.rearrange("(c k) h -> k c h", c=2)), (wu2_sb[:], wu2), (wu3_sb[:], wu3),
                         (w1a_sb[:], w1[0:D, :]), (w1b_sb[:], w1[D:D + EF, :]), (w2_sb[0:D, :], w2), (w2_sb[D:D + 1, :], b2)]
                block = s.start()

                @block.sync
                def _(sp):
                    whole = TB * P * P
                    for raw, line in ((src_raw, src), (dst_raw, dst)):
                        sp.dma_start(raw[:, 0:TB, :], line[0:whole].rearrange("(k p e) -> p k e", p=P, e=P)).then_inc(edges_in, 16)
                        sp.dma_start(raw[0:TR, TB, :], line[whole:EP].rearrange("(p e) -> p e", e=P)).then_inc(edges_in, 16)
                    for to, what in loads:
                        sp.dma_start(to, what).then_inc(weights_in, 16)
                    sp.wait_ge(counted, 1)
                    sp.dma_start(tiles_before.rearrange("(b p) -> p b", p=CP), before[0:CP, :],
                                 allow_slow_non_contiguous=True).then_inc(row_out, 16)
                    sp.wait_ge(row_out, 16)
                    sp.dma_start(row[0:1, 0, :], tiles_before.rearrange("(a n) -> a n", a=1)).then_inc(row_back, 16)
                    sp.wait_ge(row_back, 16)
                    sp.wait_ge(weights_in, 16 * len(loads))

                @block.gpsimd
                def _(pool):
                    nc.gpsimd.memset(ident[:], 0.0).then_inc(zeroed, 1)
                    numbers = dict(allow_small_or_imprecise_dtypes=True)
                    nc.gpsimd.iota(iota[:], pattern=[[1, P]], base=0, channel_multiplier=0, **numbers)
                    nc.gpsimd.iota(iota_lo[:], pattern=[[1, P]], base=0, channel_multiplier=0, **numbers)
                    nc.gpsimd.iota(iota_key[:], pattern=[[1, KEYS]], base=0, channel_multiplier=0, **numbers)
                    nc.gpsimd.iota(threshold[:], pattern=[[CD * CP, 8]], base=0, channel_multiplier=CD, **numbers)
                    nc.gpsimd.iota(window_start[:], pattern=[[WD, NW]], base=0, channel_multiplier=0, **numbers)
                    nc.gpsimd.memset(key_start[:], 0.0).then_inc(zeroed, 1)
                    pool.wait_ge(zeroed, 2)
                    nc.gpsimd.iota(key_start[:, :, 0], pattern=[[KEYS, NC + 2]], base=0, channel_multiplier=0, **numbers)
                    nc.gpsimd.affine_select(out=ident[:], in_=ident[:], compare_op=ALU.not_equal, fill=1.0,
                                            base=0, pattern=[[-1, P]], channel_multiplier=1).then_inc(consts, 1)
                    pool.wait_ge(first_row, 1)
                    nc.gpsimd.partition_broadcast(first[:], dst_cols[0:1, :], P).then_inc(spread, 1)

                @block.tensor
                def _(pe):
                    pe.wait_ge(consts, 1)
                    pe.wait_ge(floats, 2)
                    n = 0
                    for raw in (src_f, dst_f):
                        for k in range(TBS):
                            rows_in = P if k < TB else TR
                            if n >= 8:
                                pe.wait_ge(copied, n - 7)
                            nc.tensor.transpose(ps[:, n % 8, 0:rows_in], raw[0:rows_in, k, :], ident[0:rows_in, 0:rows_in]).then_inc(turned, 1)
                            n += 1

                @block.vector
                def _(dve):
                    link = linker(dve, dve_link)
                    nc.vector.memset(w0_sb[:, D:D + 1], 0.0)
                    nc.vector.memset(w0_sb[D:D + 1, 0:D], 0.0)
                    nc.vector.memset(base_row[:], 0)
                    nc.vector.memset(score[:], 0.0)
                    nc.vector.memset(src_cols[:, T:], 0)
                    link(nc.vector.memset(hT[:], 0.0))
                    nc.vector.memset(w0_sb[D:D + 1, D:D + 1], 1.0)
                    dve.wait_ge(edges_in, 64)
                    for f, raw in ((src_f, src_raw), (dst_f, dst_raw)):
                        nc.vector.tensor_copy(f[:, 0:TB, :], raw[:, 0:TB, :])
                        nc.vector.tensor_copy(f[0:TR, TB, :], raw[0:TR, TB, :]).then_inc(floats, 1)
                    n = 0
                    for to in (src_cols, dst_cols):
                        for k in range(TBS):
                            cols_in = P if k < TB else TR
                            dve.wait_ge(turned, n + 1)
                            nc.vector.tensor_copy(to[:, k * P:k * P + cols_in], ps[:, n % 8, 0:cols_in]).then_inc(copied, 1)
                            n += 1
                    dve.wait_ge(copied, n)
                    dve.sem_inc(first_row, 1)
                    low, high = (raw[:].rearrange("p k e -> p (k e)")[:, 0:T] for raw in (src_raw, dst_raw))
                    nc.vector.tensor_copy(ints[:, 0, :], src_cols[:, 0:T])
                    link(nc.vector.tensor_copy(ints[:, 1, :], dst_cols[:]))
                    nc.vector.tensor_scalar(low, ints[:, 0, :], 127, None, ALU.bitwise_and)
                    link(nc.vector.tensor_scalar(high, ints[:, 0, :], 7, None, ALU.arith_shift_right))
                    nc.vector.tensor_copy(key_lo[:, :, 1], low)
                    link(nc.vector.tensor_copy(key_lo[:, :, 0], high))
                    link(nc.vector.tensor_scalar(low, ints[:, 1, :], -(CD - 1) / 2, 1.0 / CD, ALU.add, ALU.mult))
                    link(nc.vector.scalar_tensor_tensor(high, low, -float(CD), ints[:, 1, :], ALU.mult, ALU.add))
                    link(nc.vector.scalar_tensor_tensor(key_lo[:, :, 0], high, float(NT), key_lo[:, :, 0], ALU.mult, ALU.add))
                    link(nc.vector.scalar_tensor_tensor(key_lo[:, :, 0], low, float(KEYS), key_lo[:, :, 0], ALU.mult, ALU.add))
                    dve.wait_ge(spread, 1)
                    for b in range(8):
                        link(nc.vector.tensor_scalar(below[:], first[:], threshold[:, b:b + 1], 0.0, ALU.is_lt, ALU.add, accum_out=before[:, b:b + 1]))
                    dve.sem_inc(counted, 1)
                    link(nc.vector.tensor_scalar(first[:], first[:], float(N), None, ALU.min))
                    nc.vector.tensor_copy(base_row[:, HB:HB + T], first[0:1, :])
                    nc.vector.tensor_tensor(dloc[:], dst_cols[:], first[:], ALU.subtract)
                    link(nc.vector.tensor_tensor(below[0:1, 1:T], first[0:1, 1:T], first[0:1, 0:T - 1], ALU.subtract))
                    link(nc.vector.tensor_reduce(verdict[:, 4:5], below[0:1, 1:T], AX_X, ALU.max))
                    dve.wait_ge(row_back, 16)
                    r = lambda n, *at: row[0:1, n, slice(*at)]
                    link(nc.vector.tensor_scalar(r(1, NC), r(0, NC), -1.0, 0.0, ALU.add, ALU.max))
                    nc.vector.memset(chunk_tile[:, NC:], 0)
                    nc.vector.tensor_scalar(chunk_tile[:, 0:NC], r(1, NC), float(T - CT), None, ALU.min)
                    nc.vector.tensor_scalar(window_tile[:], r(1, 0, NC, CW), float(T - WT), None, ALU.min)
                    nc.vector.tensor_tensor(r(2, NC), r(0, 1, NC + 1), r(1, NC), ALU.subtract)
                    link(nc.vector.tensor_tensor(r(3, NW), r(0, CW, NC + 1, CW), r(1, 0, NC, CW), ALU.subtract))
                    nc.vector.tensor_reduce(verdict[:, 0:1], r(2, NC), AX_X, ALU.max)
                    link(nc.vector.tensor_reduce(verdict[:, 1:2], r(3, NW), AX_X, ALU.max))
                    nc.vector.tensor_scalar(verdict[:, 2:3], verdict[:, 0:1], float(CT), None, ALU.is_le)
                    nc.vector.tensor_scalar(verdict[:, 5:6], verdict[:, 4:5], float(SPAN), None, ALU.is_lt)
                    link(nc.vector.tensor_scalar(verdict[:, 3:4], verdict[:, 1:2], float(WT), None, ALU.is_le))
                    link(nc.vector.tensor_tensor(verdict[:, 6:7], verdict[:, 2:3], verdict[:, 3:4], ALU.mult))
                    nc.vector.tensor_tensor(regular[:], verdict[:, 5:6], verdict[:, 6:7], ALU.mult)

        def norm_relu(dve, link, act_in, act_out, at):
            v = lambda i: stat[:, i, :]
            wide = lambda i: stat[:, i, :].unsqueeze(2).to_broadcast([P, NT, D])
            link(nc.vector.tensor_reduce(v(0), x_sb[:], AX_X, ALU.add))
            link(nc.vector.tensor_scalar(v(0), v(0), 1.0 / D, None, ALU.mult))
            link(nc.vector.tensor_tensor(tmp[:], x_sb[:], wide(0), ALU.subtract))
            link(nc.vector.tensor_tensor(h_sb[:, :, 0:D], tmp[:], tmp[:], ALU.mult))
            link(nc.vector.tensor_reduce(v(1), h_sb[:, :, 0:D], AX_X, ALU.add))
            nc.vector.tensor_scalar(v(1), v(1), 1.0 / D, LN_EPS, ALU.mult, ALU.add).then_inc(act_in, 1)
            dve.wait_ge(act_out, at)
            link(nc.vector.reciprocal(v(2), v(1)))
            link(nc.vector.tensor_tensor(tmp[:], tmp[:], wide(2), ALU.mult))
            link(nc.vector.tensor_scalar(h_sb[:, :, 0:D], tmp[:], 0.0, None, ALU.max))

        def turn_nodes(pe, source, ready, turned, freed):
            for k in range(NT):
                if k % 4 == 0 and k >= 32:
                    pe.wait_ge(freed, k // 4 - 7)
                last = nc.tensor.transpose(ps[0:D, (k // 4) % 8, (k % 4) * P:(k % 4 + 1) * P], source[:, k, 0:D], ident[:])
                if k % 4 == 3 or k == NT - 1:
                    last.then_inc(turned, 1)

        def save_turned(act, turned, freed):
            for q in range(-(-NT // 4)):
                act.wait_ge(turned, q + 1)
                wide = min(512, NP - q * 512)
                nc.scalar.copy(hT[:, q * 512:q * 512 + wide], ps[0:D, q % 8, 0:wide]).then_inc(freed, 1)

        def attention_nodes():
            with Stage() as s:
                dve_link, var_ready, root, norm_ready, norm_root, unit, turned, freed, stored, table_ready = (
                    s.sem(n) for n in ("dve_link", "var_ready", "root", "norm_ready", "norm_root", "unit", "turned", "freed", "stored", "table_ready"))
                block = s.start()

                @block.vector
                def _(dve):
                    link = linker(dve, dve_link)
                    norm_relu(dve, link, var_ready, root, 1)
                    nc.vector.memset(h_sb[:, :, D:D + 1], 1.0)
                    link(nc.vector.tensor_tensor(tmp[:], h_sb[:, :, 0:D], h_sb[:, :, 0:D], ALU.mult))
                    nc.vector.tensor_reduce(stat[:, 0, :], tmp[:], AX_X, ALU.add).then_inc(norm_ready, 1)
                    dve.wait_ge(norm_root, 1)
                    link(nc.vector.tensor_scalar(stat[:, 1, :], stat[:, 0, :], NORM_EPS, None, ALU.max))
                    link(nc.vector.reciprocal(stat[:, 2, :], stat[:, 1, :]))
                    nc.vector.tensor_copy(h_sb[:, :, D + 1], stat[:, 2, :]).then_inc(table_ready, 1)
                    nc.vector.tensor_tensor(tmp[:], h_sb[:, :, 0:D], stat[:, 2, :].unsqueeze(2).to_broadcast([P, NT, D]), ALU.mult).then_inc(unit, 1)

                @block.scalar
                def _(act):
                    act.wait_ge(var_ready, 1)
                    nc.scalar.activation(stat[:, 1, :], stat[:, 1, :], ACT.Sqrt).then_inc(root, 1)
                    act.wait_ge(norm_ready, 1)
                    nc.scalar.activation(stat[:, 0, :], stat[:, 0, :], ACT.Sqrt).then_inc(norm_root, 1)
                    save_turned(act, turned, freed)

                @block.tensor
                def _(pe):
                    pe.wait_ge(unit, 1)
                    turn_nodes(pe, tmp, unit, turned, freed)

                @block.sync
                def _(sp):
                    sp.wait_ge(table_ready, 1)
                    sp.dma_start(table.rearrange("(k p) d -> p k d", p=P), h_sb[:]).then_inc(stored, 16)
                    sp.wait_ge(stored, 16)

        def tile_bases(engines, at):
            _, values = nc.values_load_multi_w_load_instructions(
                base_row[0:1, bass.ds(at, HB)], engines=engines, min_val=0, max_val=N,
                skip_runtime_bounds_check_because="the setup clamps every start to the number of nodes")
            return values

        def one_hot(onehot, h, i, span):
            return nc.vector.tensor_tensor(
                onehot[:, h, :, 0:span], iota[:, 0:span].unsqueeze(1).to_broadcast([P, HB, span]),
                dloc[:, bass.ds(i * BT + h * HB, HB)].unsqueeze(2).to_broadcast([P, HB, span]), ALU.is_equal)

        def gather(pool, i, h, stage, got, staged, gathered, batches):
            pool.wait_ge(staged[h], i + 1)
            pool.sem_inc(batches, 1)
            for g in range(HB):
                pool.indirect_dma_start(out=got[:, h, g, :], out_offset=None, in_=table,
                                        in_offset=bass.IndirectOffsetOnAxis(ap=stage[:, h, g:g + 1].bitcast(U32), axis=0)
                                        ).then_inc(gathered[h], 16)

        def on_engine(eng, engines, fast, slow):
            flag = nc.values_load(regular[0:1, 0:1], engines=engines, min_val=0, max_val=1,
                                  skip_runtime_bounds_check_because="a product of two comparisons")
            with eng.If(flag):
                fast()
            with eng.Else():
                slow()

        def later(i, h):
            return (i, h + AHEAD) if h + AHEAD < NG else (i + 1, h + AHEAD - NG)

        def stage_indices(i, h, stage, rows_free, staged):
            rows_free(i, h)
            nc.scalar.copy(stage[:, h, :], src_cols[:, i * BT + h * HB:i * BT + (h + 1) * HB] if isinstance(i, int)
                           else src_cols[:, bass.ds(i * BT + h * HB, HB)]).then_inc(staged[h], 1)

        def attention_scores():
            with Stage() as s:
                per_group = lambda n: [s.sem(f"{n}_{h}") for h in range(NG)]
                stage, got = s.sb("stage", [P, NG, HB], I32), s.sb("got", [P, NG, HB, TW])
                gotT, dots = s.sb("gotT", [D, NG, HB, P]), s.sb("dots", [P, NG, HB])
                picked, local = s.sb("picked", [P, HB, P]), s.sb("local", [P, NG, HB])
                keys = s.sb("keys", [P, 2, CT, 2])
                hot_key, hot_lo = s.sb("hot_key", [P, 2, CT, KEYS], BF16), s.sb("hot_lo", [P, 2, CT, P], BF16)
                strip = s.sb("strip", [P, 2, WD * NT // 2], F16)
                staged, gathered, turned, saved, dotted, used, kept, stored = (
                    per_group(n) for n in ("staged", "gathered", "turned", "saved", "dotted", "used", "kept", "stored"))
                batches, begun, summed = s.sem("batches"), s.sem("begun"), s.sem("summed")
                keyed, hot, counted, copied, localized = (s.sem(n) for n in ("keyed", "hot", "counted", "copied", "localized"))
                strip_out, strip_free = ([s.sem(f"{n}_{half}") for half in range(2)] for n in ("strip_out", "strip_free"))
                block = s.start()
                PER = CW // 2
                STEPS = 2 * NW
                FIRST = [sum(GROUP_CHUNKS[:q]) for q in range(2 * NG)]

                @block.gpsimd
                def _(pool):
                    with pool.Fori(0, NB) as i:
                        for h in range(NG):
                            gather(pool, i, h, stage, got, staged, gathered, batches)

                @block.sync
                def _(sp):
                    for h in range(NG):
                        sp.sem_inc(kept[h], 1)
                    for half in range(2):
                        sp.sem_inc(strip_free[half], 1)

                    def keep_rows(i):
                        for h in range(NG):
                            sp.wait_ge(gathered[h], i * (16 * HB) + 16 * HB)
                            sp.dma_start(kept_rows[:, bass.ds(i * (BT * TW) + h * (HB * TW), HB * TW)],
                                         got[:, h, :, :].rearrange("p g f -> p (g f)")).then_inc(stored[h], 16)
                            sp.wait_ge(stored[h], i * 16 + 16)
                            sp.sem_inc(kept[h], 1)

                    keep_rows(0)
                    with sp.Fori(0, NW) as w:
                        for half in range(2):
                            sp.wait_ge(copied, w * CW + ((half + 1) * PER + 2))
                            sp.dma_start(counts[bass.ds(w, 1), half, :, :].rearrange("a p f -> p (a f)"),
                                         strip[:, half, :]).then_inc(strip_out[half], 16)
                            keep_rows(w * 2 + (half + 1))
                            sp.wait_ge(strip_out[half], w * 16 + 16)
                            sp.sem_inc(strip_free[half], 1)

                @block.scalar
                def _(act):
                    def rows_free(i, h):
                        act.wait_ge(used[h], i + 1)
                        act.wait_ge(kept[h], i + 1)

                    def save(i, h):
                        act.wait_ge(turned[h], i + 1)
                        nc.scalar.copy(gotT[:, h, :, :], ps[0:D, h % 2, :].rearrange("p (g e) -> p g e", e=P)).then_inc(saved[h], 1)

                    for h in range(AHEAD):
                        stage_indices(0, h, stage, rows_free, staged)
                    act.sem_inc(copied, 2)
                    with act.Fori(0, NW) as w:
                        for half in range(2):
                            i = w * 2 + half
                            for h in range(NG):
                                save(i, h)
                                stage_indices(*later(i, h), stage, rows_free, staged)
                                q = half * NG + h
                                for c in range(FIRST[q], FIRST[q] + GROUP_CHUNKS[q]):
                                    act.wait_ge(counted, w * CW + (c + 3))
                                    if c == half * PER:
                                        act.wait_ge(strip_free[half], w + 1)
                                    nc.scalar.copy(strip[:, half, (c - half * PER) * KEYS:(c - half * PER + 1) * KEYS],
                                                   ps[:, 2 + c % 2, 0:KEYS]).then_inc(copied, 1)
                    with act.Fori(STEPS, NB) as i:
                        for h in range(NG):
                            save(i, h)
                            stage_indices(*later(i, h), stage, rows_free, staged)

                def tensor(pe, span):
                    for h in range(NG):
                        pe.sem_inc(dotted[h], 1)

                    def turn(i, h):
                        pe.wait_ge(gathered[h], i * (16 * HB) + 16 * HB)
                        pe.sem_inc(begun, 1)
                        for g in range(HB):
                            last = nc.tensor.transpose(ps[0:D, h % 2, g * P:(g + 1) * P], got[:, h, g, 0:D], ident[:])
                        last.then_inc(turned[h], 1)

                    def dot(i, h, bases):
                        pe.wait_ge(saved[h], i + 1)
                        pe.wait_ge(used[h], i + 1)
                        for g in range(HB):
                            last = nc.tensor.matmul(ps[:, NG + h, g * span:(g + 1) * span], gotT[:, h, g, :],
                                                    hT[:, bass.ds(bases[g], span)], start=True, stop=True)
                        last.then_inc(dotted[h], 1)

                    with pe.Fori(0, NW) as w:
                        for half in range(2):
                            i = w * 2 + half
                            for h in range(NG):
                                bases = tile_bases(PE_ENGINE, i * BT + (h * HB + HB))
                                turn(i, h)
                                q = half * NG + h
                                for c in range(FIRST[q], FIRST[q] + GROUP_CHUNKS[q]):
                                    pe.wait_ge(hot, w * CW + (c + 1))
                                    pe.wait_ge(copied, w * CW + (c + 1))
                                    for j in range(CT):
                                        last = nc.tensor.matmul(ps[:, 2 + c % 2, 0:KEYS], hot_lo[:, c % 2, j, :], hot_key[:, c % 2, j, :],
                                                                start=(j == 0), stop=(j == CT - 1))
                                    last.then_inc(counted, 1)
                                dot(i, h, bases)
                    with pe.Fori(STEPS, NB) as i:
                        for h in range(NG):
                            bases = tile_bases(PE_ENGINE, i * BT + (h * HB + HB))
                            turn(i, h)
                            dot(i, h, bases)

                def vector(dve, span):
                    for h in range(NG):
                        dve.sem_inc(used[h], 1)
                    dve.sem_inc(counted, 2)

                    def chunk_tiles(first, n):
                        return nc.values_load_multi_w_load_instructions(
                            chunk_tile[0:1, bass.ds(first, n)], engines=DVE_ENGINE, min_val=0, max_val=T - CT,
                            skip_runtime_bounds_check_because="the setup clamps every chunk's first tile")[1]

                    def chunk_keys(chunk, tile, m):
                        dve.wait_ge(counted, chunk + 1)
                        nc.vector.tensor_tensor(keys[:, m, :, :], key_lo[:, bass.ds(tile, CT), :],
                                                key_start[:, bass.ds(chunk, 1), :].to_broadcast([P, CT, 2]), ALU.subtract).then_inc(keyed, 1)

                    def chunk_hot(chunk, m):
                        dve.wait_ge(keyed, chunk + 1)
                        for j in range(CT):
                            nc.vector.tensor_scalar(hot_key[:, m, j, :], iota_key[:], keys[:, m, j, 0:1], None, ALU.is_equal)
                            last = nc.vector.tensor_scalar(hot_lo[:, m, j, :], iota_lo[:], keys[:, m, j, 1:2], None, ALU.is_equal)
                        last.then_inc(hot, 1)

                    def take_local(i, h):
                        nc.vector.tensor_copy(local[:, h, :], dloc[:, bass.ds(i * BT + h * HB, HB)]).then_inc(localized, 1)

                    def score_group(i, h):
                        dve.wait_ge(localized, i * NG + (h + 1))
                        dve.wait_ge(dotted[h], i + 2)
                        for g in range(HB):
                            last = nc.vector.scalar_tensor_tensor(picked[:, g, 0:span], iota[:, 0:span], local[:, h, g:g + 1],
                                                                  ps[:, NG + h, g * span:(g + 1) * span],
                                                                  ALU.is_equal, ALU.mult, accum_out=dots[:, h, g:g + 1])
                        last.then_inc(summed, 1)
                        dve.wait_ge(summed, i * NG + (h + 1))
                        nc.vector.tensor_tensor(score[:, bass.ds(i * BT + h * HB, HB)], dots[:, h, :], got[:, h, :, D + 1], ALU.mult).then_inc(used[h], 1)

                    first_tiles = chunk_tiles(0, 2)
                    for m in range(2):
                        chunk_keys(m, first_tiles[m], m)
                    for m in range(2):
                        chunk_hot(m, m)
                    with dve.Fori(0, NW) as w:
                        for half in range(2):
                            i = w * 2 + half
                            tiles = chunk_tiles(w * CW + (half * PER + 2), PER)
                            for h in range(NG):
                                q = half * NG + h
                                begin = FIRST[q] + GROUP_CHUNKS[q]
                                ahead = range(begin, begin + GROUP_CHUNKS[(q + 1) % (2 * NG)])
                                for c in ahead:
                                    chunk_keys(w * CW + c, tiles[c - half * PER - 2], c % 2)
                                take_local(i, h)
                                for c in ahead:
                                    chunk_hot(w * CW + c, c % 2)
                                score_group(i, h)
                    with dve.Fori(STEPS, NB) as i:
                        for h in range(NG):
                            take_local(i, h)
                            score_group(i, h)

                @block.tensor
                def _(pe):
                    on_engine(pe, PE_ENGINE, lambda: tensor(pe, SPAN), lambda: tensor(pe, P))

                @block.vector
                def _(dve):
                    on_engine(dve, DVE_ENGINE, lambda: vector(dve, SPAN), lambda: vector(dve, P))

        def attention_weights():
            with ExitStack() as tmp_ctx, Stage() as s:
                def tb(name, shape, dt=F32):
                    return tmp_ctx.enter_context(nc.sbuf_tensor(name, shape, dt))
                lines = tb("lines", [P, TBS, P])
                value = tb("value", [P, T])[:]
                dst_i = tb("dst_i", [P, T], I32)
                dst_l = tb("dst_l", [P, T])
                cut = tb("cut", [P, T + 1])
                run = tb("run", [P, T])
                best = tmp[:].rearrange("p k d -> p (k d)")[:, 0:T]
                ends = tb("ends", [P, 4])
                line = tb("line", [4, P])
                flat = tb("flat", [1, 12, P + 2])
                carry = tb("carry", [P, 2])
                dst_in, turned, copied, sent, back, dve_link, pe_go, pe_done, shifted, wexp, out_sent, back2, turned2 = (
                    s.sem(n) for n in ("dst_in", "turned", "copied", "sent", "back", "dve_link", "pe_go", "pe_done", "shifted",
                                       "wexp", "out_sent", "back2", "turned2"))
                row_moved = s.sem("row_moved")
                scaled = s.sem("scaled")
                whole = TB * P * P
                block = s.start()

                @block.tensor
                def _(pe):
                    pe.wait_ge(scaled, 1)
                    for k in range(TBS):
                        n_in = P if k < TB else TR
                        if k >= 8:
                            pe.wait_ge(copied, k - 7)
                        nc.tensor.transpose(ps[0:n_in, k % 8, 0:P], score[:, k * P:k * P + n_in], ident[:]).then_inc(turned, 1)
                    pe.wait_ge(pe_go, 1)
                    nc.tensor.transpose(ps[0:4, 0, 0:P], ends[:], ident[:]).then_inc(pe_done, 1)
                    pe.wait_ge(pe_go, 2)
                    for n in range(2):
                        last = nc.tensor.matmul(ps[:, 1, n:n + 1], flat[0:1, 10 + n, 0:P], ident[0:1, 0:1], start=True, stop=True)
                    last.then_inc(pe_done, 1)
                    pe.wait_ge(back2, 32)
                    pe.wait_ge(copied, TBS + 2)
                    for k in range(TBS):
                        n_in = P if k < TB else TR
                        if k >= 8:
                            pe.wait_ge(copied, TBS + 2 + k - 7)
                        nc.tensor.transpose(ps[:, k % 8, 0:n_in], lines[0:n_in, k, :], ident[0:n_in, 0:n_in]).then_inc(turned2, 1)

                @block.sync
                def _(sp):
                    sp.dma_start(dst_i[:], dst.rearrange("(p j) -> p j", p=P)).then_inc(dst_in, 16)
                    sp.wait_ge(copied, TBS)
                    sp.dma_start(edge_line[0:whole].rearrange("(k p e) -> p k e", p=P, e=P), lines[:, 0:TB, :]).then_inc(sent, 16)
                    sp.dma_start(edge_line[whole:EP].rearrange("(p e) -> p e", e=P), lines[0:TR, TB, :]).then_inc(sent, 16)
                    sp.wait_ge(sent, 32)
                    sp.dma_start(value, edge_line.rearrange("(p j) -> p j", p=P)).then_inc(back, 16)
                    sp.wait_ge(copied, TBS + 1)
                    for n in range(4):
                        sp.dma_start(flat[0:1, n, 1:P + 1], line[n:n + 1, :]).then_inc(row_moved, 16)
                    sp.wait_ge(wexp, 1)
                    sp.dma_start(weight_line.rearrange("(p j) -> p j", p=P), run[:]).then_inc(out_sent, 16)
                    sp.wait_ge(out_sent, 16)
                    sp.dma_start(lines[:, 0:TB, :], weight_line[0:whole].rearrange("(k p e) -> p k e", p=P, e=P)).then_inc(back2, 16)
                    sp.dma_start(lines[0:TR, TB, :], weight_line[whole:EP].rearrange("(p e) -> p e", e=P)).then_inc(back2, 16)
                    sp.wait_ge(back2, 32)

                @block.scalar
                def _(act):
                    act.wait_ge(shifted, 1)
                    nc.scalar.activation(run[:], run[:], ACT.Exp).then_inc(wexp, 1)

                @block.vector
                def _(dve):
                    link = linker(dve, dve_link)
                    nc.vector.tensor_scalar(score[:], score[:], beta_sb[:, 0:1], None, ALU.mult).then_inc(scaled, 1)
                    for k in range(TBS):
                        n_in = P if k < TB else TR
                        dve.wait_ge(turned, k + 1)
                        nc.vector.tensor_copy(lines[0:n_in, k, :], ps[0:n_in, k % 8, 0:P]).then_inc(copied, 1)
                    dve.wait_ge(dst_in, 16)
                    link(nc.vector.tensor_copy(dst_l[:], dst_i[:]))
                    nc.vector.memset(cut[:, 0:1], FAR)
                    nc.vector.memset(cut[:, T:T + 1], FAR)
                    link(nc.vector.tensor_tensor(cut[:, 1:T], dst_l[:, 1:T], dst_l[:, 0:T - 1], ALU.not_equal))
                    link(nc.vector.tensor_scalar(cut[:, 1:T], cut[:, 1:T], FAR, None, ALU.mult))
                    dve.wait_ge(back, 16)
                    link(nc.vector.tensor_tensor_scan(run[:], cut[:, 0:T], value, FAR, ALU.add, ALU.max))
                    link(nc.vector.tensor_tensor_scan(best[:, ::-1], cut[:, 1:T + 1][:, ::-1], value[:, ::-1], FAR, ALU.add, ALU.max))
                    nc.vector.tensor_copy(ends[:, 0:1], dst_l[:, 0:1])
                    nc.vector.tensor_copy(ends[:, 1:2], dst_l[:, T - 1:T])
                    nc.vector.tensor_copy(ends[:, 2:3], run[:, T - 1:T])
                    nc.vector.tensor_copy(ends[:, 3:4], best[:, 0:1]).then_inc(pe_go, 1)
                    dve.wait_ge(pe_done, 1)
                    link(nc.vector.memset(flat[:], -1.0))
                    nc.vector.tensor_copy(line[:], ps[0:4, 0, 0:P]).then_inc(copied, 1)
                    dve.wait_ge(row_moved, 64)
                    row = lambda n, a, b: flat[0:1, n, a:b]
                    link(nc.vector.tensor_tensor(row(4, 1, P + 2), row(0, 1, P + 2), row(1, 0, P + 1), ALU.not_equal))
                    link(nc.vector.tensor_scalar(row(4, 1, P + 2), row(4, 1, P + 2), FAR, None, ALU.mult))
                    link(nc.vector.tensor_tensor(row(5, 1, P + 1), row(0, 1, P + 1), row(1, 1, P + 1), ALU.not_equal))
                    link(nc.vector.tensor_scalar(row(5, 1, P + 1), row(5, 1, P + 1), FAR, None, ALU.mult))
                    link(nc.vector.tensor_tensor(row(6, 1, P + 1), row(4, 1, P + 1), row(5, 1, P + 1), ALU.min))
                    link(nc.vector.tensor_tensor(row(7, 1, P + 1), row(4, 2, P + 2), row(5, 1, P + 1), ALU.min))
                    link(nc.vector.memset(row(8, 0, P + 2), FAR))
                    link(nc.vector.memset(row(9, 0, P + 2), FAR))
                    link(nc.vector.tensor_tensor_scan(row(8, 1, P + 1), row(6, 1, P + 1), row(2, 1, P + 1), FAR, ALU.add, ALU.max))
                    link(nc.vector.tensor_tensor_scan(row(9, 1, P + 1)[:, ::-1], row(7, 1, P + 1)[:, ::-1], row(3, 1, P + 1)[:, ::-1], FAR, ALU.add, ALU.max))
                    link(nc.vector.tensor_tensor(row(10, 0, P), row(8, 0, P), row(4, 1, P + 1), ALU.add))
                    link(nc.vector.tensor_tensor(row(11, 0, P), row(9, 2, P + 2), row(4, 2, P + 2), ALU.add))
                    nc.vector.tensor_scalar(flat[0:1, 10:12, 0:P], flat[0:1, 10:12, 0:P], FAR, None, ALU.max).then_inc(pe_go, 1)
                    dve.wait_ge(pe_done, 2)
                    nc.vector.tensor_copy(carry[:], ps[:, 1, 0:2]).then_inc(copied, 1)
                    dve.wait_ge(copied, TBS + 2)
                    nc.vector.memset(cut[:, 0:1], 0.0)
                    link(nc.vector.memset(cut[:, T:T + 1], 0.0))
                    link(nc.vector.tensor_tensor_scan(run[:], cut[:, 0:T], value, carry[:, 0:1], ALU.add, ALU.max))
                    link(nc.vector.tensor_tensor_scan(best[:, ::-1], cut[:, 1:T + 1][:, ::-1], value[:, ::-1], carry[:, 1:2], ALU.add, ALU.max))
                    link(nc.vector.tensor_tensor(best, best, run[:], ALU.max))
                    nc.vector.tensor_tensor(run[:], value, best, ALU.subtract).then_inc(shifted, 1)
                    for k in range(TBS):
                        n_in = P if k < TB else TR
                        dve.wait_ge(turned2, k + 1)
                        nc.vector.tensor_copy(score[:, k * P:k * P + n_in], ps[:, k % 8, 0:n_in]).then_inc(copied, 1)

        def general_sums(s, kind, width):
            per_group = lambda n: [s.sem(f"{n}_{h}") for h in range(NG)]
            got, onehot = s.sb("got", [P, NG, HB, TW]), s.sb("onehot", [P, NG, HB, P])
            if kind != "kept":
                stage = s.sb("stage", [P, NG, HB], I32)
            if kind == "edge":
                msg, edge_sb = s.sb("msg", [P, NG, HB, D]), s.sb("edge_sb", [EF, NG, HB * P])
            rows_in, ready, summed = (per_group(n) for n in ("rows_in", "ready", "summed"))
            if kind != "kept":
                staged, batches = per_group("staged"), s.sem("batches")
            if kind == "edge":
                joined, relued, edges_in, mapped = (per_group(n) for n in ("joined", "relued", "edges_in", "mapped"))
            added = s.sem("added")
            per_load = 16 if kind == "kept" else 16 * HB
            rows_used = joined if kind == "edge" else summed

            def gpsimd(pool):
                if kind != "kept":
                    with pool.Fori(0, NB) as i:
                        for h in range(NG):
                            gather(pool, i, h, stage, got, staged, rows_in, batches)

            def scalar(act):
                def rows_free(i, h):
                    act.wait_ge(rows_used[h], i + 1)

                if kind != "kept":
                    for h in range(AHEAD):
                        stage_indices(0, h, stage, rows_free, staged)
                    with act.Fori(0, NB) as i:
                        for h in range(NG):
                            if kind == "edge":
                                act.wait_ge(joined[h], i + 2)
                                nc.scalar.activation(msg[:, h, :, :], msg[:, h, :, :], ACT.Relu).then_inc(relued[h], 1)
                            stage_indices(*later(i, h), stage, rows_free, staged)

            def sync(sp):
                if kind == "kept":
                    with sp.Fori(0, NB) as i:
                        for h in range(NG):
                            sp.wait_ge(summed[h], i + 1)
                            sp.dma_start(got[:, h, :, :].rearrange("p g f -> p (g f)"),
                                         kept_rows[:, bass.ds(i * (BT * TW) + h * (HB * TW), HB * TW)]).then_inc(rows_in[h], 16)
                if kind == "edge":
                    with sp.Fori(0, NB) as i:
                        for h in range(NG):
                            sp.wait_ge(mapped[h], i + 1)
                            sp.dma_start(edge_sb[:, h, :], edge_t[:, bass.ds(i * (BT * P) + h * (HB * P), HB * P)]).then_inc(edges_in[h], 16)

            def tensor(pe, span):
                if kind == "edge":
                    for h in range(NG):
                        pe.sem_inc(mapped[h], 1)
                with pe.Fori(0, NB) as i:
                    for h in range(NG):
                        if kind == "edge":
                            pe.wait_ge(edges_in[h], i * 16 + 16)
                            pe.wait_ge(joined[h], i + 1)
                            for g in range(HB):
                                last = nc.tensor.matmul(ps[:, h // 2, (h % 2 * HB + g) * D:(h % 2 * HB + g + 1) * D],
                                                        edge_sb[:, h, g * P:(g + 1) * P], w1b_sb[:], start=True, stop=True)
                            last.then_inc(mapped[h], 1)
                        pe.wait_ge(rows_in[h], i * per_load + per_load)
                        pe.wait_ge(ready[h], i + 1)
                        pe.wait_ge(added, i * BT + (ZERO + (h - 2) * HB))
                        if kind == "edge":
                            pe.wait_ge(relued[h], i + 1)
                        for g in range(HB):
                            rows_g = msg[:, h, g, 0:width] if kind == "edge" else got[:, h, g, 0:width]
                            last = nc.tensor.matmul(ps[0:width, NG + h, g * span:(g + 1) * span], rows_g,
                                                    onehot[:, h, g, 0:span], start=True, stop=True)
                        last.then_inc(summed[h], 1)

            def vector(dve, span):
                nc.vector.memset(ps[0:width, 2 * NG - 1, :], 0.0).then_inc(summed[NG - 1], 1)
                for h in range(NG - 1):
                    dve.sem_inc(summed[h], 1)
                if kind == "edge":
                    for h in range(NG):
                        dve.sem_inc(joined[h], 1)
                nc.vector.memset(acc[0:width, :], 0.0).then_inc(added, ZERO)

                def add_sums(bases, count, h):
                    for g in range(HB):
                        window = acc[0:width, bass.ds(bases[g], span)]
                        dve.wait_ge(added, count + (g + ZERO))
                        nc.vector.tensor_tensor(window, window, ps[0:width, NG + h, g * span:(g + 1) * span],
                                                ALU.add).then_inc(added, 1)

                with dve.Fori(0, NB) as i:
                    for h in range(NG):
                        dve.wait_ge(summed[h], i + 1)
                        if kind == "kept":
                            for g in range(HB):
                                at = i * BT + (h * HB + g)
                                last = nc.vector.tensor_scalar(onehot[:, h, g, :], iota[:], dloc[:, bass.ds(at, 1)], score[:, bass.ds(at, 1)],
                                                               ALU.is_equal, ALU.mult)
                            last.then_inc(ready[h], 1)
                        else:
                            one_hot(onehot, h, i, span).then_inc(ready[h], 1)
                        bases = tile_bases(DVE_ENGINE, i * BT + h * HB)
                        if kind == "edge":
                            dve.wait_ge(mapped[h], i + 2)
                            dve.wait_ge(rows_in[h], i * per_load + per_load)
                            nc.vector.tensor_tensor(msg[:, h, :, :], got[:, h, :, 0:D],
                                                    ps[:, h // 2, h % 2 * HB * D:(h % 2 + 1) * HB * D].rearrange("p (g d) -> p g d", d=D),
                                                    ALU.add).then_inc(joined[h], 1)
                        dve.wait_ge(summed[h - 1], i + (1 + (h > 0)))
                        add_sums(bases, i * BT + h * HB, (h - 1) % NG)
                dve.wait_ge(summed[NG - 1], NB + 1)
                add_sums(tile_bases(DVE_ENGINE, T), T, NG - 1)

            return gpsimd, scalar, sync, tensor, vector

        def each_window(eng, body):
            with eng.Fori(0, NW // 2) as i:
                for m in range(2):
                    body(i * 2 + m, m, i)

        def each_window_late(eng, body, late):
            body(0, 0, 0)
            with eng.Fori(0, NW // 2 - 1) as i:
                for m in (1, 0):
                    body(i * 2 + (2 - m), m, i + (1 - m))
                    late(i * 2 + (1 - m), 1 - m)
            body(NW - 1, 1, NW // 2 - 1)
            late(NW - 2, 0)
            late(NW - 1, 1)

        def window_tail(s):
            sums = s.sb("sums", [P, 2, D + 1])
            product, held, turned, put = s.sem("product"), s.sem("held"), s.sem("turned"), s.sem("put")

            def turn(w, m):
                nc.tensor.wait_ge(held, w + 3)
                nc.tensor.wait_ge(put, w + 1)
                nc.tensor.transpose(ps[0:D + 1, 2 + m, 0:WD], sums[0:WD, m, :], ident[0:WD, 0:WD]).then_inc(turned, 1)

            def put_sums(act, w, m):
                act.wait_ge(turned, w + 3)
                nc.scalar.copy(acc[:, bass.ds(w * WD, WD)], ps[0:D + 1, 2 + m, 0:WD]).then_inc(put, 1)

            return sums, product, held, turned, put, turn, put_sums

        def attention_windows(s):
            rows_w = s.sb("rows_w", [P, 2, WT, TW])
            pieces = [(r * WT // 3, (r + 1) * WT // 3) for r in range(3)]
            hot_w = s.sb("hot_w", [P, 2, WT // 3, WD])
            place = s.sb("place", [P, 2, 2, WT])
            sums, product, held, turned, put, turn, put_sums = window_tail(s)
            rows_in, placed, hot, weighted, multiplied = [s.sem("wrows_in_0"), s.sem("wrows_in_1")], s.sem("placed"), s.sem("whot"), s.sem("weighted"), s.sem("multiplied")
            DONE = 4

            def first_tile(engines, w):
                return nc.values_load(window_tile[0:1, bass.ds(w, 1)], engines=engines, min_val=0, max_val=T - WT,
                                      skip_runtime_bounds_check_because="the setup clamps every window's first tile")

            def sync(sp):
                def load(w, m, n):
                    tile = first_tile([mybir.EngineType.SP], w)
                    sp.wait_ge(multiplied, w * 3 + (DONE - 3))
                    sp.dma_start(rows_w[:, m, :, :].rearrange("p j f -> p (j f)"), kept_rows[:, bass.ds(tile * TW, WT * TW)]).then_inc(rows_in[m], 16)
                each_window(sp, load)

            def vector(dve):
                dve.sem_inc(multiplied, DONE)

                def window(w, m, n):
                    tile = first_tile(DVE_ENGINE, w)
                    dve.wait_ge(multiplied, w * 3 + (DONE - 3))
                    nc.vector.tensor_scalar(place[:, m, 0, :], dst_cols[:, bass.ds(tile, WT)], window_start[:, bass.ds(w, 1)], None, ALU.subtract)
                    nc.vector.tensor_copy(place[:, m, 1, :], score[:, bass.ds(tile, WT)]).then_inc(placed, 1)
                    dve.wait_ge(placed, w + 1)
                    for r, (a, b) in enumerate(pieces):
                        dve.wait_ge(multiplied, w * 3 + (r + DONE - 1))
                        nc.vector.tensor_tensor(hot_w[:, (m + r) % 2, :, :], iota[:, 0:WD].unsqueeze(1).to_broadcast([P, b - a, WD]),
                                                place[:, m, 0, a:b].unsqueeze(2).to_broadcast([P, b - a, WD]), ALU.is_equal).then_inc(hot, 1)
                each_window(dve, window)

            def gpsimd(pool):
                def window(w, m, n):
                    pool.wait_ge(rows_in[m], n * 16 + 16)
                    pool.wait_ge(placed, w + 1)
                    for a, b in pieces:
                        pool.sem_inc(s.idle, 1)
                        nc.gpsimd.tensor_tensor(rows_w[:, m, a:b, 0:D + 1], rows_w[:, m, a:b, 0:D + 1],
                                                place[:, m, 1, a:b].unsqueeze(2).to_broadcast([P, b - a, D + 1]), ALU.mult).then_inc(weighted, 1)
                each_window(pool, window)

            def tensor(pe):
                def window(w, m, n):
                    pe.wait_ge(held, w + 1)
                    for r, (a, b) in enumerate(pieces):
                        pe.wait_ge(hot, w * 3 + (r + 1))
                        pe.wait_ge(weighted, w * 3 + (r + 1))
                        for j in range(a, b):
                            last = nc.tensor.matmul(ps[0:WD, m, 0:D + 1], hot_w[:, (m + r) % 2, j - a, :], rows_w[:, m, j, 0:D + 1],
                                                    start=(j == 0), stop=(j == WT - 1))
                        last.then_inc(multiplied, 1)
                each_window_late(pe, window, turn)

            def scalar(act):
                for counted in (put, held, turned):
                    act.sem_inc(counted, 2)

                def window(w, m, n):
                    act.wait_ge(multiplied, w * 3 + (DONE + 3))
                    act.wait_ge(turned, w + 1)
                    nc.scalar.copy(sums[0:WD, m, :], ps[0:WD, m, 0:D + 1]).then_inc(held, 1)
                    put_sums(act, w, m)
                each_window(act, window)

            return gpsimd, sync, vector, tensor, scalar

        def count_windows(s, source, rest):
            WIDE = SPLIT * D + 2
            strips = s.sb("strips", [P, 2, WD * NT], F16)
            parts = s.sb("parts", [P, NT, WIDE], BF16)
            sums, product, held, turned, put, turn, put_sums = window_tail(s)
            strip_in, split, added_up = [s.sem("strip_in_0"), s.sem("strip_in_1")], s.sem("split"), s.sem("added_up")

            def sync(sp):
                def load(w, m, n):
                    sp.wait_ge(product, w + 1)
                    sp.dma_start(strips[:, m, :].rearrange("p (h f) -> p h f", h=2),
                                 counts[bass.ds(w, 1), :, :, :].rearrange("a h p f -> p (a h) f")).then_inc(strip_in[m], 16)
                each_window(sp, load)

            def tensor(pe):
                pe.wait_ge(split, 2 * SPLIT)

                def window(w, m, n):
                    pe.wait_ge(strip_in[m], n * 16 + 16)
                    pe.wait_ge(held, w + 1)
                    for k in range(NT):
                        last = nc.tensor.matmul(ps[0:WD, m, 0:WIDE], strips[:, m, k::NT], parts[:, k, :], start=(k == 0), stop=(k == NT - 1))
                    last.then_inc(product, 1)
                each_window_late(pe, window, turn)

            def scalar(act):
                for counted in (product, put, held, turned):
                    act.sem_inc(counted, 2)
                each_window(act, lambda w, m, n: put_sums(act, w, m))

            def vector(dve):
                link = linker(dve, split)
                part = lambda c: parts[:, :, c * D:(c + 1) * D]
                nc.vector.memset(parts[:, :, SPLIT * D:WIDE], 1.0)
                link(nc.vector.tensor_copy(part(0), source))
                link(nc.vector.tensor_tensor(rest, source, part(0), ALU.subtract))
                link(nc.vector.tensor_copy(part(1), rest))
                link(nc.vector.tensor_tensor(rest, rest, part(1), ALU.subtract))
                link(nc.vector.tensor_copy(part(2), rest), 2)

                def window(w, m, n):
                    dve.wait_ge(product, w + 3)
                    dve.wait_ge(turned, w + 1)
                    nc.vector.tensor_copy(sums[0:WD, m, :], ps[0:WD, m, 2 * D:3 * D + 1]).then_inc(added_up, 1)
                    for c in (1, 0):
                        dve.wait_ge(added_up, w * 2 + (2 - c))
                        nc.vector.tensor_tensor(sums[0:WD, m, 0:D], sums[0:WD, m, 0:D], ps[0:WD, m, c * D:(c + 1) * D], ALU.add).then_inc(held if c == 0 else added_up, 1)
                each_window(dve, window)

            return sync, tensor, scalar, vector

        def sum_edges(kind, width=D, source=None, rest=None):
            with Stage() as s:
                gpsimd, scalar, sync, tensor, vector = general_sums(s, kind, width)
                fast_gpsimd = lambda pool: pool.sem_inc(s.idle, 1)
                if kind == "kept":
                    fast_gpsimd, fast_sync, fast_vector, fast_tensor, fast_scalar = attention_windows(s)
                if kind == "table":
                    fast_sync, fast_tensor, fast_scalar, fast_vector = count_windows(s, source, rest)
                both = kind != "edge"
                block = s.start()

                @block.gpsimd
                def _(pool):
                    if both:
                        on_engine(pool, [mybir.EngineType.Pool], lambda: fast_gpsimd(pool), lambda: gpsimd(pool) or pool.sem_inc(s.idle, 1))
                    else:
                        gpsimd(pool)

                @block.scalar
                def _(act):
                    if both:
                        on_engine(act, [mybir.EngineType.Activation], lambda: fast_scalar(act), lambda: scalar(act) or act.sem_inc(s.idle, 1))
                    else:
                        scalar(act)

                @block.sync
                def _(sp):
                    if both:
                        on_engine(sp, [mybir.EngineType.SP], lambda: fast_sync(sp), lambda: sync(sp) or sp.sem_inc(s.idle, 1))
                    else:
                        sync(sp)

                @block.tensor
                def _(pe):
                    if both:
                        on_engine(pe, PE_ENGINE, lambda: fast_tensor(pe), lambda: tensor(pe, P))
                    else:
                        on_engine(pe, PE_ENGINE, lambda: tensor(pe, SPAN), lambda: tensor(pe, P))

                @block.vector
                def _(dve):
                    if both:
                        on_engine(dve, DVE_ENGINE, lambda: fast_vector(dve), lambda: vector(dve, P))
                    else:
                        on_engine(dve, DVE_ENGINE, lambda: vector(dve, SPAN), lambda: vector(dve, P))

        def add_attention():
            with Stage() as s:
                dve_link, var_ready, root, out_ready, taken, stored = (
                    s.sem(n) for n in ("dve_link", "var_ready", "root", "out_ready", "taken", "stored"))
                table_ready = s.sem("table_ready")
                block = s.start()

                @block.tensor
                def _(pe):
                    for k in range(NT):
                        if k >= 8:
                            pe.wait_ge(taken, k - 7)
                        nc.tensor.matmul(ps[:, k % 8, 0:D + 1], acc[:, k * P:(k + 1) * P], w0_sb[:], start=True, stop=True).then_inc(out_ready, 1)

                @block.vector
                def _(dve):
                    link = linker(dve, dve_link)
                    for k in range(NT):
                        dve.wait_ge(out_ready, k + 1)
                        link(nc.vector.tensor_scalar(stat[:, 0, k:k + 1], ps[:, k % 8, D:D + 1], 1e-30, None, ALU.max))
                        link(nc.vector.reciprocal(stat[:, 1, k:k + 1], stat[:, 0, k:k + 1]))
                        nc.vector.scalar_tensor_tensor(x_sb[:, k, :], ps[:, k % 8, 0:D], stat[:, 1, k:k + 1], x_sb[:, k, :],
                                                       ALU.mult, ALU.add).then_inc(taken, 1)
                    dve.wait_ge(taken, NT)
                    norm_relu(dve, link, var_ready, root, 1)
                    dve.sem_inc(table_ready, 1)

                @block.scalar
                def _(act):
                    act.wait_ge(var_ready, 1)
                    nc.scalar.activation(stat[:, 1, :], stat[:, 1, :], ACT.Sqrt).then_inc(root, 1)

                @block.sync
                def _(sp):
                    sp.wait_ge(table_ready, 1)
                    sp.dma_start(table.rearrange("(k p) d -> p k d", p=P), h_sb[:]).then_inc(stored, 16)
                    sp.wait_ge(stored, 16)

        CH = [(c, min(512, NP - c)) for c in range(0, NP, 512)]

        def mlp(s, first, last_w, last_rows, take, bias, sems, second):
            m1, a1, m2, a2, m3, t3 = sems
            hid = s.sb("hid", [P, 2, 2, 512])

            def tensor(pe, start_waits):
                start_waits(pe)
                for n, (c, wide) in enumerate(CH):
                    if n >= 2:
                        pe.wait_ge(a1, n - 1)
                    for j, (w, rows_of) in enumerate(first):
                        last = nc.tensor.matmul(ps[:, n % 2, 0:wide], w, rows_of[0:D, c:c + wide], start=(j == 0), stop=(j == len(first) - 1))
                    last.then_inc(m1, 1)
                    pe.wait_ge(a1, n + 1)
                    nc.tensor.matmul(ps[:, 2 + n % 2, 0:wide], second, hid[:, 0, n % 2, 0:wide], start=True, stop=True).then_inc(m2, 1)
                    pe.wait_ge(a2, n + 1)
                    if n >= 2:
                        pe.wait_ge(t3, n - 1)
                    for q in range(wide // P):
                        last = nc.tensor.matmul(ps[:, 4 + n % 2, q * D:(q + 1) * D], hid[:, 1, n % 2, q * P:(q + 1) * P], last_w, start=True, stop=True)
                    last.then_inc(m3, 1)

            def scalar(act):
                for n, (c, wide) in enumerate(CH):
                    act.wait_ge(m1, n + 1)
                    if n >= 2:
                        act.wait_ge(m2, n - 1)
                    nc.scalar.activation(hid[:, 0, n % 2, 0:wide], ps[:, n % 2, 0:wide], ACT.Relu, bias=cols_sb[:, bias:bias + 1]).then_inc(a1, 1)
                    act.wait_ge(m2, n + 1)
                    if n >= 2:
                        act.wait_ge(m3, n - 1)
                    nc.scalar.activation(hid[:, 1, n % 2, 0:wide], ps[:, 2 + n % 2, 0:wide], ACT.Relu, bias=cols_sb[:, bias + 1:bias + 2]).then_inc(a2, 1)

            def vector(dve):
                for n, (c, wide) in enumerate(CH):
                    dve.wait_ge(m3, n + 1)
                    q = wide // P
                    take(c // P, q, ps[:, 4 + n % 2, 0:q * D].rearrange("p (k d) -> p k d", d=D)).then_inc(t3, 1)

            return tensor, scalar, vector

        def row_of(name, q):
            return rows_sb[:, ROWS.index(name), :].unsqueeze(1).to_broadcast([P, q, D])

        def message_nodes():
            with Stage() as s:
                dve_link, var_ready, root, out_ready, taken, stored, h_ready, turned, freed, table_ready = (
                    s.sem(n) for n in ("dve_link", "var_ready", "root", "out_ready", "taken", "stored", "h_ready", "turned", "freed", "table_ready"))
                sems = [s.sem(n) for n in ("m1", "a1", "m2", "a2", "m3", "t3")]
                take = lambda k, q, got_ps: nc.vector.tensor_tensor(tmp[:, k:k + q, :], got_ps, row_of("bM3", q), ALU.add)
                tensor, scalar, vector = mlp(s, [(wm1_sb[:], hT)], wm3_sb[:], None, take, 0, sems, wm2_sb[:])
                block = s.start()

                @block.tensor
                def _(pe):
                    for k in range(NT):
                        if k >= 8:
                            pe.wait_ge(taken, k - 7)
                        nc.tensor.matmul(ps[:, k % 8, 0:D + 1], acc[:, k * P:(k + 1) * P], ident[0:D + 1, 0:D + 1], start=True, stop=True).then_inc(out_ready, 1)
                    pe.wait_ge(h_ready, 1)
                    turn_nodes(pe, h_sb, h_ready, turned, freed)
                    tensor(pe, lambda pe: pe.wait_ge(freed, -(-NT // 4)))

                @block.vector
                def _(dve):
                    link = linker(dve, dve_link)
                    for k in range(NT):
                        dve.wait_ge(out_ready, k + 1)
                        nc.vector.tensor_copy(count[:, k:k + 1], ps[:, k % 8, D:D + 1])
                        nc.vector.tensor_tensor(x_sb[:, k, :], ps[:, k % 8, 0:D], x_sb[:, k, :], ALU.add).then_inc(taken, 1)
                    dve.wait_ge(taken, NT)
                    norm_relu(dve, link, var_ready, root, 1)
                    dve.sem_inc(h_ready, 1)
                    vector(dve)
                    dve.wait_ge(sems[5], len(CH))
                    dve.sem_inc(table_ready, 1)

                @block.scalar
                def _(act):
                    act.wait_ge(var_ready, 1)
                    nc.scalar.activation(stat[:, 1, :], stat[:, 1, :], ACT.Sqrt).then_inc(root, 1)
                    save_turned(act, turned, freed)
                    scalar(act)

                @block.sync
                def _(sp):
                    sp.wait_ge(table_ready, 1)
                    sp.dma_start(table.rearrange("(k p) d -> p k d", p=P)[:, :, 0:D], tmp[:]).then_inc(stored, 16)
                    sp.wait_ge(stored, 16)

        def update_nodes():
            with Stage() as s:
                dve_link, var_ready, root, stored, h_ready, turned, freed, table_ready = (
                    s.sem(n) for n in ("dve_link", "var_ready", "root", "stored", "h_ready", "turned", "freed", "table_ready"))
                mapped, taken = s.sem("mapped"), s.sem("taken")
                biased = s.sem("biased")
                sems = [s.sem(n) for n in ("m1", "a1", "m2", "a2", "m3", "t3")]
                take = lambda k, q, got_ps: nc.vector.tensor_tensor(x_sb[:, k:k + q, :], got_ps, x_sb[:, k:k + q, :], ALU.add)
                tensor, scalar, vector = mlp(s, [(wu1_sb[:, 0, :], hT), (wu1_sb[:, 1, :], acc)], wu3_sb[:], None, take, 2, sems, wu2_sb[:])
                block = s.start()

                @block.tensor
                def _(pe):
                    pe.wait_ge(biased, 1)
                    tensor(pe, lambda pe: None)
                    pe.wait_ge(h_ready, 1)
                    turn_nodes(pe, h_sb, h_ready, turned, freed)
                    pe.wait_ge(freed, -(-NT // 4))
                    for k in range(NT):
                        if k % 8 == 0 and k >= 64:
                            pe.wait_ge(taken, k // 8 - 7)
                        last = nc.tensor.matmul(ps[:, (k // 8) % 8, (k % 8) * D:(k % 8 + 1) * D], hT[:, k * P:(k + 1) * P], w1a_sb[:], start=True, stop=True)
                        if k % 8 == 7 or k == NT - 1:
                            last.then_inc(mapped, 1)

                @block.vector
                def _(dve):
                    link = linker(dve, dve_link)
                    nc.vector.tensor_tensor(x_sb[:], x_sb[:], row_of("bU3", NT), ALU.add).then_inc(biased, 1)
                    vector(dve)
                    dve.wait_ge(sems[5], len(CH))
                    norm_relu(dve, link, var_ready, root, 1)
                    dve.sem_inc(h_ready, 1)
                    for b in range(-(-NT // 8)):
                        q = min(8, NT - 8 * b)
                        dve.wait_ge(mapped, b + 1)
                        last = nc.vector.tensor_tensor(tmp[:, 8 * b:8 * b + q, :], ps[:, b % 8, 0:q * D].rearrange("p (k d) -> p k d", d=D),
                                                       row_of("b1", q), ALU.add)
                        last.then_inc(taken, 1)
                    dve.wait_ge(taken, -(-NT // 8))
                    dve.sem_inc(table_ready, 1)

                @block.scalar
                def _(act):
                    scalar(act)
                    act.wait_ge(var_ready, 1)
                    nc.scalar.activation(stat[:, 1, :], stat[:, 1, :], ACT.Sqrt).then_inc(root, 1)
                    save_turned(act, turned, freed)

                @block.sync
                def _(sp):
                    sp.wait_ge(table_ready, 1)
                    sp.dma_start(table.rearrange("(k p) d -> p k d", p=P)[:, :, 0:D], tmp[:]).then_inc(stored, 16)
                    sp.wait_ge(stored, 16)

        def finish_nodes():
            with Stage() as s:
                dve_link, out_ready, taken, var_ready, root, stored, done, count_turned, count_row = (
                    s.sem(n) for n in ("dve_link", "out_ready", "taken", "var_ready", "root", "stored", "done", "count_turned", "count_row"))
                block = s.start()

                @block.tensor
                def _(pe):
                    for k in range(NT):
                        if k >= 8:
                            pe.wait_ge(taken, k - 7)
                        nc.tensor.matmul(ps[:, k % 8, 0:D], acc[0:D, k * P:(k + 1) * P], w2_sb[0:D, :], start=True, stop=False)
                        nc.tensor.matmul(ps[:, k % 8, 0:D], acc[D:D + 1, k * P:(k + 1) * P], w2_sb[D:D + 1, :], start=False, stop=True).then_inc(out_ready, 1)

                @block.vector
                def _(dve):
                    link = linker(dve, dve_link)
                    link(nc.vector.tensor_scalar(stat[:, 0, :], count[:], 1.0, None, ALU.max))
                    link(nc.vector.reciprocal(stat[:, 1, :], stat[:, 0, :]))
                    for k in range(NT):
                        dve.wait_ge(out_ready, k + 1)
                        nc.vector.scalar_tensor_tensor(tmp[:, k, :], ps[:, k % 8, 0:D], stat[:, 1, k:k + 1], h_sb[:, k, 0:D],
                                                       ALU.mult, ALU.add).then_inc(taken, 1)
                    dve.wait_ge(taken, NT)
                    v = lambda i: stat[:, i, :]
                    wide = lambda i: stat[:, i, :].unsqueeze(2).to_broadcast([P, NT, D])
                    link(nc.vector.tensor_reduce(v(0), tmp[:], AX_X, ALU.add))
                    link(nc.vector.tensor_scalar(v(0), v(0), 1.0 / D, None, ALU.mult))
                    link(nc.vector.tensor_tensor(tmp[:], tmp[:], wide(0), ALU.subtract))
                    link(nc.vector.tensor_tensor(h_sb[:, :, 0:D], tmp[:], tmp[:], ALU.mult))
                    link(nc.vector.tensor_reduce(v(1), h_sb[:, :, 0:D], AX_X, ALU.add))
                    nc.vector.tensor_scalar(v(1), v(1), 1.0 / D, LN_EPS, ALU.mult, ALU.add).then_inc(var_ready, 1)
                    dve.wait_ge(root, 1)
                    link(nc.vector.reciprocal(v(2), v(1)))
                    link(nc.vector.tensor_tensor(tmp[:], tmp[:], wide(2), ALU.mult))
                    link(nc.vector.tensor_tensor(tmp[:], tmp[:], row_of("gamma", NT), ALU.mult))
                    link(nc.vector.tensor_tensor(tmp[:], tmp[:], row_of("beta3", NT), ALU.add))
                    nc.vector.tensor_tensor(x_sb[:], x_sb[:], tmp[:], ALU.add).then_inc(done, 1)

                @block.scalar
                def _(act):
                    act.wait_ge(var_ready, 1)
                    nc.scalar.activation(stat[:, 1, :], stat[:, 1, :], ACT.Sqrt).then_inc(root, 1)

                @block.sync
                def _(sp):
                    sp.wait_ge(done, 1)
                    sp.dma_start(out.rearrange("(k p) d -> p k d", p=P), x_sb[:]).then_inc(stored, 16)
                    sp.wait_ge(stored, 16)

        load_indices()
        attention_nodes()
        attention_scores()
        attention_weights()
        sum_edges("kept", D + 1)
        add_attention()
        sum_edges("table", D + 1, source=h_sb[:, :, 0:D], rest=tmp[:])
        message_nodes()
        sum_edges("table", D, source=tmp[:], rest=h_sb[:, :, 0:D])
        update_nodes()
        sum_edges("edge")
        finish_nodes()


def kernel(x, src, dst, edge_attr_32, L0_gnn_W, L0_gnn_beta, L2_gnn_WM1, L2_gnn_bM1, L2_gnn_WM2, L2_gnn_bM2, L2_gnn_WM3, L2_gnn_bM3,
           L2_gnn_WU1, L2_gnn_bU1, L2_gnn_WU2, L2_gnn_bU2, L2_gnn_WU3, L2_gnn_bU3, L3_gnn_W1, L3_gnn_b1, L3_gnn_W2, L3_gnn_b2,
           L3_gnn_gamma, L3_gnn_beta):
    import numpy as np
    import concourse.bacc as bacc
    from concourse.bass_utils import run_bass_kernel_spmd

    f = np.float32
    x_pad = np.zeros((NP, D), f)
    x_pad[:N] = x
    src_pad = np.zeros(EP, np.int32)
    src_pad[:E] = src
    dst_pad = np.full(EP, PAD_DST, np.int32)
    dst_pad[:E] = dst
    edge_t = np.zeros((EF, EP), f)
    edge_t[:, :E] = np.asarray(edge_attr_32).T
    row_vectors = [L2_gnn_bM3, L2_gnn_bU3, L3_gnn_b1, L3_gnn_gamma, L3_gnn_beta]
    rows = np.ascontiguousarray(np.broadcast_to(np.stack([np.asarray(v) for v in row_vectors])[None], (P, len(row_vectors), D)))
    cols = np.ascontiguousarray(np.stack([np.asarray(v) for v in (L2_gnn_bM1, L2_gnn_bM2, L2_gnn_bU1, L2_gnn_bU2)], axis=1))
    arrays = {
        "x": x_pad, "src": src_pad, "dst": dst_pad, "edge_t": edge_t,
        "beta": np.ascontiguousarray(np.broadcast_to(np.asarray(L0_gnn_beta)[None], (P, 1))), "rows": rows, "cols": cols,
        "w0t": np.ascontiguousarray(np.asarray(L0_gnn_W).T),
        "wm1": np.asarray(L2_gnn_WM1), "wm2": np.asarray(L2_gnn_WM2), "wm3": np.asarray(L2_gnn_WM3),
        "wu1": np.asarray(L2_gnn_WU1), "wu2": np.asarray(L2_gnn_WU2), "wu3": np.asarray(L2_gnn_WU3),
        "w1": np.asarray(L3_gnn_W1), "w2": np.asarray(L3_gnn_W2), "b2": np.asarray(L3_gnn_b2).reshape(1, D),
    }
    nc = bacc.Bacc("TRN2", target_bir_lowering=False, num_devices=1)
    args = [nc.dram_tensor("in_" + n, a.shape, mybir.dt.from_np(a.dtype), kind="ExternalInput").ap() for n, a in arrays.items()]
    result = nc.dram_tensor("out_x", (NP, D), F32, kind="ExternalOutput").ap()
    gnn_kernel(nc, *args, result)
    r = run_bass_kernel_spmd(nc, [{"in_" + n: a for n, a in arrays.items()}], core_ids=[0])
    return r.results[0]["out_x"][:N]
```

```python
from contextlib import ExitStack

import concourse.bass as bass
from concourse import mybir

P = 128
D = 64
EF = 32
H = 128
N = 6250
E = 206250
NT = -(-N // P)
NP = NT * P
HB = 4
NG = 4
AHEAD = 2
BT = NG * HB
ZERO = 1 + (NG - 2) * HB
LATE = 2
NB = -(-E // (P * BT))
T = NB * BT
EP = T * P
TB = T // P
TR = T - TB * P
TBS = TB + 1
TW = D + 2
ACC = NP + P
PAD_DST = 16384
SPAN = 32
CD = 9
CW = P // CD
WD = CW * CD
NW = -(-N // WD)
NC = NW * CW
CT = 4
KEYS = NT * CD
CB = -(-(NC + 1) // P)
HOT = 7
RING = HOT * CD
RING_KEYS = RING * NT
EARLY = 4
EARLY_KEYS = 6
GROUP_CHUNKS = [2, 2, 2, 1] * 2
STRIPS = 3
SPLIT = 3
LN_EPS = 1e-5
NORM_EPS = 1e-12
FAR = -1.0e38

ALU = mybir.AluOpType
ACT = mybir.ActivationFunctionType
F32 = mybir.dt.float32
I32 = mybir.dt.int32
U32 = mybir.dt.uint32
BF16 = mybir.dt.bfloat16
F16 = mybir.dt.float16
AX_X = mybir.AxisListType.X
PE_ENGINE = [mybir.EngineType.PE]
DVE_ENGINE = [mybir.EngineType.DVE]
SP_ENGINE = [mybir.EngineType.SP]
POOL_ENGINE = [mybir.EngineType.Pool]
ROWS = ["bM3", "bU3", "b1", "gamma", "beta3"]
assert EP == T * P and E <= (T - HB) * P and sum(GROUP_CHUNKS) == CW and 2 * NW + 1 == NB and NW % 2 == 0 and NB % 2 == 1 and NW * WD <= ACC and NT % 2
BK = 7
NBK = NT // BK
assert NBK * BK == NT and NBK < 8 and BK * (D + 1) <= 512
assert 2 * SPAN < RING + 2 and RING_KEYS // 2 < 2048 - NT


def gnn_kernel(nc, x, src, dst, edge_t, beta, rows, cols, w0t, wm1, wm2, wm3, wu1, wu2, wu3, w1, w2, b2, out):
    ctx = ExitStack()
    with ctx:
        def sb(name, shape, dt=F32):
            return ctx.enter_context(nc.sbuf_tensor(name, shape, dt))

        table = nc.dram_tensor("node_table", [NP, TW], F32, kind="Internal").ap()
        kept_rows = nc.dram_tensor("kept_rows", [P, T * TW], F32, kind="Internal").ap()
        counts = nc.dram_tensor("counts", [NW, 2, P, WD * NT // 2], F16, kind="Internal").ap()
        tiles_before = nc.dram_tensor("tiles_before", [CB * P], F32, kind="Internal").ap()
        edge_line = nc.dram_tensor("edge_line", [EP], F32, kind="Internal").ap()
        weight_line = nc.dram_tensor("weight_line", [EP], F32, kind="Internal").ap()

        ident = sb("ident", [P, P])
        iota = sb("iota", [P, P])
        iota_lo = sb("iota_lo", [P, P], F16)
        iota_key = sb("iota_key", [P, RING_KEYS], F16)
        beta_sb = sb("beta_sb", [P, 1])
        rows_sb = sb("rows_sb", [P, len(ROWS), D])
        cols_sb = sb("cols_sb", [P, 4])
        w0_sb = sb("w0_sb", [D + 1, D + 1])
        wm1_sb = sb("wm1_sb", [D, H])
        wm2_sb = sb("wm2_sb", [H, H])
        wm3_sb = sb("wm3_sb", [H, D])
        wu1_sb = sb("wu1_sb", [D, 2, H])
        wu2_sb = sb("wu2_sb", [H, H])
        wu3_sb = sb("wu3_sb", [H, D])
        w1a_sb = sb("w1a_sb", [D, D])
        w1b_sb = sb("w1b_sb", [EF, D])
        w2_sb = sb("w2_sb", [D + 1, D])
        src_cols = sb("src_cols", [P, T + AHEAD * HB], I32)
        dst_cols = sb("dst_cols", [P, T])
        dloc = sb("dloc", [P, T])
        key_lo = sb("key_lo", [P, T, 2])
        chunk_tile = sb("chunk_tile", [1, NC + EARLY_KEYS], I32)
        regular = sb("regular", [1, 1], I32)
        score = sb("score", [P, T])
        base_row = sb("base_row", [1, (NG + LATE) * HB + T], I32)
        group_row = sb("group_row", [1, NG + LATE + T // HB], I32)
        x_sb = sb("x_sb", [P, NT, D])
        h_sb = sb("h_sb", [P, NT, TW])
        tmp = sb("tmp", [P, NT, D])
        stat = sb("stat", [P, 4, NT])
        count = sb("count", [P, NT])
        acc_all = sb("acc_all", [P, ACC])
        acc = acc_all[0:D + 1, :]
        hT = sb("hT", [D, ACC])
        ps = ctx.enter_context(nc.psum_tensor("ps", [P, 8, 512], F32))

        stages = [0]

        class Stage:

            def __init__(self):
                stages[0] += 1
                self.tag = f"s{stages[0]}_"
                self.ctx = ExitStack()
                self.sems = []

            def __enter__(self):
                return self

            def sem(self, name):
                self.sems.append(nc.alloc_semaphore(name=self.tag + name))
                return self.sems[-1]

            def sb(self, name, shape, dt=F32):
                return self.ctx.enter_context(nc.sbuf_tensor(self.tag + name, shape, dt))

            def start(self):
                self.idle = self.sem("idle")
                return self.ctx.enter_context(nc.Block())

            def __exit__(self, *what):
                self.ctx.__exit__(*what)
                if what[0] is None:
                    nc.clear_and_free_semaphores(self.sems)
                    nc.all_engine_barrier()

        def linker(eng, sem):
            done = [0]

            def link(ins, n=1):
                done[0] += n
                ins.then_inc(sem, n)
                eng.wait_ge(sem, done[0])
            return link

        def on_engine(eng, engines, fast, slow):
            flag = nc.values_load(regular[0:1, 0:1], engines=engines, min_val=0, max_val=1,
                                  skip_runtime_bounds_check_because="a product of two comparisons")
            with eng.If(flag):
                fast()
            with eng.Else():
                slow()

        def load_indices():
            with Stage() as s:
                src_raw, dst_raw = s.sb("src_raw", [P, TBS, P], I32), s.sb("dst_raw", [P, TBS, P], I32)
                src_f, dst_f = s.sb("src_f", [P, TBS, P]), s.sb("dst_f", [P, TBS, P])
                first = s.sb("first", [P, T])
                below = s.sb("below", [P, T])
                threshold = s.sb("threshold", [P, CB])
                before = s.sb("before", [P, CB])
                row = s.sb("row", [1, 3, CB * P])
                ints = h_sb[:].rearrange("p k d -> p (k d)")[:, 0:2 * T].bitcast(I32).rearrange("p (a t) -> p a t", a=2)
                verdict = s.sb("verdict", [1, 8])
                names = ("weights_in", "edges_in", "consts", "zeroed", "floats", "turned", "copied", "first_row", "spread",
                         "dve_link", "counted", "row_out", "row_back")
                (weights_in, edges_in, consts, zeroed, floats, turned, copied, first_row, spread,
                 dve_link, counted, row_out, row_back) = (s.sem(n) for n in names)
                loads = [(x_sb[:], x.rearrange("(k p) d -> p k d", p=P)), (beta_sb[:], beta), (rows_sb[:], rows), (cols_sb[:], cols),
                         (w0_sb[0:D, 0:D], w0t), (wm1_sb[:], wm1), (wm2_sb[:], wm2), (wm3_sb[:], wm3),
                         (wu1_sb[:], wu1.rearrange("(c k) h -> k c h", c=2)), (wu2_sb[:], wu2), (wu3_sb[:], wu3),
                         (w1a_sb[:], w1[0:D, :]), (w1b_sb[:], w1[D:D + EF, :]), (w2_sb[0:D, :], w2), (w2_sb[D:D + 1, :], b2)]
                block = s.start()

                @block.sync
                def _(sp):
                    whole = TB * P * P
                    for raw, line in ((src_raw, src), (dst_raw, dst)):
                        sp.dma_start(raw[:, 0:TB, :], line[0:whole].rearrange("(k p e) -> p k e", p=P, e=P)).then_inc(edges_in, 16)
                        sp.dma_start(raw[0:TR, TB, :], line[whole:EP].rearrange("(p e) -> p e", e=P)).then_inc(edges_in, 16)
                    for to, what in loads:
                        sp.dma_start(to, what).then_inc(weights_in, 16)
                    sp.wait_ge(counted, 1)
                    sp.dma_start(tiles_before.rearrange("(b p) -> p b", p=P), before[:],
                                 allow_slow_non_contiguous=True).then_inc(row_out, 16)
                    sp.wait_ge(row_out, 16)
                    sp.dma_start(row[0:1, 0, :], tiles_before.rearrange("(a n) -> a n", a=1)).then_inc(row_back, 16)
                    sp.wait_ge(row_back, 16)
                    sp.wait_ge(weights_in, 16 * len(loads))

                @block.gpsimd
                def _(pool):
                    nc.gpsimd.memset(ident[:], 0.0).then_inc(zeroed, 1)
                    numbers = dict(allow_small_or_imprecise_dtypes=True)
                    nc.gpsimd.iota(iota[:], pattern=[[1, P]], base=0, channel_multiplier=0, **numbers)
                    nc.gpsimd.iota(iota_lo[:], pattern=[[1, P]], base=0, channel_multiplier=0, **numbers)
                    nc.gpsimd.iota(iota_key[:], pattern=[[1, RING_KEYS]], base=-(RING_KEYS // 2), channel_multiplier=0, **numbers)
                    nc.gpsimd.iota(threshold[:], pattern=[[CD * P, CB]], base=0, channel_multiplier=CD, **numbers)
                    pool.wait_ge(zeroed, 1)
                    nc.gpsimd.affine_select(out=ident[:], in_=ident[:], compare_op=ALU.not_equal, fill=1.0,
                                            base=0, pattern=[[-1, P]], channel_multiplier=1).then_inc(consts, 1)
                    pool.wait_ge(first_row, 1)
                    nc.gpsimd.partition_broadcast(first[:], dst_cols[0:1, :], P).then_inc(spread, 1)

                @block.tensor
                def _(pe):
                    pe.wait_ge(consts, 1)
                    pe.wait_ge(floats, 2)
                    n = 0
                    for raw in (src_f, dst_f):
                        for k in range(TBS):
                            rows_in = P if k < TB else TR
                            if n >= 8:
                                pe.wait_ge(copied, n - 7)
                            nc.tensor.transpose(ps[:, n % 8, 0:rows_in], raw[0:rows_in, k, :], ident[0:rows_in, 0:rows_in]).then_inc(turned, 1)
                            n += 1

                @block.vector
                def _(dve):
                    link = linker(dve, dve_link)
                    nc.vector.memset(w0_sb[:, D:D + 1], 0.0)
                    nc.vector.memset(w0_sb[D:D + 1, 0:D], 0.0)
                    nc.vector.memset(base_row[:], 0)
                    nc.vector.memset(group_row[:], 0)
                    nc.vector.memset(src_cols[:, T:], 0)
                    link(nc.vector.memset(hT[:, NP:], 0.0))
                    nc.vector.memset(w0_sb[D:D + 1, D:D + 1], 1.0)
                    dve.wait_ge(edges_in, 64)
                    for f, raw in ((src_f, src_raw), (dst_f, dst_raw)):
                        nc.vector.tensor_copy(f[:, 0:TB, :], raw[:, 0:TB, :])
                        nc.vector.tensor_copy(f[0:TR, TB, :], raw[0:TR, TB, :]).then_inc(floats, 1)
                    n = 0
                    for to in (src_cols, dst_cols):
                        for k in range(TBS):
                            cols_in = P if k < TB else TR
                            dve.wait_ge(turned, n + 1)
                            nc.vector.tensor_copy(to[:, k * P:k * P + cols_in], ps[:, n % 8, 0:cols_in]).then_inc(copied, 1)
                            n += 1
                    dve.wait_ge(copied, n)
                    dve.sem_inc(first_row, 1)
                    low, high = (raw[:].rearrange("p k e -> p (k e)")[:, 0:T] for raw in (src_raw, dst_raw))
                    nc.vector.tensor_copy(ints[:, 0, :], src_cols[:, 0:T])
                    link(nc.vector.tensor_copy(ints[:, 1, :], dst_cols[:]))
                    nc.vector.tensor_scalar(low, ints[:, 0, :], 127, None, ALU.bitwise_and)
                    link(nc.vector.tensor_scalar(high, ints[:, 0, :], 7, None, ALU.arith_shift_right))
                    nc.vector.tensor_copy(key_lo[:, :, 1], low)
                    link(nc.vector.tensor_copy(key_lo[:, :, 0], high))
                    link(nc.vector.tensor_scalar(low, ints[:, 1, :], -(RING - 1) / 2, 1.0 / RING, ALU.add, ALU.mult))
                    link(nc.vector.scalar_tensor_tensor(high, low, -float(RING), ints[:, 1, :], ALU.mult, ALU.add))
                    link(nc.vector.scalar_tensor_tensor(key_lo[:, :, 0], high, float(NT), key_lo[:, :, 0], ALU.mult, ALU.add))
                    link(nc.vector.tensor_scalar(below[:], dst_cols[:], float(N), 4096.0, ALU.is_ge, ALU.mult))
                    link(nc.vector.scalar_tensor_tensor(key_lo[:, :, 0], below[:], -float(RING_KEYS // 2), key_lo[:, :, 0], ALU.add, ALU.add))
                    dve.wait_ge(spread, 1)
                    for b in range(CB):
                        link(nc.vector.tensor_scalar(below[:], first[:], threshold[:, b:b + 1], 0.0, ALU.is_lt, ALU.add, accum_out=before[:, b:b + 1]))
                    dve.sem_inc(counted, 1)
                    link(nc.vector.tensor_scalar(first[:], first[:], float(N), None, ALU.min))
                    nc.vector.tensor_copy(base_row[:, LATE * HB:LATE * HB + T], first[0:1, :])
                    nc.vector.tensor_copy(group_row[:, LATE:LATE + T // HB], first[0:1, 0:T:HB])
                    nc.vector.tensor_tensor(dloc[:], dst_cols[:], first[:], ALU.subtract)
                    link(nc.vector.tensor_tensor(below[0:1, 0:T // HB - 1], first[0:1, HB:T:HB], first[0:1, 0:T - HB:HB], ALU.subtract))
                    link(nc.vector.tensor_reduce(verdict[:, 2:3], below[0:1, 0:T // HB - 1], AX_X, ALU.max))
                    dve.wait_ge(row_back, 16)
                    r = lambda n, *at: row[0:1, n, slice(*at)]
                    link(nc.vector.tensor_scalar(r(1, NC), r(0, NC), -1.0, 0.0, ALU.add, ALU.max))
                    nc.vector.memset(chunk_tile[:, NC:], 0)
                    nc.vector.tensor_scalar(chunk_tile[:, 0:NC], r(1, NC), float(T - CT), None, ALU.min)
                    link(nc.vector.tensor_tensor(r(2, NC), r(0, 1, NC + 1), r(1, NC), ALU.subtract))
                    link(nc.vector.tensor_reduce(verdict[:, 0:1], r(2, NC), AX_X, ALU.max))
                    nc.vector.tensor_scalar(verdict[:, 1:2], verdict[:, 0:1], float(CT), None, ALU.is_le)
                    link(nc.vector.tensor_scalar(verdict[:, 3:4], verdict[:, 2:3], float(SPAN), None, ALU.is_lt))
                    link(nc.vector.tensor_tensor(regular[:], verdict[:, 1:2], verdict[:, 3:4], ALU.mult))

                    def from_group():
                        grouped = lambda a: a[:].rearrange("p (q g) -> p q g", g=HB)
                        nc.vector.tensor_tensor(grouped(dloc), grouped(dst_cols), grouped(first)[:, :, 0:1].to_broadcast([P, T // HB, HB]),
                                                ALU.subtract).then_inc(s.idle, 1)
                    on_engine(dve, DVE_ENGINE, from_group, lambda: dve.sem_inc(s.idle, 1))

        def center(link, k, var_ready=None):
            v = lambda i: stat[:, i, k]
            wide = lambda i: v(i).unsqueeze(2).to_broadcast([P, k.stop - k.start, D])
            link(nc.vector.tensor_reduce(v(0), x_sb[:, k, :], AX_X, ALU.add))
            link(nc.vector.tensor_scalar(v(0), v(0), 1.0 / D, None, ALU.mult))
            link(nc.vector.tensor_tensor(tmp[:, k, :], x_sb[:, k, :], wide(0), ALU.subtract))
            link(nc.vector.tensor_tensor(h_sb[:, k, 0:D], tmp[:, k, :], tmp[:, k, :], ALU.mult))
            link(nc.vector.tensor_reduce(v(1), h_sb[:, k, 0:D], AX_X, ALU.add))
            last = nc.vector.tensor_scalar(v(1), v(1), 1.0 / D, LN_EPS, ALU.mult, ALU.add)
            if var_ready:
                last.then_inc(var_ready, 1)
            else:
                link(last)

        def scale_relu(dve, link, root, h_ready):
            dve.wait_ge(root, 1)
            link(nc.vector.reciprocal(stat[:, 2, :], stat[:, 1, :]))
            for c, wide in CH:
                k, n = slice(c // P, (c + wide) // P), wide // P
                nc.vector.scalar_tensor_tensor(h_sb[:, k, 0:D], tmp[:, k, :], 0.0, stat[:, 2, k].unsqueeze(2).to_broadcast([P, n, D]),
                                               ALU.max, ALU.mult).then_inc(h_ready, 1)

        ALL = slice(0, NT)
        CH = [(c, min(512, NP - c)) for c in range(0, NP, 512)]

        def bank(b, width):
            return ps[:, b, 0:BK * width].rearrange("p (k d) -> p k d", d=width)

        def of_bank(b):
            return slice(b * BK, (b + 1) * BK)

        def node_products(weights, width, out_ready):
            for k in range(NT):
                last = nc.tensor.matmul(ps[:, k // BK, k % BK * width:(k % BK + 1) * width], acc[:, k * P:(k + 1) * P], weights, start=True, stop=True)
                if k % BK == BK - 1:
                    last.then_inc(out_ready, 1)

        def turn_chunk(pe, source, q, bank, turned):
            c, wide = CH[q]
            for n in range(wide // P):
                last = nc.tensor.transpose(ps[0:D, bank, n * P:(n + 1) * P], source[:, c // P + n, 0:D], ident[:])
            last.then_inc(turned, 1)

        def save_chunk(act, q, bank, turned, freed):
            c, wide = CH[q]
            act.wait_ge(turned, q + 1)
            nc.scalar.copy(hT[:, c:c + wide], ps[0:D, bank, 0:wide]).then_inc(freed, 1)

        def attention_nodes():
            with Stage() as s:
                dve_link, var_ready, root, h_ready, norm_ready, norm_root, unit, turned, freed, stored, table_ready = (
                    s.sem(n) for n in ("dve_link", "var_ready", "root", "h_ready", "norm_ready", "norm_root", "unit", "turned", "freed", "stored", "table_ready"))
                block = s.start()

                @block.vector
                def _(dve):
                    link = linker(dve, dve_link)
                    center(link, ALL, var_ready)
                    scale_relu(dve, link, root, h_ready)
                    dve.wait_ge(h_ready, len(CH))
                    nc.vector.memset(h_sb[:, :, D:D + 1], 1.0)
                    link(nc.vector.tensor_tensor(tmp[:], h_sb[:, :, 0:D], h_sb[:, :, 0:D], ALU.mult))
                    nc.vector.tensor_reduce(stat[:, 0, :], tmp[:], AX_X, ALU.add).then_inc(norm_ready, 1)
                    dve.wait_ge(norm_root, 1)
                    link(nc.vector.tensor_scalar(stat[:, 1, :], stat[:, 0, :], NORM_EPS, None, ALU.max))
                    link(nc.vector.reciprocal(stat[:, 2, :], stat[:, 1, :]))
                    nc.vector.tensor_copy(h_sb[:, :, D + 1], stat[:, 2, :]).then_inc(table_ready, 1)
                    for c, wide in CH:
                        k = slice(c // P, (c + wide) // P)
                        nc.vector.tensor_tensor(tmp[:, k, :], h_sb[:, k, 0:D], stat[:, 2, k].unsqueeze(2).to_broadcast([P, wide // P, D]), ALU.mult).then_inc(unit, 1)

                @block.scalar
                def _(act):
                    act.wait_ge(var_ready, 1)
                    nc.scalar.activation(stat[:, 1, :], stat[:, 1, :], ACT.Sqrt).then_inc(root, 1)
                    act.wait_ge(norm_ready, 1)
                    nc.scalar.activation(stat[:, 0, :], stat[:, 0, :], ACT.Sqrt).then_inc(norm_root, 1)
                    for q in range(len(CH)):
                        save_chunk(act, q, q % 8, turned, freed)

                @block.tensor
                def _(pe):
                    for q in range(len(CH)):
                        pe.wait_ge(unit, q + 1)
                        if q >= 8:
                            pe.wait_ge(freed, q - 7)
                        turn_chunk(pe, tmp, q, q % 8, turned)

                @block.sync
                def _(sp):
                    sp.wait_ge(table_ready, 1)
                    sp.dma_start(table.rearrange("(k p) d -> p k d", p=P), h_sb[:]).then_inc(stored, 16)
                    sp.wait_ge(stored, 16)

        def window_bases(engines, i, behind, span):
            clamped = "the setup clamps every start to the number of nodes"

            def load(row, at, n):
                at = row[0:1, at:at + n] if isinstance(i, int) else row[0:1, bass.ds(at, n)]
                return nc.values_load_multi_w_load_instructions(at, engines=engines, min_val=0, max_val=N, skip_runtime_bounds_check_because=clamped)[1]

            if span == SPAN:
                bases = load(group_row, i * NG + (LATE - behind), NG)
                return lambda h: [bases[h]] * HB
            return lambda h: load(base_row, i * BT + (h + LATE - behind) * HB, HB)

        def one_hot(onehot, h, i, span):
            return nc.vector.tensor_tensor(
                onehot[:, h, :, 0:span], iota[:, 0:span].unsqueeze(1).to_broadcast([P, HB, span]),
                dloc[:, bass.ds(i * BT + h * HB, HB)].unsqueeze(2).to_broadcast([P, HB, span]), ALU.is_equal)

        def gather(pool, i, h, stage, got, staged, gathered, batches):
            pool.wait_ge(staged[h], i + 1)
            pool.sem_inc(batches, 1)
            for g in range(HB):
                pool.indirect_dma_start(out=got[:, h, g, :], out_offset=None, in_=table,
                                        in_offset=bass.IndirectOffsetOnAxis(ap=stage[:, h, g:g + 1].bitcast(U32), axis=0)
                                        ).then_inc(gathered[h], 16)

        def later(i, h):
            return (i, h + AHEAD) if h + AHEAD < NG else (i + 1, h + AHEAD - NG)

        def stage_indices(i, h, stage, rows_free, staged):
            rows_free(i, h)
            nc.scalar.copy(stage[:, h, :], src_cols[:, i * BT + h * HB:i * BT + (h + 1) * HB] if isinstance(i, int)
                           else src_cols[:, bass.ds(i * BT + h * HB, HB)]).then_inc(staged[h], 1)

        def attention_scores():
            with Stage() as s:
                per_group = lambda n: [s.sem(f"{n}_{h}") for h in range(NG)]
                stage, got = s.sb("stage", [P, NG, HB], I32), s.sb("got", [P, NG, HB, TW])
                gotT, dots = s.sb("gotT", [D, NG, HB, P]), s.sb("dots", [P, NG, HB])
                picked, local = s.sb("picked", [P, HB, P]), s.sb("local", [P, NG, HB])
                keys = s.sb("keys", [P, HOT, CT, 2])
                hot_key = acc_all[:, 0:HOT * CT * KEYS // 2].bitcast(BF16).rearrange("p (m j f) -> p m j f", m=HOT, j=CT)
                hot_lo = s.sb("hot_lo", [P, HOT, CT, P], BF16)
                strip = s.sb("strip", [P, 2, WD * NT // 2], F16)
                staged, gathered, turned, saved, dotted, used, kept, stored = (
                    per_group(n) for n in ("staged", "gathered", "turned", "saved", "dotted", "used", "kept", "stored"))
                batches, begun, summed = s.sem("batches"), s.sem("begun"), s.sem("summed")
                keyed, hot, counted, copied, localized = (s.sem(n) for n in ("keyed", "hot", "counted", "copied", "localized"))
                strip_out, strip_free = ([s.sem(f"{n}_{half}") for half in range(2)] for n in ("strip_out", "strip_free"))
                block = s.start()
                PER = CW // 2
                STEPS = 2 * NW
                FIRST = [sum(GROUP_CHUNKS[:q]) for q in range(2 * NG)]

                @block.gpsimd
                def _(pool):
                    with pool.Fori(0, NB) as i:
                        for h in range(NG):
                            gather(pool, i, h, stage, got, staged, gathered, batches)

                @block.sync
                def _(sp):
                    for h in range(NG):
                        sp.sem_inc(kept[h], 1)
                    for half in range(2):
                        sp.sem_inc(strip_free[half], 1)

                    def keep_rows(i):
                        for h in range(NG):
                            sp.wait_ge(gathered[h], i * (16 * HB) + 16 * HB)
                            sp.dma_start(kept_rows[:, bass.ds(i * (BT * TW) + h * (HB * TW), HB * TW)],
                                         got[:, h, :, :].rearrange("p g f -> p (g f)")).then_inc(stored[h], 16)
                            sp.wait_ge(stored[h], i * 16 + 16)
                            sp.sem_inc(kept[h], 1)

                    keep_rows(0)
                    with sp.Fori(0, NW) as w:
                        for half in range(2):
                            sp.wait_ge(copied, w * CW + ((half + 1) * PER + 2))
                            sp.dma_start(counts[bass.ds(w, 1), half, :, :].rearrange("a p f -> p (a f)"),
                                         strip[:, half, :]).then_inc(strip_out[half], 16)
                            keep_rows(w * 2 + (half + 1))
                            sp.wait_ge(strip_out[half], w * 16 + 16)
                            sp.sem_inc(strip_free[half], 1)

                @block.scalar
                def _(act):
                    def rows_free(i, h):
                        act.wait_ge(used[h], i + 1)
                        act.wait_ge(kept[h], i + 1)

                    def save(i, h):
                        act.wait_ge(turned[h], i + 1)
                        nc.scalar.copy(gotT[:, h, :, :], ps[0:D, h % 2, :].rearrange("p (g e) -> p g e", e=P)).then_inc(saved[h], 1)

                    def chunk_tiles(first, n):
                        return nc.values_load_multi_w_load_instructions(
                            chunk_tile[0:1, bass.ds(first, n)], engines=[mybir.EngineType.Activation], min_val=0, max_val=T - CT,
                            skip_runtime_bounds_check_because="the setup clamps every chunk's first tile")[1]

                    def chunk_keys(chunk, tile, m):
                        act.wait_ge(hot, chunk + 1)
                        nc.scalar.copy(keys[:, m, :, :], key_lo[:, bass.ds(tile, CT), :]).then_inc(keyed, 1)

                    def take_local(i, h):
                        act.wait_ge(used[h], i + 1)
                        nc.scalar.copy(local[:, h, :], dloc[:, bass.ds(i * BT + h * HB, HB)]).then_inc(localized, 1)

                    for h in range(AHEAD):
                        stage_indices(0, h, stage, rows_free, staged)
                    act.sem_inc(copied, 2)
                    for m, tile in enumerate(chunk_tiles(0, EARLY_KEYS)):
                        chunk_keys(m, tile, m)
                    with act.Fori(0, NW) as w:
                        for half in range(2):
                            i = w * 2 + half
                            tiles = chunk_tiles(w * CW + (half * PER + EARLY_KEYS), PER)
                            for h in range(NG):
                                q = half * NG + h
                                save(i, h)
                                stage_indices(*later(i, h), stage, rows_free, staged)
                                take_local(i, h)
                                begin = FIRST[q] + sum(GROUP_CHUNKS[(q + n) % (2 * NG)] for n in range(3))
                                for c in range(begin, begin + GROUP_CHUNKS[(q + 3) % (2 * NG)]):
                                    chunk_keys(w * CW + c, tiles[c - half * PER - EARLY_KEYS], c % HOT)
                                for c in range(FIRST[q], FIRST[q] + GROUP_CHUNKS[q]):
                                    act.wait_ge(counted, w * CW + (c + HOT + 1))
                                    if c == half * PER:
                                        act.wait_ge(strip_free[half], w + 1)
                                    nc.scalar.copy(strip[:, half, (c - half * PER) * KEYS:(c - half * PER + 1) * KEYS],
                                                   ps[:, 2 + c % 2, 0:KEYS]).then_inc(copied, 1)
                    with act.Fori(STEPS, NB) as i:
                        for h in range(NG):
                            save(i, h)
                            stage_indices(*later(i, h), stage, rows_free, staged)
                            take_local(i, h)

                def tensor(pe, span):
                    for h in range(NG):
                        pe.sem_inc(dotted[h], 1)

                    def turn(i, h):
                        pe.wait_ge(gathered[h], i * (16 * HB) + 16 * HB)
                        pe.sem_inc(begun, 1)
                        for g in range(HB):
                            last = nc.tensor.transpose(ps[0:D, h % 2, g * P:(g + 1) * P], got[:, h, g, 0:D], ident[:])
                        last.then_inc(turned[h], 1)

                    def dot(i, h, bases):
                        pe.wait_ge(saved[h], i + 1)
                        pe.wait_ge(used[h], i + 1)
                        for g in range(HB):
                            last = nc.tensor.matmul(ps[:, NG + h, g * span:(g + 1) * span], gotT[:, h, g, :],
                                                    hT[:, bass.ds(bases[g], span)], start=True, stop=True)
                        last.then_inc(dotted[h], 1)

                    with pe.Fori(0, NW) as w:
                        for half in range(2):
                            i = w * 2 + half
                            bases_of = window_bases(PE_ENGINE, i, 0, span)
                            for h in range(NG):
                                bases = bases_of(h)
                                turn(i, h)
                                q = half * NG + h
                                for c in range(FIRST[q], FIRST[q] + GROUP_CHUNKS[q]):
                                    pe.wait_ge(hot, w * CW + (c + HOT + 1))
                                    pe.wait_ge(copied, w * CW + (c + 1))
                                    for j in range(CT):
                                        last = nc.tensor.matmul(ps[:, 2 + c % 2, 0:KEYS], hot_lo[:, c % HOT, j, :], hot_key[:, c % HOT, j, :],
                                                                start=(j == 0), stop=(j == CT - 1))
                                    last.then_inc(counted, 1)
                                dot(i, h, bases)
                    with pe.Fori(STEPS, NB) as i:
                        bases_of = window_bases(PE_ENGINE, i, 0, span)
                        for h in range(NG):
                            bases = bases_of(h)
                            turn(i, h)
                            dot(i, h, bases)

                def vector(dve, span):
                    for h in range(NG):
                        dve.sem_inc(used[h], 1)
                    dve.sem_inc(counted, HOT)
                    dve.sem_inc(hot, HOT)

                    def chunk_hot(chunk, m):
                        dve.wait_ge(keyed, chunk + 1)
                        dve.wait_ge(counted, chunk + 1)
                        for j in range(CT):
                            nc.vector.tensor_scalar(hot_key[:, m, j, :], iota_key[:, m * KEYS:(m + 1) * KEYS], keys[:, m, j, 0:1], None, ALU.is_equal)
                            last = nc.vector.tensor_scalar(hot_lo[:, m, j, :], iota_lo[:], keys[:, m, j, 1:2], None, ALU.is_equal)
                        last.then_inc(hot, 1)

                    def score_group(i, h):
                        dve.wait_ge(localized, i * NG + (h + 1))
                        dve.wait_ge(dotted[h], i + 2)
                        for g in range(HB):
                            last = nc.vector.scalar_tensor_tensor(picked[:, g, 0:span], iota[:, 0:span], local[:, h, g:g + 1],
                                                                  ps[:, NG + h, g * span:(g + 1) * span],
                                                                  ALU.is_equal, ALU.mult, accum_out=dots[:, h, g:g + 1])
                        last.then_inc(summed, 1)
                        dve.wait_ge(summed, i * NG + (h + 1))
                        nc.vector.tensor_tensor(score[:, bass.ds(i * BT + h * HB, HB)], dots[:, h, :], got[:, h, :, D + 1], ALU.mult).then_inc(used[h], 1)

                    for m in range(EARLY):
                        chunk_hot(m, m)
                    with dve.Fori(0, NW) as w:
                        for half in range(2):
                            i = w * 2 + half
                            for h in range(NG):
                                q = half * NG + h
                                begin = FIRST[q] + GROUP_CHUNKS[q] + GROUP_CHUNKS[(q + 1) % (2 * NG)]
                                ahead = range(begin, begin + GROUP_CHUNKS[(q + 2) % (2 * NG)])
                                for c in ahead:
                                    chunk_hot(w * CW + c, c % HOT)
                                score_group(i, h)
                    with dve.Fori(STEPS, NB) as i:
                        for h in range(NG):
                            score_group(i, h)

                @block.tensor
                def _(pe):
                    on_engine(pe, PE_ENGINE, lambda: tensor(pe, SPAN), lambda: tensor(pe, P))

                @block.vector
                def _(dve):
                    on_engine(dve, DVE_ENGINE, lambda: vector(dve, SPAN), lambda: vector(dve, P))

        def attention_weights():
            with ExitStack() as tmp_ctx, Stage() as s:
                def tb(name, shape, dt=F32):
                    return tmp_ctx.enter_context(nc.sbuf_tensor(name, shape, dt))
                lines = tb("lines", [P, TBS, P])
                value = tb("value", [P, T])[:]
                dst_i = tb("dst_i", [P, T], I32)
                dst_l = tb("dst_l", [P, T])
                cut = tb("cut", [P, T + 1])
                run = tb("run", [P, T])
                best = tmp[:].rearrange("p k d -> p (k d)")[:, 0:T]
                ends = tb("ends", [P, 4])
                line = tb("line", [4, P])
                flat = tb("flat", [1, 12, P + 2])
                carry = tb("carry", [P, 2])
                dst_in, turned, copied, sent, back, dve_link, pe_go, pe_done, shifted, wexp, out_sent, back2, turned2 = (
                    s.sem(n) for n in ("dst_in", "turned", "copied", "sent", "back", "dve_link", "pe_go", "pe_done", "shifted",
                                       "wexp", "out_sent", "back2", "turned2"))
                row_moved = s.sem("row_moved")
                scaled = s.sem("scaled")
                whole = TB * P * P
                block = s.start()

                @block.gpsimd
                def _(pool):
                    nc.gpsimd.memset(acc, 0.0).then_inc(s.idle, 1)

                @block.tensor
                def _(pe):
                    pe.wait_ge(scaled, 1)
                    for k in range(TBS):
                        n_in = P if k < TB else TR
                        if k >= 8:
                            pe.wait_ge(copied, k - 7)
                        nc.tensor.transpose(ps[0:n_in, k % 8, 0:P], score[:, k * P:k * P + n_in], ident[:]).then_inc(turned, 1)
                    pe.wait_ge(pe_go, 1)
                    nc.tensor.transpose(ps[0:4, 0, 0:P], ends[:], ident[:]).then_inc(pe_done, 1)
                    pe.wait_ge(pe_go, 2)
                    for n in range(2):
                        last = nc.tensor.matmul(ps[:, 1, n:n + 1], flat[0:1, 10 + n, 0:P], ident[0:1, 0:1], start=True, stop=True)
                    last.then_inc(pe_done, 1)
                    pe.wait_ge(back2, 32)
                    pe.wait_ge(copied, TBS + 2)
                    for k in range(TBS):
                        n_in = P if k < TB else TR
                        if k >= 8:
                            pe.wait_ge(copied, TBS + 2 + k - 7)
                        nc.tensor.transpose(ps[:, k % 8, 0:n_in], lines[0:n_in, k, :], ident[0:n_in, 0:n_in]).then_inc(turned2, 1)

                @block.sync
                def _(sp):
                    sp.dma_start(dst_i[:], dst.rearrange("(p j) -> p j", p=P)).then_inc(dst_in, 16)
                    sp.wait_ge(copied, TBS)
                    sp.dma_start(edge_line[0:whole].rearrange("(k p e) -> p k e", p=P, e=P), lines[:, 0:TB, :]).then_inc(sent, 16)
                    sp.dma_start(edge_line[whole:EP].rearrange("(p e) -> p e", e=P), lines[0:TR, TB, :]).then_inc(sent, 16)
                    sp.wait_ge(sent, 32)
                    sp.dma_start(value, edge_line.rearrange("(p j) -> p j", p=P)).then_inc(back, 16)
                    sp.wait_ge(copied, TBS + 1)
                    for n in range(4):
                        sp.dma_start(flat[0:1, n, 1:P + 1], line[n:n + 1, :]).then_inc(row_moved, 16)
                    sp.wait_ge(wexp, 1)
                    sp.dma_start(weight_line.rearrange("(p j) -> p j", p=P), run[:]).then_inc(out_sent, 16)
                    sp.wait_ge(out_sent, 16)
                    sp.dma_start(lines[:, 0:TB, :], weight_line[0:whole].rearrange("(k p e) -> p k e", p=P, e=P)).then_inc(back2, 16)
                    sp.dma_start(lines[0:TR, TB, :], weight_line[whole:EP].rearrange("(p e) -> p e", e=P)).then_inc(back2, 16)
                    sp.wait_ge(back2, 32)

                @block.scalar
                def _(act):
                    act.wait_ge(shifted, 1)
                    nc.scalar.activation(run[:], run[:], ACT.Exp).then_inc(wexp, 1)

                @block.vector
                def _(dve):
                    link = linker(dve, dve_link)
                    nc.vector.tensor_scalar(score[:], score[:], beta_sb[:, 0:1], None, ALU.mult).then_inc(scaled, 1)
                    for k in range(TBS):
                        n_in = P if k < TB else TR
                        dve.wait_ge(turned, k + 1)
                        nc.vector.tensor_copy(lines[0:n_in, k, :], ps[0:n_in, k % 8, 0:P]).then_inc(copied, 1)
                    dve.wait_ge(dst_in, 16)
                    link(nc.vector.tensor_copy(dst_l[:], dst_i[:]))
                    nc.vector.memset(cut[:, 0:1], FAR)
                    nc.vector.memset(cut[:, T:T + 1], FAR)
                    link(nc.vector.tensor_tensor(cut[:, 1:T], dst_l[:, 1:T], dst_l[:, 0:T - 1], ALU.not_equal))
                    link(nc.vector.tensor_scalar(cut[:, 1:T], cut[:, 1:T], FAR, None, ALU.mult))
                    dve.wait_ge(back, 16)
                    link(nc.vector.tensor_tensor_scan(run[:], cut[:, 0:T], value, FAR, ALU.add, ALU.max))
                    link(nc.vector.tensor_tensor_scan(best[:, ::-1], cut[:, 1:T + 1][:, ::-1], value[:, ::-1], FAR, ALU.add, ALU.max))
                    nc.vector.tensor_copy(ends[:, 0:1], dst_l[:, 0:1])
                    nc.vector.tensor_copy(ends[:, 1:2], dst_l[:, T - 1:T])
                    nc.vector.tensor_copy(ends[:, 2:3], run[:, T - 1:T])
                    nc.vector.tensor_copy(ends[:, 3:4], best[:, 0:1]).then_inc(pe_go, 1)
                    dve.wait_ge(pe_done, 1)
                    link(nc.vector.memset(flat[:], -1.0))
                    nc.vector.tensor_copy(line[:], ps[0:4, 0, 0:P]).then_inc(copied, 1)
                    dve.wait_ge(row_moved, 64)
                    row = lambda n, a, b: flat[0:1, n, a:b]
                    link(nc.vector.tensor_tensor(row(4, 1, P + 2), row(0, 1, P + 2), row(1, 0, P + 1), ALU.not_equal))
                    link(nc.vector.tensor_scalar(row(4, 1, P + 2), row(4, 1, P + 2), FAR, None, ALU.mult))
                    link(nc.vector.tensor_tensor(row(5, 1, P + 1), row(0, 1, P + 1), row(1, 1, P + 1), ALU.not_equal))
                    link(nc.vector.tensor_scalar(row(5, 1, P + 1), row(5, 1, P + 1), FAR, None, ALU.mult))
                    link(nc.vector.tensor_tensor(row(6, 1, P + 1), row(4, 1, P + 1), row(5, 1, P + 1), ALU.min))
                    link(nc.vector.tensor_tensor(row(7, 1, P + 1), row(4, 2, P + 2), row(5, 1, P + 1), ALU.min))
                    link(nc.vector.memset(row(8, 0, P + 2), FAR))
                    link(nc.vector.memset(row(9, 0, P + 2), FAR))
                    link(nc.vector.tensor_tensor_scan(row(8, 1, P + 1), row(6, 1, P + 1), row(2, 1, P + 1), FAR, ALU.add, ALU.max))
                    link(nc.vector.tensor_tensor_scan(row(9, 1, P + 1)[:, ::-1], row(7, 1, P + 1)[:, ::-1], row(3, 1, P + 1)[:, ::-1], FAR, ALU.add, ALU.max))
                    link(nc.vector.tensor_tensor(row(10, 0, P), row(8, 0, P), row(4, 1, P + 1), ALU.add))
                    link(nc.vector.tensor_tensor(row(11, 0, P), row(9, 2, P + 2), row(4, 2, P + 2), ALU.add))
                    nc.vector.tensor_scalar(flat[0:1, 10:12, 0:P], flat[0:1, 10:12, 0:P], FAR, None, ALU.max).then_inc(pe_go, 1)
                    dve.wait_ge(pe_done, 2)
                    nc.vector.tensor_copy(carry[:], ps[:, 1, 0:2]).then_inc(copied, 1)
                    dve.wait_ge(copied, TBS + 2)
                    nc.vector.memset(cut[:, 0:1], 0.0)
                    link(nc.vector.memset(cut[:, T:T + 1], 0.0))
                    link(nc.vector.tensor_tensor_scan(run[:], cut[:, 0:T], value, carry[:, 0:1], ALU.add, ALU.max))
                    link(nc.vector.tensor_tensor_scan(best[:, ::-1], cut[:, 1:T + 1][:, ::-1], value[:, ::-1], carry[:, 1:2], ALU.add, ALU.max))
                    link(nc.vector.tensor_tensor(best, best, run[:], ALU.max))
                    nc.vector.tensor_tensor(run[:], value, best, ALU.subtract).then_inc(shifted, 1)
                    for k in range(TBS):
                        n_in = P if k < TB else TR
                        dve.wait_ge(turned2, k + 1)
                        nc.vector.tensor_copy(score[:, k * P:k * P + n_in], ps[:, k % 8, 0:n_in]).then_inc(copied, 1)

        def general_sums(s, kind, width):
            per_group = lambda n: [s.sem(f"{n}_{h}") for h in range(NG)]
            got, onehot = s.sb("got", [P, 1 + (kind == "kept"), NG, HB, TW]), s.sb("onehot", [P, NG, HB, P])
            if kind != "kept":
                stage = s.sb("stage", [P, NG, HB], I32)
            if kind == "edge":
                msg, edge_sb = s.sb("msg", [P, NG, HB, D]), s.sb("edge_sb", [EF, NG, HB * P])
            ready, summed = (per_group(n) for n in ("ready", "summed"))
            rows_in = per_group("rows_in")
            if kind != "kept":
                staged, batches = per_group("staged"), s.sem("batches")
            if kind == "edge":
                joined, relued, edges_in, mapped = (per_group(n) for n in ("joined", "relued", "edges_in", "mapped"))
            added, hot = s.sem("added"), s.sem("hot")
            rows_used = joined if kind == "edge" else summed

            def each_step(eng, body):
                if kind == "kept":
                    with eng.Fori(0, NB // 2) as i:
                        for m in range(2):
                            body(i * 2 + m, m, i)
                    body(NB - 1, 0, NB // 2)
                else:
                    with eng.Fori(0, NB) as i:
                        body(i, 0, i)

            def wait_rows(eng, h, m, n):
                if kind == "kept":
                    eng.wait_ge(rows_in[m * 2 + h // 2], n * 16 + 16)
                else:
                    eng.wait_ge(rows_in[h], n * (16 * HB) + 16 * HB)

            def weigh(pool):
                def step(i, m, n):
                    for h in range(NG):
                        pool.wait_ge(hot, i * NG + (h + 1))
                        pool.sem_inc(s.idle, 1)
                        at = i * BT + h * HB
                        nc.gpsimd.tensor_tensor(onehot[:, h, :, 0:SPAN], onehot[:, h, :, 0:SPAN],
                                                (score[:, at:at + HB] if isinstance(i, int) else score[:, bass.ds(at, HB)]).unsqueeze(2).to_broadcast([P, HB, SPAN]),
                                                ALU.mult).then_inc(ready[h], 1)
                each_step(pool, step)

            def gpsimd(pool):
                if kind != "kept":
                    with pool.Fori(0, NB) as i:
                        for h in range(NG):
                            gather(pool, i, h, stage, got[:, 0], staged, rows_in, batches)

            def scalar(act):
                def rows_free(i, h):
                    act.wait_ge(rows_used[h], i + 1)

                if kind != "kept":
                    for h in range(AHEAD):
                        stage_indices(0, h, stage, rows_free, staged)
                    with act.Fori(0, NB) as i:
                        for h in range(NG):
                            if kind == "edge":
                                act.wait_ge(joined[h], i + 2)
                                nc.scalar.activation(msg[:, h, :, :], msg[:, h, :, :], ACT.Relu).then_inc(relued[h], 1)
                            stage_indices(*later(i, h), stage, rows_free, staged)

            def sync(sp):
                if kind == "kept":
                    HALF = BT * TW // 2

                    def load(i, m, half):
                        at = i * (2 * HALF) + half * HALF
                        sp.dma_start(got[:, m, 2 * half:2 * half + 2, :, :].rearrange("p h g f -> p (h g f)"),
                                     kept_rows[:, at:at + HALF] if isinstance(i, int) else kept_rows[:, bass.ds(at, HALF)]).then_inc(rows_in[m * 2 + half], 16)

                    for i in range(2):
                        for half in range(2):
                            load(i, i, half)
                    with sp.Fori(0, (NB - 3) // 2) as i:
                        for m in range(2):
                            for half in range(2):
                                sp.wait_ge(summed[2 * half + 1], i * 2 + (m + 2))
                                load(i * 2 + (m + 2), m, half)
                    for half in range(2):
                        sp.wait_ge(summed[2 * half + 1], NB - 1)
                        load(NB - 1, 0, half)
                if kind == "edge":
                    with sp.Fori(0, NB) as i:
                        for h in range(NG):
                            sp.wait_ge(mapped[h], i + 1)
                            sp.dma_start(edge_sb[:, h, :], edge_t[:, bass.ds(i * (BT * P) + h * (HB * P), HB * P)]).then_inc(edges_in[h], 16)

            def tensor(pe, span):
                if kind == "edge":
                    for h in range(NG):
                        pe.sem_inc(mapped[h], 1)

                def step(i, m, n):
                    for h in range(NG):
                        if kind == "edge":
                            pe.wait_ge(edges_in[h], i * 16 + 16)
                            pe.wait_ge(joined[h], i + 1)
                            for g in range(HB):
                                last = nc.tensor.matmul(ps[:, h // 2, (h % 2 * HB + g) * D:(h % 2 * HB + g + 1) * D],
                                                        edge_sb[:, h, g * P:(g + 1) * P], w1b_sb[:], start=True, stop=True)
                            last.then_inc(mapped[h], 1)
                        wait_rows(pe, h, m, n)
                        pe.wait_ge(ready[h], i + 1)
                        pe.wait_ge(added, i * BT + (ZERO + (h + LATE - NG + 1) * HB))
                        if kind == "edge":
                            pe.wait_ge(relued[h], i + 1)
                        for g in range(HB):
                            rows_g = msg[:, h, g, 0:width] if kind == "edge" else got[:, m, h, g, 0:width]
                            if span == SPAN:
                                last = nc.tensor.matmul(ps[0:width, NG + h, 0:span], rows_g, onehot[:, h, g, 0:span], start=(g == 0), stop=(g == HB - 1))
                            else:
                                last = nc.tensor.matmul(ps[0:width, NG + h, g * span:(g + 1) * span], rows_g, onehot[:, h, g, 0:span], start=True, stop=True)
                        last.then_inc(summed[h], 1)
                each_step(pe, step)

            def vector(dve, span):
                for h in range(NG - LATE, NG):
                    nc.vector.memset(ps[0:width, NG + h, :], 0.0).then_inc(summed[h], 1)
                for h in range(NG - LATE):
                    dve.sem_inc(summed[h], 1)
                if kind == "edge":
                    for h in range(NG):
                        dve.sem_inc(joined[h], 1)
                if kind == "kept":
                    dve.sem_inc(added, ZERO)
                else:
                    nc.vector.memset(acc[0:width, :], 0.0).then_inc(added, ZERO)

                def add_sums(bases, count, h):
                    for g in range(1 if span == SPAN else HB):
                        window = acc[0:width, bass.ds(bases[g], span)]
                        dve.wait_ge(added, count + (g + ZERO))
                        nc.vector.tensor_tensor(window, window, ps[0:width, NG + h, g * span:(g + 1) * span],
                                                ALU.add).then_inc(added, HB if span == SPAN else 1)

                def step(i, m, n):
                    bases_of = window_bases(DVE_ENGINE, i, LATE, span)
                    for h in range(NG):
                        dve.wait_ge(summed[h], i + 1)
                        if kind == "kept" and span == SPAN:
                            one_hot(onehot, h, i, span).then_inc(hot, 1)
                        elif kind == "kept":
                            for g in range(HB):
                                at = i * BT + (h * HB + g)
                                last = nc.vector.tensor_scalar(onehot[:, h, g, :], iota[:], dloc[:, bass.ds(at, 1)], score[:, bass.ds(at, 1)],
                                                               ALU.is_equal, ALU.mult)
                            last.then_inc(ready[h], 1)
                        else:
                            one_hot(onehot, h, i, span).then_inc(ready[h], 1)
                        bases = bases_of(h)
                        if kind == "edge":
                            dve.wait_ge(mapped[h], i + 2)
                            wait_rows(dve, h, m, n)
                            nc.vector.tensor_tensor(msg[:, h, :, :], got[:, m, h, :, 0:D],
                                                    ps[:, h // 2, h % 2 * HB * D:(h % 2 + 1) * HB * D].rearrange("p (g d) -> p g d", d=D),
                                                    ALU.add).then_inc(joined[h], 1)
                        dve.wait_ge(summed[h - LATE], i + (1 + (h >= LATE)))
                        add_sums(bases, i * BT + h * HB, (h - LATE) % NG)
                each_step(dve, step)
                bases_of = window_bases(DVE_ENGINE, NB, LATE, span)
                for h in range(LATE):
                    dve.wait_ge(summed[NG - LATE + h], NB + 1)
                    add_sums(bases_of(h), T + h * HB, NG - LATE + h)

            return gpsimd, scalar, sync, tensor, vector, weigh

        def each_window(eng, body, late=None):
            def one(w, m, i, first=False):
                body(w, m % 2, m % STRIPS, i * 2 + m // STRIPS)
                if late and not first:
                    late(w - 1 if isinstance(w, int) else i * 6 + (m - 1), (m + 1) % 2)

            for m in range(6):
                one(m, m, 0, first=(m == 0))
            with eng.Fori(1, NW // 6) as i:
                for m in range(6):
                    one(i * 6 + m, m, i)
            for m in range(NW % 6):
                one(NW - NW % 6 + m, m, NW // 6)
            if late:
                late(NW - 1, (NW - 1) % 2)

        def window_tail(s):
            sums = s.sb("sums", [P, 2, D + 1])
            product, held, turned, put = s.sem("product"), s.sem("held"), s.sem("turned"), s.sem("put")

            def turn(w, m):
                nc.tensor.wait_ge(held, w + 3)
                nc.tensor.wait_ge(put, w + 1)
                nc.tensor.transpose(ps[0:D + 1, 2 + m, 0:WD], sums[0:WD, m, :], ident[0:WD, 0:WD]).then_inc(turned, 1)

            def put_sums(act, w, m):
                act.wait_ge(turned, w + 3)
                nc.scalar.copy(acc[:, bass.ds(w * WD, WD)], ps[0:D + 1, 2 + m, 0:WD]).then_inc(put, 1)

            return sums, product, held, turned, put, turn, put_sums

        def count_windows(s, source, rest, spare):
            WIDE = SPLIT * D + 2
            strips = s.sb("strips", [P, STRIPS - 1, WD * NT], F16)
            parts = s.sb("parts", [P, NT, WIDE], BF16)
            sums, product, held, turned, put, turn, put_sums = window_tail(s)
            strip_in, split, added_up = [s.sem(f"strip_in_{b}") for b in range(STRIPS)], s.sem("split"), s.sem("added_up")

            def strip(b):
                return strips[:, b, :] if b < STRIPS - 1 else spare[:, 0:WD * NT // 2].bitcast(F16)

            def sync(sp):
                def load(w, m, b, n):
                    if isinstance(w, int) and w == STRIPS - 1:
                        sp.wait_ge(split, 2 * SPLIT)
                    if not (isinstance(w, int) and w < STRIPS):
                        sp.wait_ge(product, w + (3 - STRIPS))
                    sp.dma_start(strip(b).rearrange("p (h f) -> p h f", h=2),
                                 counts[bass.ds(w, 1), :, :, :].rearrange("a h p f -> p (a h) f")).then_inc(strip_in[b], 16)
                each_window(sp, load)

            def tensor(pe):
                pe.wait_ge(split, 2 * SPLIT)

                def window(w, m, b, n):
                    pe.wait_ge(strip_in[b], n * 16 + 16)
                    pe.wait_ge(held, w + 1)
                    for k in range(NT):
                        last = nc.tensor.matmul(ps[0:WD, m, 0:WIDE], strip(b)[:, k::NT], parts[:, k, :], start=(k == 0), stop=(k == NT - 1))
                    last.then_inc(product, 1)
                each_window(pe, window, late=turn)

            def scalar(act):
                for counted in (product, put, held, turned):
                    act.sem_inc(counted, 2)
                each_window(act, lambda w, m, b, n: put_sums(act, w, m))

            def vector(dve):
                link = linker(dve, split)
                part = lambda c: parts[:, :, c * D:(c + 1) * D]
                nc.vector.memset(parts[:, :, SPLIT * D:WIDE], 1.0)
                link(nc.vector.tensor_copy(part(0), source))
                link(nc.vector.tensor_tensor(rest, source, part(0), ALU.subtract))
                link(nc.vector.tensor_copy(part(1), rest))
                link(nc.vector.tensor_tensor(rest, rest, part(1), ALU.subtract))
                link(nc.vector.tensor_copy(part(2), rest), 2)

                def window(w, m, b, n):
                    dve.wait_ge(product, w + 3)
                    dve.wait_ge(turned, w + 1)
                    nc.vector.tensor_copy(sums[0:WD, m, :], ps[0:WD, m, 2 * D:3 * D + 1]).then_inc(added_up, 1)
                    for c in (1, 0):
                        dve.wait_ge(added_up, w * 2 + (2 - c))
                        nc.vector.tensor_tensor(sums[0:WD, m, 0:D], sums[0:WD, m, 0:D], ps[0:WD, m, c * D:(c + 1) * D], ALU.add).then_inc(held if c == 0 else added_up, 1)
                each_window(dve, window)

            return sync, tensor, scalar, vector

        def sum_edges(kind, width=D, source=None, rest=None, spare=None):
            with Stage() as s:
                gpsimd, scalar, sync, tensor, vector, weigh = general_sums(s, kind, width)
                if kind == "table":
                    fast_sync, fast_tensor, fast_scalar, fast_vector = count_windows(s, source, rest, spare)
                block = s.start()

                def nothing(eng):
                    return lambda: eng.sem_inc(s.idle, 1)

                @block.gpsimd
                def _(pool):
                    if kind == "table":
                        on_engine(pool, POOL_ENGINE, nothing(pool), lambda: gpsimd(pool))
                    elif kind == "kept":
                        on_engine(pool, POOL_ENGINE, lambda: weigh(pool), nothing(pool))
                    else:
                        gpsimd(pool)

                @block.scalar
                def _(act):
                    if kind == "table":
                        on_engine(act, [mybir.EngineType.Activation], lambda: fast_scalar(act), lambda: scalar(act))
                    else:
                        scalar(act)

                @block.sync
                def _(sp):
                    if kind == "table":
                        on_engine(sp, [mybir.EngineType.SP], lambda: fast_sync(sp), nothing(sp))
                    else:
                        sync(sp)

                @block.tensor
                def _(pe):
                    fast = (lambda: fast_tensor(pe)) if kind == "table" else (lambda: tensor(pe, SPAN))
                    on_engine(pe, PE_ENGINE, fast, lambda: tensor(pe, P))

                @block.vector
                def _(dve):
                    fast = (lambda: fast_vector(dve)) if kind == "table" else (lambda: vector(dve, SPAN))
                    on_engine(dve, DVE_ENGINE, fast, lambda: vector(dve, P))

        def add_attention():
            with Stage() as s:
                dve_link, var_ready, root, out_ready, table_ready, stored = (
                    s.sem(n) for n in ("dve_link", "var_ready", "root", "out_ready", "table_ready", "stored"))
                block = s.start()

                @block.tensor
                def _(pe):
                    node_products(w0_sb[:], D + 1, out_ready)

                @block.vector
                def _(dve):
                    link = linker(dve, dve_link)
                    for b in range(NBK):
                        dve.wait_ge(out_ready, b + 1)
                        last = nc.vector.tensor_scalar(stat[:, 0, of_bank(b)], bank(b, D + 1)[:, :, D], 1e-30, None, ALU.max)
                    link(last)
                    link(nc.vector.reciprocal(stat[:, 1, :], stat[:, 0, :]))
                    for b in range(NBK):
                        last = nc.vector.tensor_tensor(tmp[:, of_bank(b), :], bank(b, D + 1)[:, :, 0:D],
                                                       stat[:, 1, of_bank(b)].unsqueeze(2).to_broadcast([P, BK, D]), ALU.mult)
                    link(last)
                    link(nc.vector.tensor_tensor(x_sb[:], x_sb[:], tmp[:], ALU.add))
                    center(link, ALL, var_ready)
                    scale_relu(dve, link, root, table_ready)

                @block.scalar
                def _(act):
                    act.wait_ge(var_ready, 1)
                    nc.scalar.activation(stat[:, 1, :], stat[:, 1, :], ACT.Sqrt).then_inc(root, 1)

                @block.sync
                def _(sp):
                    on_engine(sp, SP_ENGINE, lambda: sp.sem_inc(s.idle, 1), lambda: store_table(sp, h_sb[:], TW, table_ready, len(CH), stored))

        def store_table(sp, rows_of, width, table_ready, parts, stored):
            sp.wait_ge(table_ready, parts)
            sp.dma_start(table.rearrange("(k p) d -> p k d", p=P)[:, :, 0:width], rows_of).then_inc(stored, 16)
            sp.wait_ge(stored, 16)

        def mlp(s, first, last_w, take, bias, sems, second, turned=None, freed=None, h_ready=None):
            m1, a1, m2, a2, m3, t3 = sems
            hid = s.sb("hid", [P, 2, 2, 512])

            def tensor(pe):
                if turned:
                    pe.wait_ge(h_ready, 1)
                    turn_chunk(pe, h_sb, 0, 6, turned)
                for n in range(len(CH) + 2):
                    if turned and n + 1 < len(CH):
                        if n >= 1:
                            pe.wait_ge(freed, n)
                        pe.wait_ge(h_ready, n + 2)
                        turn_chunk(pe, h_sb, n + 1, 6 + (n + 1) % 2, turned)
                    if n < len(CH):
                        c, wide = CH[n]
                        if turned:
                            pe.wait_ge(freed, n + 1)
                        if n >= 2:
                            pe.wait_ge(a1, n - 1)
                        for j, (w, rows_of) in enumerate(first):
                            last = nc.tensor.matmul(ps[:, n % 2, 0:wide], w, rows_of[0:D, c:c + wide], start=(j == 0), stop=(j == len(first) - 1))
                        last.then_inc(m1, 1)
                    if 1 <= n <= len(CH):
                        k, wide = n - 1, CH[n - 1][1]
                        pe.wait_ge(a1, k + 1)
                        if k >= 2:
                            pe.wait_ge(a2, k - 1)
                        nc.tensor.matmul(ps[:, 2 + k % 2, 0:wide], second, hid[:, 0, k % 2, 0:wide], start=True, stop=True).then_inc(m2, 1)
                    if n >= 2:
                        k, wide = n - 2, CH[n - 2][1]
                        pe.wait_ge(a2, k + 1)
                        if k >= 2:
                            pe.wait_ge(t3, k - 1)
                        for q in range(wide // P):
                            last = nc.tensor.matmul(ps[:, 4 + k % 2, q * D:(q + 1) * D], hid[:, 1, k % 2, q * P:(q + 1) * P], last_w, start=True, stop=True)
                        last.then_inc(m3, 1)

            def scalar(act):
                if turned:
                    save_chunk(act, 0, 6, turned, freed)
                for n in range(len(CH) + 1):
                    if turned and n + 1 < len(CH):
                        save_chunk(act, n + 1, 6 + (n + 1) % 2, turned, freed)
                    if n < len(CH):
                        wide = CH[n][1]
                        act.wait_ge(m1, n + 1)
                        if n >= 2:
                            act.wait_ge(m2, n - 1)
                        nc.scalar.activation(hid[:, 0, n % 2, 0:wide], ps[:, n % 2, 0:wide], ACT.Relu, bias=cols_sb[:, bias:bias + 1]).then_inc(a1, 1)
                    if n >= 1:
                        k, wide = n - 1, CH[n - 1][1]
                        act.wait_ge(m2, k + 1)
                        if k >= 2:
                            act.wait_ge(m3, k - 1)
                        nc.scalar.activation(hid[:, 1, k % 2, 0:wide], ps[:, 2 + k % 2, 0:wide], ACT.Relu, bias=cols_sb[:, bias + 1:bias + 2]).then_inc(a2, 1)

            def vector(dve, then=None):
                for n, (c, wide) in enumerate(CH):
                    dve.wait_ge(m3, n + 1)
                    q = wide // P
                    take(c // P, q, ps[:, 4 + n % 2, 0:q * D].rearrange("p (k d) -> p k d", d=D)).then_inc(t3, 1)
                    if then:
                        dve.wait_ge(t3, n + 1)
                        then(slice(c // P, c // P + q))

            return tensor, scalar, vector

        def row_of(name, q):
            return rows_sb[:, ROWS.index(name), :].unsqueeze(1).to_broadcast([P, q, D])

        def message_nodes():
            with Stage() as s:
                dve_link, var_ready, root, out_ready, stored, h_ready, turned, freed, table_ready = (
                    s.sem(n) for n in ("dve_link", "var_ready", "root", "out_ready", "stored", "h_ready", "turned", "freed", "table_ready"))
                sems = [s.sem(n) for n in ("m1", "a1", "m2", "a2", "m3", "t3")]
                take = lambda k, q, got_ps: nc.vector.tensor_tensor(tmp[:, k:k + q, :], got_ps, row_of("bM3", q), ALU.add)
                tensor, scalar, vector = mlp(s, [(wm1_sb[:], hT)], wm3_sb[:], take, 0, sems, wm2_sb[:], turned, freed, h_ready)
                block = s.start()

                @block.tensor
                def _(pe):
                    node_products(ident[0:D + 1, 0:D + 1], D + 1, out_ready)
                    tensor(pe)

                @block.vector
                def _(dve):
                    link = linker(dve, dve_link)
                    for b in range(NBK):
                        dve.wait_ge(out_ready, b + 1)
                        nc.vector.tensor_copy(count[:, of_bank(b)], bank(b, D + 1)[:, :, D])
                        last = nc.vector.tensor_tensor(x_sb[:, of_bank(b), :], bank(b, D + 1)[:, :, 0:D], x_sb[:, of_bank(b), :], ALU.add)
                    link(last)
                    center(link, ALL, var_ready)
                    scale_relu(dve, link, root, h_ready)
                    vector(dve)
                    dve.wait_ge(sems[5], len(CH))
                    dve.sem_inc(table_ready, 1)

                @block.scalar
                def _(act):
                    act.wait_ge(var_ready, 1)
                    nc.scalar.activation(stat[:, 1, :], stat[:, 1, :], ACT.Sqrt).then_inc(root, 1)
                    scalar(act)

                @block.sync
                def _(sp):
                    on_engine(sp, SP_ENGINE, lambda: sp.sem_inc(s.idle, 1), lambda: store_table(sp, tmp[:], D, table_ready, 1, stored))

        def update_nodes():
            with Stage() as s:
                dve_link, var_ready, root, stored, h_ready, turned, freed = (
                    s.sem(n) for n in ("dve_link", "var_ready", "root", "stored", "h_ready", "turned", "freed"))
                mapped, taken = s.sem("mapped"), s.sem("taken")
                biased = s.sem("biased")
                sems = [s.sem(n) for n in ("m1", "a1", "m2", "a2", "m3", "t3")]
                take = lambda k, q, got_ps: nc.vector.tensor_tensor(x_sb[:, k:k + q, :], got_ps, x_sb[:, k:k + q, :], ALU.add)
                tensor, scalar, vector = mlp(s, [(wu1_sb[:, 0, :], hT), (wu1_sb[:, 1, :], acc)], wu3_sb[:], take, 2, sems, wu2_sb[:])
                block = s.start()

                @block.tensor
                def _(pe):
                    pe.wait_ge(biased, 1)
                    tensor(pe)
                    for q in range(len(CH) + 1):
                        if q < len(CH):
                            if q >= 4:
                                pe.wait_ge(freed, q - 3)
                            pe.wait_ge(h_ready, q + 1)
                            turn_chunk(pe, h_sb, q, q % 4, turned)
                        if q >= 1:
                            k, (c, wide) = q - 1, CH[q - 1]
                            pe.wait_ge(freed, k + 1)
                            if k >= 4:
                                pe.wait_ge(taken, k - 3)
                            for n in range(wide // P):
                                last = nc.tensor.matmul(ps[:, 4 + k % 4, n * D:(n + 1) * D], hT[:, c + n * P:c + (n + 1) * P], w1a_sb[:], start=True, stop=True)
                            last.then_inc(mapped, 1)

                @block.vector
                def _(dve):
                    link = linker(dve, dve_link)
                    nc.vector.tensor_tensor(x_sb[:], x_sb[:], row_of("bU3", NT), ALU.add).then_inc(biased, 1)
                    vector(dve, then=lambda k: center(link, k))
                    dve.sem_inc(var_ready, 1)
                    scale_relu(dve, link, root, h_ready)
                    for q, (c, wide) in enumerate(CH):
                        dve.wait_ge(mapped, q + 1)
                        k, n = c // P, wide // P
                        nc.vector.tensor_tensor(tmp[:, k:k + n, :], ps[:, 4 + q % 4, 0:n * D].rearrange("p (k d) -> p k d", d=D),
                                                row_of("b1", n), ALU.add).then_inc(taken, 1)

                @block.scalar
                def _(act):
                    scalar(act)
                    act.wait_ge(var_ready, 1)
                    nc.scalar.activation(stat[:, 1, :], stat[:, 1, :], ACT.Sqrt).then_inc(root, 1)
                    for q in range(len(CH)):
                        save_chunk(act, q, q % 4, turned, freed)

                @block.sync
                def _(sp):
                    for q, (c, wide) in enumerate(CH):
                        sp.wait_ge(taken, q + 1)
                        sp.dma_start(table[c:c + wide, 0:D].rearrange("(k p) d -> p k d", p=P), tmp[:, c // P:(c + wide) // P, :]).then_inc(stored, 16)
                    sp.wait_ge(stored, 16 * len(CH))

        def finish_nodes():
            with Stage() as s:
                dve_link, out_ready, var_ready, root, stored, done, shifted = (
                    s.sem(n) for n in ("dve_link", "out_ready", "var_ready", "root", "stored", "done", "shifted"))
                block = s.start()

                @block.gpsimd
                def _(pool):
                    nc.gpsimd.tensor_tensor(x_sb[:], x_sb[:], row_of("beta3", NT), ALU.add).then_inc(shifted, 1)

                @block.tensor
                def _(pe):
                    node_products(w2_sb[:], D, out_ready)

                @block.vector
                def _(dve):
                    link = linker(dve, dve_link)
                    link(nc.vector.tensor_scalar(stat[:, 0, :], count[:], 1.0, None, ALU.max))
                    link(nc.vector.reciprocal(stat[:, 1, :], stat[:, 0, :]))
                    for b in range(NBK):
                        dve.wait_ge(out_ready, b + 1)
                        last = nc.vector.tensor_tensor(tmp[:, of_bank(b), :], bank(b, D), stat[:, 1, of_bank(b)].unsqueeze(2).to_broadcast([P, BK, D]), ALU.mult)
                    link(last)
                    link(nc.vector.tensor_tensor(tmp[:], tmp[:], h_sb[:, :, 0:D], ALU.add))
                    v = lambda i: stat[:, i, :]
                    wide = lambda i: stat[:, i, :].unsqueeze(2).to_broadcast([P, NT, D])
                    link(nc.vector.tensor_reduce(v(0), tmp[:], AX_X, ALU.add))
                    link(nc.vector.tensor_scalar(v(0), v(0), 1.0 / D, None, ALU.mult))
                    link(nc.vector.tensor_tensor(tmp[:], tmp[:], wide(0), ALU.subtract))
                    link(nc.vector.tensor_tensor(h_sb[:, :, 0:D], tmp[:], tmp[:], ALU.mult))
                    link(nc.vector.tensor_reduce(v(1), h_sb[:, :, 0:D], AX_X, ALU.add))
                    nc.vector.tensor_scalar(v(1), v(1), 1.0 / D, LN_EPS, ALU.mult, ALU.add).then_inc(var_ready, 1)
                    dve.wait_ge(root, 1)
                    link(nc.vector.reciprocal(v(2), v(1)))
                    link(nc.vector.tensor_tensor(tmp[:], tmp[:], wide(2), ALU.mult))
                    link(nc.vector.tensor_tensor(tmp[:], tmp[:], row_of("gamma", NT), ALU.mult))
                    dve.wait_ge(shifted, 1)
                    for b in range(NBK):
                        nc.vector.tensor_tensor(x_sb[:, of_bank(b), :], x_sb[:, of_bank(b), :], tmp[:, of_bank(b), :], ALU.add).then_inc(done, 1)

                @block.scalar
                def _(act):
                    act.wait_ge(var_ready, 1)
                    nc.scalar.activation(stat[:, 1, :], stat[:, 1, :], ACT.Sqrt).then_inc(root, 1)

                @block.sync
                def _(sp):
                    for b in range(NBK):
                        sp.wait_ge(done, b + 1)
                        sp.dma_start(out.rearrange("(k p) d -> p k d", p=P)[:, of_bank(b), :], x_sb[:, of_bank(b), :]).then_inc(stored, 16)
                    sp.wait_ge(stored, 16 * NBK)

        load_indices()
        attention_nodes()
        attention_scores()
        attention_weights()
        sum_edges("kept", D + 1)
        add_attention()
        sum_edges("table", D + 1, source=h_sb[:, :, 0:D], rest=tmp[:], spare=tmp[:].rearrange("p k d -> p (k d)"))
        message_nodes()
        sum_edges("table", D, source=tmp[:], rest=h_sb[:, :, 0:D], spare=h_sb[:].rearrange("p k d -> p (k d)"))
        update_nodes()
        sum_edges("edge")
        finish_nodes()


def kernel(x, src, dst, edge_attr_32, L0_gnn_W, L0_gnn_beta, L2_gnn_WM1, L2_gnn_bM1, L2_gnn_WM2, L2_gnn_bM2, L2_gnn_WM3, L2_gnn_bM3,
           L2_gnn_WU1, L2_gnn_bU1, L2_gnn_WU2, L2_gnn_bU2, L2_gnn_WU3, L2_gnn_bU3, L3_gnn_W1, L3_gnn_b1, L3_gnn_W2, L3_gnn_b2,
           L3_gnn_gamma, L3_gnn_beta):
    import numpy as np
    import concourse.bacc as bacc
    from concourse.bass_utils import run_bass_kernel_spmd

    f = np.float32
    x_pad = np.zeros((NP, D), f)
    x_pad[:N] = x
    src_pad = np.zeros(EP, np.int32)
    src_pad[:E] = src
    dst_pad = np.full(EP, PAD_DST, np.int32)
    dst_pad[:E] = dst
    edge_t = np.zeros((EF, EP), f)
    edge_t[:, :E] = np.asarray(edge_attr_32).T
    row_vectors = [L2_gnn_bM3, L2_gnn_bU3, L3_gnn_b1, L3_gnn_gamma, L3_gnn_beta]
    rows = np.ascontiguousarray(np.broadcast_to(np.stack([np.asarray(v) for v in row_vectors])[None], (P, len(row_vectors), D)))
    cols = np.ascontiguousarray(np.stack([np.asarray(v) for v in (L2_gnn_bM1, L2_gnn_bM2, L2_gnn_bU1, L2_gnn_bU2)], axis=1))
    arrays = {
        "x": x_pad, "src": src_pad, "dst": dst_pad, "edge_t": edge_t,
        "beta": np.ascontiguousarray(np.broadcast_to(np.asarray(L0_gnn_beta)[None], (P, 1))), "rows": rows, "cols": cols,
        "w0t": np.ascontiguousarray(np.asarray(L0_gnn_W).T),
        "wm1": np.asarray(L2_gnn_WM1), "wm2": np.asarray(L2_gnn_WM2), "wm3": np.asarray(L2_gnn_WM3),
        "wu1": np.asarray(L2_gnn_WU1), "wu2": np.asarray(L2_gnn_WU2), "wu3": np.asarray(L2_gnn_WU3),
        "w1": np.asarray(L3_gnn_W1), "w2": np.asarray(L3_gnn_W2), "b2": np.asarray(L3_gnn_b2).reshape(1, D),
    }
    nc = bacc.Bacc("TRN2", target_bir_lowering=False, num_devices=1)
    args = [nc.dram_tensor("in_" + n, a.shape, mybir.dt.from_np(a.dtype), kind="ExternalInput").ap() for n, a in arrays.items()]
    result = nc.dram_tensor("out_x", (NP, D), F32, kind="ExternalOutput").ap()
    gnn_kernel(nc, *args, result)
    r = run_bass_kernel_spmd(nc, [{"in_" + n: a for n, a in arrays.items()}], core_ids=[0])
    return r.results[0]["out_x"][:N]
```
